# Optimizing a Trainium2 kernel written in Bass

```python
import numpy as np
import jax
import jax.numpy as jnp

def _softmax(x, axis=-1):
    return jax.nn.softmax(x, axis=axis)

def _gelu(x):
    return jax.nn.gelu(x, approximate=True)

def _silu(x):
    return jax.nn.silu(x)

def _sigmoid(x):
    return jax.nn.sigmoid(x)

def _layernorm(x, axis=-1, eps=1e-05):
    m = jnp.mean(x, axis=axis, keepdims=True)
    v = jnp.var(x, axis=axis, keepdims=True)
    return (x - m) / jnp.sqrt(v + eps)

def _scatter_add(tgt, idx, src, axis=0):
    return tgt.at[idx].add(src)

def _segment_sum(src, seg, n):
    return jax.ops.segment_sum(src, seg, n)
kernel_name = 'mk_vit_tower_d2_tok_img512_r4_f906ef'

def setup_inputs(seed: int=0):
    np.random.seed(seed)
    _w = jnp.asarray

    def _rec_inputs():
        import jax
        import jax.numpy as jnp
        _rk = jax.random.key(seed)
        x = -0.000121822 + 0.999869 * jax.random.normal(jax.random.fold_in(_rk, 1), (64, 3, 196, 196), jnp.float32)
        return x
    x = _rec_inputs()

    def _L0_tok_setup():
        import jax, jax.numpy as jnp
        import numpy as np
        B, C, H, N_P, HID = (64, 3, 196, 14, 128)
        P = H // N_P
        IN_DIM = C * P * P
        SEQ = N_P * N_P + 1

        def sinusoidal_position(length, d):
            pos = jnp.arange(length, dtype=jnp.float32)[:, None]
            i = jnp.arange(d)[None, :]
            angle = pos / jnp.power(10000.0, (2 * (i // 2)).astype(jnp.float32) / d)
            return jnp.where(i % 2 == 0, jnp.sin(angle), jnp.cos(angle)).astype(jnp.float32)
        key = jax.random.key(seed)
        k_img, k_w, k_b, k_tok = jax.random.split(key, 4)
        img = jax.random.normal(k_img, (B, C, H, H), dtype=jnp.float32)
        W = jax.random.normal(k_w, (HID, IN_DIM), dtype=jnp.float32) / np.sqrt(IN_DIM)
        b = jax.random.normal(k_b, (HID,), dtype=jnp.float32) * 0.01
        token = jax.random.uniform(k_tok, (1, HID), dtype=jnp.float32)
        pos = sinusoidal_position(SEQ, HID)
        return {'img': img, 'W': W, 'b': b, 'token': token, 'pos': pos}
    _L0_tok_all = _L0_tok_setup()
    _L0_tok_in = {k: v for k, v in _L0_tok_all.items() if k in ('W', 'b', 'token', 'pos')}
    del _L0_tok_all

    def _L0_attn_setup():
        import jax, jax.numpy as jnp
        import numpy as np
        GAMMA = 1.0
        key = jax.random.key(seed)
        x = jax.random.normal(key, (4, 512, 128), dtype=jnp.float32)
        return {'x': x}
    _L0_attn_all = _L0_attn_setup()
    _L0_attn_in = {k: v for k, v in _L0_attn_all.items() if k in ()}
    del _L0_attn_all

    def _L0_ffn_setup():
        import jax, jax.numpy as jnp
        import numpy as np
        B, L, H, E, F, C = (8, 2048, 128, 8, 256, 2)
        key = jax.random.key(seed)
        ks = jax.random.split(key, 4)
        x = jax.random.normal(ks[0], (B, L, H), jnp.float32)
        Wg = jax.random.normal(ks[1], (H, E), jnp.float32) * H ** (-0.5)
        W1 = jax.random.normal(ks[2], (E, H, F), jnp.float32) * H ** (-0.5)
        b1 = jnp.zeros((E, F), jnp.float32)
        W2 = jax.random.normal(ks[3], (E, F, H), jnp.float32) * F ** (-0.5)
        b2 = jnp.zeros((E, H), jnp.float32)
        return {'x': x, 'Wg': Wg, 'W1': W1, 'b1': b1, 'W2': W2, 'b2': b2}
    _L0_ffn_all = _L0_ffn_setup()
    _L0_ffn_in = {k: v for k, v in _L0_ffn_all.items() if k in ('Wg', 'W1', 'b1', 'W2', 'b2')}
    del _L0_ffn_all

    def _L1_attn_setup():
        import jax, jax.numpy as jnp
        import numpy as np
        B, N, D, H, E = (4, 512, 128, 8, 128)
        D1 = 2 * D
        HD = D1 // H
        GAMMA = 0.999

        def _srms(x):
            return x / (jnp.sqrt(jnp.mean(jnp.square(x), axis=-1, keepdims=True)) + 1e-08)
        key = jax.random.key(seed)
        ks = jax.random.split(key, 10)
        s = 0.02

        def lin(k, i, o):
            kw, kb = jax.random.split(k)
            return (jax.random.normal(kw, (i, o), jnp.float32) * s, jax.random.normal(kb, (o,), jnp.float32) * s)
        Wu, bu = lin(ks[0], D, D1)
        Wv, bv = lin(ks[1], D, D1)
        Wo, bo = lin(ks[2], D1, D)
        Wp, bp = lin(ks[3], 1, E)
        W1, b1 = lin(ks[4], E, E)
        W2, b2 = lin(ks[5], E, E)
        W3, b3 = lin(ks[6], E, E)
        Wz, bz = lin(ks[7], E, H * HD)
        x = jax.random.normal(ks[8], (B, N, D), jnp.float32)
        return dict(x=x, Wu=Wu, bu=bu, Wv=Wv, bv=bv, Wo=Wo, bo=bo, Wp=Wp, bp=bp, W1=W1, b1=b1, W2=W2, b2=b2, W3=W3, b3=b3, Wz=Wz, bz=bz)
    _L1_attn_all = _L1_attn_setup()
    _L1_attn_in = {k: v for k, v in _L1_attn_all.items() if k in ('Wu', 'bu', 'Wv', 'bv', 'Wo', 'bo', 'Wp', 'bp', 'W1', 'b1', 'W2', 'b2', 'W3', 'b3', 'Wz', 'bz')}
    del _L1_attn_all

    def _L1_ffn_setup():
        import jax, jax.numpy as jnp
        import numpy as np
        B, T, D = (4, 256, 128)
        E, TOP_K, H = (8, 2, 64)
        key = jax.random.key(seed)
        ks = jax.random.split(key, 8)
        s = 0.02
        return {'x': jax.random.normal(ks[0], (B, T, D), dtype=jnp.float32), 'router': jax.random.normal(ks[1], (D, E), dtype=jnp.float32) * s, 'shared_gate': jax.random.normal(ks[2], (D, H), dtype=jnp.float32) * s, 'shared_up': jax.random.normal(ks[3], (D, H), dtype=jnp.float32) * s, 'shared_down': jax.random.normal(ks[4], (H, D), dtype=jnp.float32) * s, 'W_gate': jax.random.normal(ks[5], (E, D, H), dtype=jnp.float32) * s, 'W_up': jax.random.normal(ks[6], (E, D, H), dtype=jnp.float32) * s, 'W_down': jax.random.normal(ks[7], (E, H, D), dtype=jnp.float32) * s}
    _L1_ffn_all = _L1_ffn_setup()
    _L1_ffn_in = {k: v for k, v in _L1_ffn_all.items() if k in ('router', 'shared_gate', 'shared_up', 'shared_down', 'W_gate', 'W_up', 'W_down')}
    del _L1_ffn_all
    return {'x': x, 'L0_tok_W': _L0_tok_in['W'], 'L0_tok_b': _L0_tok_in['b'], 'L0_tok_token': _L0_tok_in['token'], 'L0_tok_pos': _L0_tok_in['pos'], 'L0_ffn_Wg': _L0_ffn_in['Wg'], 'L0_ffn_W1': _L0_ffn_in['W1'], 'L0_ffn_b1': _L0_ffn_in['b1'], 'L0_ffn_W2': _L0_ffn_in['W2'], 'L0_ffn_b2': _L0_ffn_in['b2'], 'L1_attn_Wu': _L1_attn_in['Wu'], 'L1_attn_bu': _L1_attn_in['bu'], 'L1_attn_Wv': _L1_attn_in['Wv'], 'L1_attn_bv': _L1_attn_in['bv'], 'L1_attn_Wo': _L1_attn_in['Wo'], 'L1_attn_bo': _L1_attn_in['bo'], 'L1_attn_Wp': _L1_attn_in['Wp'], 'L1_attn_bp': _L1_attn_in['bp'], 'L1_attn_W1': _L1_attn_in['W1'], 'L1_attn_b1': _L1_attn_in['b1'], 'L1_attn_W2': _L1_attn_in['W2'], 'L1_attn_b2': _L1_attn_in['b2'], 'L1_attn_W3': _L1_attn_in['W3'], 'L1_attn_b3': _L1_attn_in['b3'], 'L1_attn_Wz': _L1_attn_in['Wz'], 'L1_attn_bz': _L1_attn_in['bz'], 'L1_ffn_router': _L1_ffn_in['router'], 'L1_ffn_shared_gate': _L1_ffn_in['shared_gate'], 'L1_ffn_shared_up': _L1_ffn_in['shared_up'], 'L1_ffn_shared_down': _L1_ffn_in['shared_down'], 'L1_ffn_W_gate': _L1_ffn_in['W_gate'], 'L1_ffn_W_up': _L1_ffn_in['W_up'], 'L1_ffn_W_down': _L1_ffn_in['W_down']}

def reference(x, L0_tok_W, L0_tok_b, L0_tok_token, L0_tok_pos, L0_ffn_Wg, L0_ffn_W1, L0_ffn_b1, L0_ffn_W2, L0_ffn_b2, L1_attn_Wu, L1_attn_bu, L1_attn_Wv, L1_attn_bv, L1_attn_Wo, L1_attn_bo, L1_attn_Wp, L1_attn_bp, L1_attn_W1, L1_attn_b1, L1_attn_W2, L1_attn_b2, L1_attn_W3, L1_attn_b3, L1_attn_Wz, L1_attn_bz, L1_ffn_router, L1_ffn_shared_gate, L1_ffn_shared_up, L1_ffn_shared_down, L1_ffn_W_gate, L1_ffn_W_up, L1_ffn_W_down):
    import jax
    import jax.numpy as jnp

    def _L0_tok_ref(img, W, b, token, pos):
        import jax, jax.numpy as jnp
        import numpy as np
        B, C, H, N_P, HID = (64, 3, 196, 14, 128)
        P = H // N_P
        IN_DIM = C * P * P
        SEQ = N_P * N_P + 1

        def sinusoidal_position(length, d):
            pos = jnp.arange(length, dtype=jnp.float32)[:, None]
            i = jnp.arange(d)[None, :]
            angle = pos / jnp.power(10000.0, (2 * (i // 2)).astype(jnp.float32) / d)
            return jnp.where(i % 2 == 0, jnp.sin(angle), jnp.cos(angle)).astype(jnp.float32)
        Bn = img.shape[0]
        patches = img.reshape(Bn, C, N_P, P, N_P, P)
        patches = patches.transpose(0, 2, 4, 1, 3, 5).reshape(Bn, N_P * N_P, IN_DIM)
        tokens = jnp.einsum('bsd,hd->bsh', patches, W) + b
        cls = jnp.broadcast_to(token[None, :, :], (Bn, 1, HID))
        out = jnp.concatenate([cls, tokens], axis=1) + pos
        return out

    def _L0_attn_ref(x):
        import jax, jax.numpy as jnp
        import numpy as np
        GAMMA = 1.0
        sq = jnp.sum(x * x, axis=-1)
        dots = jnp.einsum('bse,bte->bst', x, x)
        dist2 = sq[:, :, None] + sq[:, None, :] - 2.0 * dots
        dist2 = jnp.maximum(dist2, 0.0)
        K = jnp.exp(-GAMMA * dist2)
        attn = jax.nn.softmax(K, axis=-1)
        return jnp.einsum('bst,bte->bse', attn, x)

    def _L0_ffn_ref(x, Wg, W1, b1, W2, b2):
        import jax, jax.numpy as jnp
        import numpy as np
        B, L, H, E, F, C = (8, 2048, 128, 8, 256, 2)
        b, l, h = x.shape
        e = Wg.shape[1]
        k = min(max(int(l * C / e), 1), l)
        S = jax.nn.softmax(x @ Wg, axis=-1)
        St = jnp.swapaxes(S, 1, 2)
        G, I = jax.lax.top_k(St, k)
        ex = jnp.take_along_axis(x[:, None], I[..., None], axis=2)
        hmid = jax.nn.gelu(jnp.einsum('bekh,ehf->bekf', ex, W1) + b1[None, :, None, :], approximate=False)
        out = jnp.einsum('bekf,efh->bekh', hmid, W2) + b2[None, :, None, :]
        vals = G[..., None] * out
        new_x = jnp.zeros_like(x).at[jnp.arange(b)[:, None, None], I].add(vals)
        return new_x

    def _L1_attn_ref(x, Wu, bu, Wv, bv, Wo, bo, Wp, bp, W1, b1, W2, b2, W3, b3, Wz, bz):
        import jax, jax.numpy as jnp
        import numpy as np
        B, N, D, H, E = (4, 512, 128, 8, 128)
        D1 = 2 * D
        HD = D1 // H
        GAMMA = 0.999

        def _srms(x):
            return x / (jnp.sqrt(jnp.mean(jnp.square(x), axis=-1, keepdims=True)) + 1e-08)
        shortcut = x
        xn = _srms(x)
        u = jax.nn.silu(xn @ Wu + bu)
        v = jax.nn.silu(xn @ Wv + bv)
        b, n, _ = x.shape
        v = v.reshape(b, n, H, HD).transpose(0, 2, 1, 3)
        pos = jnp.arange(0, n, dtype=x.dtype).reshape(n, 1)
        hcf = pos @ Wp + bp
        for W, bb in ((W1, b1), (W2, b2), (W3, b3)):
            hcf = jax.nn.relu(_srms(hcf)) @ W + bb
        coef = jax.nn.relu(_srms(hcf)) @ Wz + bz
        coef = coef.reshape(n, H, HD).transpose(1, 0, 2)
        zero = coef[:, :1]
        posc = coef[:, 1:]
        decay = GAMMA ** jnp.arange(1, n, dtype=x.dtype)[None, :, None]
        a = jnp.concatenate([zero, decay * posc, zero], axis=1)
        m = 2 * n
        fv = jnp.fft.rfft(v, m, axis=2)
        fa = jnp.fft.rfft(a, m, axis=1)[None]
        out = jnp.fft.irfft(fv * fa, m, axis=2)[:, :, :n]
        out = out.transpose(0, 2, 1, 3).reshape(b, n, H * HD)
        out = u * out
        return out @ Wo + bo + shortcut

    def _L1_ffn_ref(x, router, shared_gate, shared_up, shared_down, W_gate, W_up, W_down):
        import jax, jax.numpy as jnp
        import numpy as np
        B, T, D = (4, 256, 128)
        E, TOP_K, H = (8, 2, 64)
        b, t, d = x.shape
        n = b * t
        x_flat = x.reshape(n, d)
        shared_out = jax.nn.silu(x_flat @ shared_gate) * (x_flat @ shared_up) @ shared_down
        probs = jax.nn.softmax(x_flat @ router, axis=-1)
        topk_scores, topk_idx = jax.lax.top_k(probs, TOP_K)
        combine = jnp.zeros((n, E), dtype=x.dtype)
        combine = combine.at[jnp.arange(n)[:, None], topk_idx].set(topk_scores)
        gate = jax.nn.silu(jnp.einsum('nd,edh->enh', x_flat, W_gate))
        up = jnp.einsum('nd,edh->enh', x_flat, W_up)
        y = jnp.einsum('enh,ehd->end', gate * up, W_down)
        routed_out = jnp.einsum('ne,end->nd', combine, y)
        return (shared_out + routed_out).reshape(b, t, d)
    h = _L0_tok_ref(x, L0_tok_W, L0_tok_b, L0_tok_token, L0_tok_pos)
    h = h + _L0_attn_ref(_layernorm(h, axis=-1))
    h = h + _L0_ffn_ref(_layernorm(h, axis=-1), L0_ffn_Wg, L0_ffn_W1, L0_ffn_b1, L0_ffn_W2, L0_ffn_b2)
    h = h + _L1_attn_ref(_layernorm(h, axis=-1), L1_attn_Wu, L1_attn_bu, L1_attn_Wv, L1_attn_bv, L1_attn_Wo, L1_attn_bo, L1_attn_Wp, L1_attn_bp, L1_attn_W1, L1_attn_b1, L1_attn_W2, L1_attn_b2, L1_attn_W3, L1_attn_b3, L1_attn_Wz, L1_attn_bz)
    h = h + _L1_ffn_ref(_layernorm(h, axis=-1), L1_ffn_router, L1_ffn_shared_gate, L1_ffn_shared_up, L1_ffn_shared_down, L1_ffn_W_gate, L1_ffn_W_up, L1_ffn_W_down)
    return h

_drawn_inputs = setup_inputs


def setup_inputs(seed=0):
    import zlib

    import numpy as np

    out = dict(_drawn_inputs(seed))
    spreads = {'L0_ffn_b1': (0.0, 0.401), 'L0_ffn_b2': (0.0, 0.274)}
    factors = {'L0_tok_b': 3.738,
     'L1_attn_Wu': 3.17,
     'L1_attn_bu': 8.0,
     'L1_attn_Wv': 3.101,
     'L1_attn_bv': 8.0,
     'L1_attn_Wo': 2.92,
     'L1_attn_bo': 7.037,
     'L1_attn_Wp': 6.128,
     'L1_attn_bp': 8.0,
     'L1_attn_W1': 4.366,
     'L1_attn_b1': 8.0,
     'L1_attn_W2': 5.138,
     'L1_attn_b2': 8.0,
     'L1_attn_W3': 3.666,
     'L1_attn_b3': 8.0,
     'L1_attn_Wz': 2.833,
     'L1_attn_bz': 8.0,
     'L1_ffn_router': 8.0,
     'L1_ffn_shared_gate': 8.0,
     'L1_ffn_shared_up': 8.0,
     'L1_ffn_shared_down': 8.0,
     'L1_ffn_W_gate': 8.0,
     'L1_ffn_W_up': 8.0,
     'L1_ffn_W_down': 8.0,
     'L0_tok_token': 2.684}
    for name, (base, spread) in spreads.items():
        noise = np.random.default_rng([zlib.crc32(name.encode()), seed]).standard_normal(out[name].shape)
        drawn = base * np.exp(spread * noise) if base else spread * noise
        out[name] = jnp.asarray(drawn.astype(out[name].dtype))
    for name, factor in factors.items():
        out[name] = (out[name] * factor).astype(out[name].dtype)
    return out
```

```python
from contextlib import ExitStack

import concourse.bass as bass
from concourse import mybir

F32 = mybir.dt.float32
BF16 = mybir.dt.bfloat16
I32 = mybir.dt.int32
U32 = mybir.dt.uint32
ALU = mybir.AluOpType
ACT = mybir.ActivationFunctionType
AX = mybir.AxisListType

B, C, IMG, NP = 64, 3, 196, 14
PX = IMG // NP
D = 128
KIN = C * PX * PX
S = NP * NP + 1
TP = 99
SP = 2 * TP
EPS = 1e-5
E0, F0 = 8, 256
KTOP = int(S * 2 / E0)
GI = 8
NG = B // GI
ROWS = GI * NP
CPY = C * PX
CH = [9, 9, 8, 8, 8]
CH0 = [sum(CH[:i]) for i in range(len(CH))]
JP = NP // 2


class Mem:

    def __init__(self, nc, stack):
        self.nc, self.stack = nc, stack

    def sb(self, name, shape, dt=F32):
        return self.stack.enter_context(self.nc.sbuf_tensor(name, shape, dt))

    def ps(self, name, shape, dt=F32):
        return self.stack.enter_context(self.nc.psum_tensor(name, shape, dt))

    def sem(self, name):
        return self.stack.enter_context(self.nc.semaphore(name))


def hold(eng, sem, value, passed):
    eng.wait_ge(sem, value)
    eng.sem_inc(passed, 1)


def persistent(m):
    return {
        "ident": m.sb("ident", [D, D]),
        "wT": m.sb("patch_wT", [CH[0] * PX, len(CH), D]),
        "posT": m.sb("posT", [D, SP]),
        "score": m.sb("score", [TP, 2, B, E0]),
        "slot_idx": m.sb("slot_idx", [SLOT2, B * NPAIR]),
        "slot_gate": m.sb("slot_gate", [SLOT2, B * NPAIR]),
        "slot_row": m.sb("slot_row", [SLOT2, B * NPAIR], I32),
    }


def setup(nc, m, t, keep):
    with ExitStack() as ctx:
        l = Mem(nc, ctx)
        wtok = l.sb("wtok_rows", [D, KIN])
        pos = l.sb("pos_rows", [TP, 2, D])
        btok = l.sb("btok", [D, 1])
        tokc = l.sb("tokc", [D, 1])
        w3 = l.sb("coef_w", [D, 3, D])
        wz = l.sb("coef_wz", [D, 2 * D])
        rows = l.sb("coef_rows", [TP, 5, D])
        bz = l.sb("coef_bz", [D, 2])
        decay = l.sb("decay", [D, SP])
        half = l.sb("one_half", [TP, 2])
        posi = l.sb("posi", [TP, 2], I32)
        posf = l.sb("posf", [TP, 2])
        hc = l.sb("hc", [TP, 2, D])
        hn = l.sb("hn", [TP, 2, D])
        sq = l.sb("hc_sq", [TP, 2, D])
        ss = l.sb("hc_ss", [TP, 2])
        hT = l.sb("hT", [D, SP])
        apad = l.sb("apad", [D, 2, TP - 1 + SP])
        ptr = l.ps("setup_tr", [D, 4, 512])
        pmm = l.ps("setup_mm", [D, 512])
        ident, wT, posT = keep["ident"], keep["wT"], keep["posT"]
        loads, loads2, idz, idd, iot = (l.sem(n) for n in ("su_loads", "su_loads2", "su_idz", "su_ident", "su_iota"))
        tr, ev, mm, dv = (l.sem(n) for n in ("su_tr", "su_evac", "su_mm", "su_dve"))
        apd, apz, rms = l.sem("su_apad_out"), l.sem("su_pz"), l.sem("su_rms")
        with nc.Block() as block:

            @block.sync
            def _(sp):
                sp.dma_start(wtok[:, :], t["L0_tok_W"]).then_inc(loads, 16)
                sp.dma_start(pos[:, 0, :], t["L0_tok_pos"][0:TP, :]).then_inc(loads, 16)
                sp.wait_ge(apz, 1)
                sp.dma_start(pos[0:S - TP, 1, :], t["L0_tok_pos"][TP:S, :]).then_inc(loads, 16)
                sp.dma_start(btok[:, :], t["L0_tok_b"].rearrange("(p a) -> p a", a=1)).then_inc(loads, 16)
                sp.dma_start(tokc[:, :], t["L0_tok_token"].rearrange("a p -> p a")).then_inc(loads, 16)
                for i in range(3):
                    sp.dma_start(w3[:, i, :], t[f"L1_attn_W{i + 1}"]).then_inc(loads2, 16)
                sp.dma_start(wz[:, :], t["L1_attn_Wz"]).then_inc(loads2, 16)
                for i in range(2):
                    sp.dma_start(bz[:, i:i + 1], t["L1_attn_bz"][i * D:(i + 1) * D].rearrange("(p a) -> p a", a=1)).then_inc(loads2, 16)
                sp.dma_start(decay[:, :], t["decay"].broadcast_to([D, SP])).then_inc(loads2, 16)
                for i, n in enumerate(("Wp", "bp", "b1", "b2", "b3")):
                    v = t["L1_attn_" + n]
                    v = v if n == "Wp" else v.rearrange("(a p) -> a p", a=1)
                    sp.dma_start(rows[:, i, :], v.broadcast_to([TP, D])).then_inc(loads2, 16)
                sp.wait_ge(dv, 23)
                sp.dma_start(t["apad"].rearrange("(a p) n -> p a n", p=D), apad[:, :, :]).then_inc(apd, 16)
                sp.wait_ge(apd, 16)

            @block.gpsimd
            def _(pool):
                nc.gpsimd.memset(pos[:, 1, :], 0.0).then_inc(apz, 1)
                nc.gpsimd.memset(half[:, :], 0.5)
                nc.gpsimd.memset(ident[:, :], 0.0).then_inc(idz, 1)
                pool.wait_ge(idz, 1)
                nc.gpsimd.affine_select(out=ident[:, :], in_=ident[:, :], compare_op=ALU.not_equal, fill=1.0,
                                        base=0, pattern=[[-1, D]], channel_multiplier=1).then_inc(idd, 1)
                nc.gpsimd.iota(posi[:, :], pattern=[[TP, 2]], base=0, channel_multiplier=1).then_inc(iot, 1)
                for k in range(4):
                    pool.wait_ge(dv, 3 + 5 * k)
                    nc.gpsimd.tensor_tensor(ss[:, :], ss[:, :], half[:, :], ALU.pow).then_inc(rms, 1)

            @block.tensor
            def _(pe):
                pe.wait_ge(idd, 1)
                pe.wait_ge(loads, 80)
                for i, n in enumerate(CH):
                    k0, k = CH0[i] * PX, n * PX
                    nc.tensor.transpose(ptr[0:k, i // 2, (i % 2) * D:(i % 2 + 1) * D], wtok[:, k0:k0 + k], ident[:, :])
                for i in range(2):
                    x = nc.tensor.transpose(ptr[:, 3, i * TP:(i + 1) * TP], pos[:, i, :], ident[0:TP, 0:TP])
                x.then_inc(tr, 1)
                for k in range(4):
                    pe.wait_ge(dv, 6 + 5 * k)
                    pe.wait_ge(ev, 6 + k)
                    for i in range(2):
                        x = nc.tensor.transpose(ptr[:, 3, i * TP:(i + 1) * TP], hn[:, i, :], ident[0:TP, 0:TP])
                    x.then_inc(tr, 1)
                    pe.wait_ge(ev, 7 + k)
                    if k == 0:
                        pe.wait_ge(loads2, 16 * 12)
                    for i in range(2):
                        if k < 3:
                            x = nc.tensor.matmul(pmm[0:TP, i * D:(i + 1) * D], hT[:, i * TP:(i + 1) * TP], w3[:, k, :], start=True, stop=True)
                        else:
                            x = nc.tensor.matmul(pmm[:, i * SP:(i + 1) * SP], wz[:, i * D:(i + 1) * D], hT[:, :], start=True, stop=True)
                    x.then_inc(mm, 1)

            @block.scalar
            def _(act):
                act.wait_ge(tr, 1)
                for i, n in enumerate(CH):
                    nc.scalar.copy(wT[0:n * PX, i, :], ptr[0:n * PX, i // 2, (i % 2) * D:(i % 2 + 1) * D]).then_inc(ev, 1)
                nc.scalar.activation(posT[:, 1:SP], ptr[:, 3, 1:SP], ACT.Identity, bias=btok[:, 0:1])
                nc.scalar.activation(posT[:, 0:1], ptr[:, 3, 0:1], ACT.Identity, bias=tokc[:, 0:1]).then_inc(ev, 1)
                for k in range(4):
                    act.wait_ge(tr, 2 + k)
                    if k:
                        act.wait_ge(mm, k)
                    nc.scalar.copy(hT[:, :], ptr[:, 3, 0:SP]).then_inc(ev, 1)

            @block.vector
            def _(v):
                n = [0]

                def link(x):
                    n[0] += 1
                    x.then_inc(dv, 1)
                    v.wait_ge(dv, n[0])

                v.wait_ge(iot, 1)
                nc.vector.memset(apad[:, :, :], 0.0)
                nc.vector.tensor_copy(posf[:, :], posi[:, :])
                v.wait_ge(loads2, 16 * 12)
                link(nc.vector.memset(sq[:, :, :], 0.0))
                for k in range(4):
                    for i in range(2):
                        if k == 0:
                            x = nc.vector.scalar_tensor_tensor(out=hc[:, i, :], in0=rows[:, 0, :], scalar=posf[:, i:i + 1], in1=rows[:, 1, :], op0=ALU.mult, op1=ALU.add)
                        else:
                            v.wait_ge(mm, k)
                            x = nc.vector.tensor_tensor(hc[:, i, :], pmm[0:TP, i * D:(i + 1) * D], rows[:, 1 + k, :], ALU.add)
                    link(x)
                    for i in range(2):
                        x = nc.vector.tensor_tensor_reduce(out=sq[:, i, :], in0=hc[:, i, :], in1=hc[:, i, :], scale=1.0 / D, scalar=0.0, op0=ALU.mult, op1=ALU.add, accum_out=ss[:, i:i + 1])
                    link(x)
                    v.wait_ge(rms, k + 1)
                    link(nc.vector.tensor_scalar(ss[:, :], ss[:, :], 1e-8, None, ALU.add))
                    link(nc.vector.reciprocal(ss[:, :], ss[:, :]))
                    if k:
                        v.wait_ge(tr, 1 + k)
                    for i in range(2):
                        x = nc.vector.tensor_scalar(hn[:, i, :], hc[:, i, :], ss[:, i:i + 1], 0.0, ALU.mult, ALU.max)
                    link(x)
                v.wait_ge(mm, 4)
                for i in range(2):
                    link(nc.vector.scalar_tensor_tensor(out=apad[:, i, TP - 1:TP - 1 + SP], in0=pmm[:, i * SP:(i + 1) * SP], scalar=bz[:, i:i + 1], in1=decay[:, :], op0=ALU.add, op1=ALU.mult))


def embed_and_attend(nc, m, t, keep):
    with ExitStack() as ctx:
        l = Mem(nc, ctx)
        px = l.sb("pixels", [ROWS, 2, C, PX * IMG])
        cut = l.sb("pixels_cut", [ROWS, 2, 2, KIN])
        xT = l.sb("pixelsT", [CH[0] * PX, 2, len(CH), 2 * ROWS])
        h0T = l.sb("tokensT", [D, GI, SP])
        h = l.sb("h", [TP, GI, 2, D])
        xn = l.sb("xn", [TP, GI, 2, D])
        xnT = l.sb("xnT", [D, GI, SP])
        sqT = l.sb("xnT_sq", [D, GI, SP])
        dist = l.sb("neg_half_dist", [TP, GI, 2, SP])
        wgt = l.sb("attn_weights", [TP, GI, 2, SP])
        h1 = l.sb("h1", [TP, GI, 2, D])
        xn1 = l.sb("xn1", [TP, GI, 2, D])
        xn1T = l.sb("xn1T", [D, GI, SP])
        wg = l.sb("router_w", [D, E0])
        nhalf = l.sb("minus_half", [D, TP])
        st = l.sb("ln_stats", [TP, 8, 4, 6])
        mv = l.sb("ln_meanvar", [TP, 8, 4, 2])
        rstd = l.sb("ln_rstd", [TP, 8, 4])
        vare = l.sb("ln_var_eps", [TP, 8, 4])
        mhalf = l.sb("pow_minus_half", [TP, 4])
        epst = l.sb("ln_eps", [TP, 4])
        tmp4 = l.sb("var_rstd", [TP, 4, 4])
        nhsq = l.sb("neg_half_sq", [TP, GI, 2])
        rsum = l.sb("row_sum", [TP, GI, 2])
        rinv = l.sb("row_inv", [TP, 4])
        lmax = l.sb("logit_max", [TP, 2, GI])
        lsub = l.sb("logit_sub", [TP, 2, GI, E0])
        lexp = l.sb("logit_exp", [TP, 2, GI, E0])
        lsum = l.sb("logit_sum", [TP, 2, GI])
        linv = l.sb("logit_inv", [TP, 2, GI])
        pT = [l.ps(f"ps_pixelsT{i}", [D, 512]) for i in range(3)]
        pO = l.ps("ps_tokens", [D, 512])
        ring = [l.ps(f"ps_ring{i}", [D, 512]) for i in range(3)]
        pL = l.ps("ps_logits", [D, 512])
        ident, wT, posT, score = keep["ident"], keep["wT"], keep["posT"], keep["score"]
        px_in, wg_in = [l.sem(f"px_in{i}") for i in range(2)], l.sem("wg_in")
        tokT, evAC, evB, tokM, evO = (l.sem(n) for n in ("tok_T", "tok_evacAC", "tok_evacB", "tok_M", "tok_added"))
        full = l.sem("ring_full")
        hrd, xnr, xtr, ds_r, ex_r = (l.sem(n) for n in ("h_ready", "xn_ready", "xnT_ready", "dist_ready", "weights_ready"))
        h1r, xn1r, xn1tr, lgr, lfree, scr = (l.sem(n) for n in ("h1_ready", "xn1_ready", "xn1T_ready", "logits_ready", "lsub_ready", "lexp_ready"))
        dv, ac, cst, stored = l.sem("p1_dve"), l.sem("p1_act"), l.sem("p1_const"), l.sem("h1_stored")
        score_done, sqr, cutr = l.sem("score_done"), l.sem("sq_ready"), l.sem("cut_ready")
        mvr, rsr, epsr, pgo = l.sem("meanvar_ready"), l.sem("rstd_ready"), l.sem("vareps_ready"), l.sem("p1_powers")
        held = l.sem("p1_dve_held")

        U0, U1, U2, U3, U4, NU = 0, 4, 8, 16, 20, 24

        def slot(u):
            return ring[u % 3]

        def take(pe, g, u):
            u -= 3
            if u < 0:
                pe.wait_ge(xn1tr, 4 * g + u + NU - U4 + 1)
            elif u < U1:
                pe.wait_ge(hrd, 4 * g + u + 1)
            elif u < U2:
                pe.wait_ge(xtr, 4 * g + u - U1 + 1)
            elif u < U3:
                pe.wait_ge(ds_r, 8 * g + u - U2 + 1)
            elif u < U4:
                pe.wait_ge(h1r, 4 * g + u - U3 + 1)
            else:
                pe.wait_ge(xn1tr, 4 * g + u - U4 + 5)

        def filled(eng, g, u):
            eng.wait_ge(full, NU * g + u + 1)

        with nc.Block() as block:

            @block.sync
            def _(sp):
                def load(g, par):
                    for b in range(GI):
                        sp.dma_start(px[b * NP:(b + 1) * NP, par, :, :],
                                     t["x"][g * GI + b].rearrange("c (i y) w -> i c (y w)", i=NP)).then_inc(px_in[par], 16)

                sp.dma_start(wg[:, :], t["L0_ffn_Wg"]).then_inc(wg_in, 16)
                load(0, 0)
                load(1, 1)

                def store(g):
                    sp.wait_ge(h1r, 4 * g + 4)
                    sp.dma_start(t["h1"][bass.ds(g * GI, GI)].rearrange("b (t p) d -> p b t d", p=TP), h1[:, :, :, :]).then_inc(stored, 16)
                    sp.wait_ge(xn1r, 4 * g + 4)
                    sp.dma_start(t["xn1"][bass.ds(g * GI, GI)].rearrange("b (t p) d -> p b t d", p=TP), xn1[:, :, :, :]).then_inc(stored, 16)

                with sp.Fori(0, 3) as it:
                    for par in range(2):
                        g = it * 2 + par
                        sp.wait_ge(cutr, JP * g + JP)
                        load(g + 2, par)
                        store(g)
                store(6)
                store(7)
                sp.wait_ge(stored, 32 * NG + 32)

            @block.gpsimd
            def _(pool):
                nc.gpsimd.memset(nhalf[:, :], -0.5).then_inc(cst, 1)
                nc.gpsimd.memset(h0T[:, :, SP - 1:SP], 0.0).then_inc(cst, 1)
                nc.gpsimd.memset(wgt[:, :, :, SP - 1:SP], 1.0).then_inc(cst, 1)
                nc.gpsimd.memset(mhalf[:, :], -0.5).then_inc(pgo, 1)
                nc.gpsimd.memset(epst[:, :], EPS).then_inc(pgo, 1)
                pool.sem_inc(stored, 32)

                def rstds(g, k, first):
                    pool.wait_ge(mvr, 8 * g + k + (1 if first else 5))
                    if first and k == 0:
                        pool.wait_ge(pgo, 2)
                    j = k if first else 4 + k
                    nc.gpsimd.tensor_tensor(vare[:, j, :], mv[:, j, :, 1], epst[:, :], ALU.add).then_inc(epsr, 1)
                    pool.wait_ge(epsr, 8 * g + j + 1)
                    nc.gpsimd.tensor_tensor(rstd[:, j, :], vare[:, j, :], mhalf[:, :], ALU.pow).then_inc(rsr, 1)

                with pool.Fori(0, NG) as g:
                    for k in range(4):
                        rstds(g, k, True)
                    for k in range(4):
                        rstds(g, k, False)

            @block.tensor
            def _(pe):
                def T(g, jp):
                    u = JP * g + jp
                    pe.wait_ge(cutr, u + 1)
                    if not (isinstance(g, int) and u == 0):
                        pe.wait_ge(evAC, u * 2)
                        pe.wait_ge(evB, u)
                    for c, n in enumerate(CH):
                        for j in range(2):
                            o = (c % 2) * 2 * ROWS + j * ROWS
                            x = nc.tensor.transpose(pT[c // 2][0:n * PX, o:o + ROWS], cut[:, jp % 2, j, CH0[c] * PX:(CH0[c] + n) * PX], ident[0:ROWS, 0:ROWS])
                    x.then_inc(tokT, 1)

                def M(g, jp):
                    u = JP * g + jp
                    pe.wait_ge(evAC, u * 2 + 2)
                    pe.wait_ge(evB, u + 1)
                    if not (isinstance(g, int) and u == 0):
                        pe.wait_ge(evO, u)
                    for c, n in enumerate(CH):
                        x = nc.tensor.matmul(pO[:, 0:2 * ROWS], wT[0:n * PX, c, :], xT[0:n * PX, jp % 2, c, :], start=c == 0, stop=c == len(CH) - 1)
                    x.then_inc(tokM, 1)

                def tokens_rows(g, k):
                    take(pe, g, U0 + k)
                    if k == 0:
                        pe.wait_ge(evO, JP * g + JP)
                    for i in range(2):
                        for q in range(2):
                            o = (2 * i + q) * D
                            x = nc.tensor.transpose(slot(U0 + k)[0:TP, o:o + D], h0T[:, 2 * k + i, q * TP:(q + 1) * TP], ident[:, :])
                    x.then_inc(full, 1)

                def turn(src, ready, g, k, use):
                    take(pe, g, use + k)
                    pe.wait_ge(ready, 4 * g + k + 1)
                    for i in range(2):
                        for q in range(2):
                            o = i * SP + q * TP
                            x = nc.tensor.transpose(slot(use + k)[:, o:o + TP], src[:, 2 * k + i, q, :], ident[0:TP, 0:TP])
                    x.then_inc(full, 1)

                def dots(g, b):
                    take(pe, g, U2 + b)
                    pe.wait_ge(xtr, 4 * g + b // 2 + 1)
                    for q in range(2):
                        o = slot(U2 + b)[0:TP, q * SP:(q + 1) * SP]
                        nc.tensor.matmul(o, xnT[:, b, q * TP:(q + 1) * TP], xnT[:, b, :], start=True, stop=False)
                        x = nc.tensor.matmul(o, nhalf[:, :], sqT[:, b, :], start=False, stop=True)
                    x.then_inc(full, 1)

                def mix(g, k):
                    take(pe, g, U3 + k)
                    pe.wait_ge(ex_r, 8 * g + 2 * k + 2)
                    for i in range(2):
                        for q in range(2):
                            o = (2 * i + q) * D
                            for s, n in enumerate((TP, S - TP)):
                                x = nc.tensor.matmul(slot(U3 + k)[0:TP, o:o + D], wgt[0:n, 2 * k + i, s, q * TP:(q + 1) * TP], xn[0:n, 2 * k + i, s, :], start=s == 0, stop=s == 1)
                    x.then_inc(full, 1)

                def logits(g):
                    pe.wait_ge(xn1tr, 4 * g + 8)
                    pe.wait_ge(lfree, g + 1)
                    for b in range(GI):
                        for q in range(2):
                            o = (q * GI + b) * E0
                            x = nc.tensor.matmul(pL[0:TP, o:o + E0], xn1T[:, b, q * TP:(q + 1) * TP], wg[:, :], start=True, stop=True)
                    x.then_inc(lgr, 1)

                def body(g, more):
                    f = [lambda jp=jp: (M(g + 1, jp - 1) if jp else None, T(g + 1, jp) if jp < JP else None) for jp in range(JP + 1)]
                    if not more:
                        f = [lambda: None] * (JP + 1)
                    for k in range(4):
                        tokens_rows(g, k)
                    f[0]()
                    turn(xn, xnr, g, 0, U1)
                    turn(xn, xnr, g, 1, U1)
                    f[1]()
                    turn(xn, xnr, g, 2, U1)
                    turn(xn, xnr, g, 3, U1)
                    f[2]()
                    for k in range(4):
                        dots(g, 2 * k)
                        dots(g, 2 * k + 1)
                        f[3 + k]()
                    mix(g, 0)
                    mix(g, 1)
                    f[7]()
                    mix(g, 2)
                    mix(g, 3)
                    for k in range(4):
                        turn(xn1, xn1r, g, k, U4)
                    logits(g)

                pe.wait_ge(cst, 4)
                pe.wait_ge(wg_in, 16)
                for jp in range(JP):
                    T(0, jp)
                    M(0, jp)
                with pe.Fori(0, 3) as it:
                    body(it * 2, True)
                    body(it * 2 + 1, True)
                body(6, True)
                body(7, False)

            @block.scalar
            def _(act):
                n = [0]

                def pixels(g, jp):
                    u = JP * g + jp
                    act.wait_ge(tokT, u + 1)
                    if not (isinstance(g, int) and u < 2):
                        act.wait_ge(tokM, u - 1 if jp else u)
                    k = CH[0] * PX
                    nc.scalar.copy(xT[0:k, jp % 2, 0:2, :], pT[0][0:k, 0:4 * ROWS].rearrange("p (c n) -> p c n", c=2)).then_inc(evAC, 1)
                    k = CH[4] * PX
                    nc.scalar.copy(xT[0:k, jp % 2, 4, :], pT[2][0:k, 0:2 * ROWS]).then_inc(evAC, 1)

                def cut_pair(g, jp, par, half):
                    u = JP * g + jp
                    if jp == 0:
                        act.wait_ge(px_in[par], 128 * half + 128)
                    if not (isinstance(g, int) and g == 0 and jp < 2):
                        act.wait_ge(tokT, u - 1 if jp else u)
                    rows = px[:, par, :, :].rearrange("p c (y j x) -> p j (c y) x", y=PX, j=NP)
                    nc.scalar.copy(cut[:, jp % 2, :, :].rearrange("p j (r x) -> p j r x", x=PX), rows[:, 2 * jp:2 * jp + 2]).then_inc(cutr, 1)

                def take_rows(g, k):
                    filled(act, g, U0 + k)
                    nc.scalar.copy(h[:, 2 * k:2 * k + 2, :, :].rearrange("p i q d -> p (i q d)"), slot(U0 + k)[0:TP, :]).then_inc(hrd, 1)

                def turned(g, k):
                    filled(act, g, U1 + k)
                    o = xnT[:, 2 * k:2 * k + 2, :].rearrange("p i n -> p (i n)")
                    nc.scalar.copy(o, slot(U1 + k)[:, 0:2 * SP])
                    nc.scalar.activation(sqT[:, 2 * k:2 * k + 2, :].rearrange("p i n -> p (i n)"), slot(U1 + k)[:, 0:2 * SP], ACT.Square).then_inc(xtr, 1)

                def weights(g, b):
                    act.wait_ge(ds_r, 8 * g + b + 1)
                    nc.scalar.activation(dist[:, b, :, :], dist[:, b, :, :], ACT.Exp, scale=2.0).then_inc(ac, 1)
                    act.wait_ge(ac, 8 * g + b + 1)
                    for q in range(2):
                        x = nc.scalar.activation(wgt[:, b, q, 0:S], dist[:, b, q, 0:S], ACT.Exp, accum_out=rsum[:, b, q:q + 1])
                    x.then_inc(ex_r, 1)

                def turned1(g, k):
                    filled(act, g, U4 + k)
                    nc.scalar.copy(xn1T[:, 2 * k:2 * k + 2, :].rearrange("p i n -> p (i n)"), slot(U4 + k)[:, 0:2 * SP]).then_inc(xn1tr, 1)

                def body(g, par, half, more):
                    f = [lambda jp=jp: (cut_pair(g + 1, jp + 1, 1 - par, half + par) if jp + 1 < JP else None, pixels(g + 1, jp)) for jp in range(JP)]
                    if more:
                        cut_pair(g + 1, 0, 1 - par, half + par)
                    else:
                        f = [lambda: None] * JP
                    for k in range(4):
                        take_rows(g, k)
                    f[0]()
                    turned(g, 0)
                    turned(g, 1)
                    f[1]()
                    turned(g, 2)
                    turned(g, 3)
                    f[2]()
                    for k in range(4):
                        weights(g, 2 * k)
                        weights(g, 2 * k + 1)
                        f[3 + k]()
                    for k in range(4):
                        turned1(g, k)
                    act.wait_ge(lfree, g + 2)
                    nc.scalar.activation(lexp[:, :, :, :], lsub[:, :, :, :], ACT.Exp).then_inc(scr, 1)

                act.sem_inc(xn1tr, 4)
                cut_pair(0, 0, 0, 0)
                for jp in range(JP):
                    if jp + 1 < JP:
                        cut_pair(0, jp + 1, 0, 0)
                    pixels(0, jp)
                with act.Fori(0, 3) as it:
                    body(it * 2, 0, it, True)
                    body(it * 2 + 1, 1, it, True)
                body(6, 0, 3, True)
                body(7, 1, 3, False)

            @block.vector
            def _(v):
                def pixels(g, jp):
                    u = JP * g + jp
                    v.wait_ge(tokT, u + 1)
                    if not (isinstance(g, int) and u < 2):
                        v.wait_ge(tokM, u - 1 if jp else u)
                    k = CH[2] * PX
                    nc.vector.tensor_copy(xT[0:CH[2] * PX, jp % 2, 2:4, :], pT[1][0:k, 0:4 * ROWS].rearrange("p (c n) -> p c n", c=2)).then_inc(evB, 1)

                def add_pos(g, jp):
                    u = JP * g + jp
                    v.wait_ge(tokM, u + 1)
                    if jp == 0:
                        if isinstance(g, int) and g == 0:
                            v.wait_ge(cst, 3)
                        else:
                            filled(v, g - 1, U0 + 3)
                    o = h0T[:, :, 1:S].rearrange("p b (i j) -> p j b i", j=NP)[:, 2 * jp:2 * jp + 2]
                    a = pO[:, 0:2 * ROWS].rearrange("p (j b i) -> p j b i", j=2, b=GI)
                    b = posT[:, 1:S].rearrange("p (i j) -> p j i", j=NP)[:, 2 * jp:2 * jp + 2].unsqueeze(2).broadcast_to([D, 2, GI, NP])
                    for j in range(2):
                        x = nc.vector.tensor_tensor(o[:, j], a[:, j], b[:, j], ALU.add)
                    x.then_inc(evO, 1)

                def link(x, base, i):
                    x.then_inc(dv, 1)
                    v.wait_ge(dv, base + i)

                NL = 2 * 4 + 4 + 4 + 3

                def body(g, more):
                    i = [0]

                    def c(x):
                        i[0] += 1
                        link(x, NL * g, i[0])

                    def stats(src, k, j):
                        for q in range(4):
                            x = nc.vector.bn_stats(st[:, j, q, :], src[:, 2 * k + q // 2, q % 2, :])
                        i[0] += 1
                        x.then_inc(dv, 1)
                        hold(v, dv, NL * g + i[0], held)
                        for q in range(4):
                            x = nc.vector.bn_aggr(mv[:, j, q, :], st[:, j, q, :])
                        x.then_inc(mvr, 1)

                    def apply(src, out, k, j, ready):
                        v.wait_ge(rsr, 8 * g + j + 1)
                        for q in range(4):
                            x = nc.vector.tensor_scalar(out[:, 2 * k + q // 2, q % 2, :], src[:, 2 * k + q // 2, q % 2, :], mv[:, j, q, 0:1], rstd[:, j, q:q + 1], ALU.subtract, ALU.mult)
                        x.then_inc(ready, 1)

                    def first(k):
                        v.wait_ge(hrd, 4 * g + k + 1)
                        stats(h, k, k)

                    def second(k):
                        apply(h, xn, k, k, xnr)
                        c(nc.vector.tensor_tensor(tmp4[:, k, :], mv[:, k, :, 1], rstd[:, k, :], ALU.mult))
                        nc.vector.scalar_tensor_tensor(out=nhsq[:, 2 * k:2 * k + 2, :].rearrange("p i q -> p (i q)"), in0=tmp4[:, k, :], scalar=-D / 2, in1=rstd[:, k, :], op0=ALU.mult, op1=ALU.mult).then_inc(sqr, 1)

                    def distance(b):
                        filled(v, g, U2 + b)
                        if b % 2 == 0:
                            v.wait_ge(sqr, 4 * g + b // 2 + 1)
                        for q in range(2):
                            x = nc.vector.tensor_scalar(dist[:, b, q, :], slot(U2 + b)[0:TP, q * SP:(q + 1) * SP], nhsq[:, b, q:q + 1], 0.0, ALU.add, ALU.min)
                        x.then_inc(ds_r, 1)

                    def residual(k):
                        filled(v, g, U3 + k)
                        if k == 0:
                            v.wait_ge(stored, 32 * g + 32)
                        c(nc.vector.reciprocal(rinv[:, :], rsum[:, 2 * k:2 * k + 2, :].rearrange("p i q -> p (i q)")))
                        for q in range(4):
                            x = nc.vector.scalar_tensor_tensor(out=h1[:, 2 * k + q // 2, q % 2, :], in0=slot(U3 + k)[0:TP, q * D:(q + 1) * D], scalar=rinv[:, q:q + 1], in1=h[:, 2 * k + q // 2, q % 2, :], op0=ALU.mult, op1=ALU.add)
                        x.then_inc(h1r, 1)
                        v.wait_ge(h1r, 4 * g + k + 1)
                        stats(h1, k, 4 + k)

                    f = [lambda jp=jp: (add_pos(g + 1, jp - 1) if jp else None, pixels(g + 1, jp) if jp < JP else None) for jp in range(JP + 1)]
                    if not more:
                        f = [lambda: None] * (JP + 1)
                    first(0)
                    first(1)
                    second(0)
                    first(2)
                    second(1)
                    f[0]()
                    first(3)
                    second(2)
                    second(3)
                    f[1]()
                    f[2]()
                    for k in range(4):
                        distance(2 * k)
                        distance(2 * k + 1)
                        f[3 + k]()
                    residual(0)
                    residual(1)
                    apply(h1, xn1, 0, 4, xn1r)
                    f[7]()
                    residual(2)
                    apply(h1, xn1, 1, 5, xn1r)
                    residual(3)
                    apply(h1, xn1, 2, 6, xn1r)
                    apply(h1, xn1, 3, 7, xn1r)
                    v.wait_ge(lgr, g + 1)
                    lg = pL[0:TP, 0:2 * GI * E0].rearrange("p (q b e) -> p q b e", q=2, b=GI)
                    c(nc.vector.tensor_reduce(lmax[:, :, :], lg, AX.X, ALU.max))
                    nc.vector.tensor_tensor(lsub[:, :, :, :], lg, lmax[:, :, :].unsqueeze(3).broadcast_to([TP, 2, GI, E0]), ALU.subtract).then_inc(lfree, 1)
                    v.wait_ge(scr, g + 1)
                    c(nc.vector.tensor_reduce(lsum[:, :, :], lexp[:, :, :, :], AX.X, ALU.add))
                    c(nc.vector.reciprocal(linv[:, :, :], lsum[:, :, :]))
                    nc.vector.tensor_tensor(score[:, :, bass.ds(g * GI, GI), :], lexp[:, :, :, :], linv[:, :, :].unsqueeze(3).broadcast_to([TP, 2, GI, E0]), ALU.mult).then_inc(score_done, 1)
                    assert i[0] == NL, i[0]

                v.sem_inc(lfree, 1)
                nc.vector.tensor_copy(h0T[:, :, 0:1], posT[:, 0:1].unsqueeze(1).broadcast_to([D, GI, 1])).then_inc(cst, 1)
                for jp in range(JP):
                    pixels(0, jp)
                    add_pos(0, jp)
                with v.Fori(0, 3) as it:
                    body(it * 2, True)
                    body(it * 2 + 1, True)
                body(6, True)
                body(7, False)
                v.wait_ge(score_done, NG)


HB = 16
NPAIR = E0 // 2
SLOT2 = 2 * KTOP
ROUNDS = -(-KTOP // 8)


def choose_tokens(nc, m, t, keep):
    with ExitStack() as ctx:
        l = Mem(nc, ctx)
        ng = B // HB
        work = l.sb("topk_work", [D, ng, S])
        val = l.sb("topk_val", [D, ng, ROUNDS * 8])
        idx = l.sb("topk_idx", [D, ng, ROUNDS * 8], U32)
        spread = l.sb("topk_spread", [D, 2, ng, SLOT2])
        odd = l.sb("odd_even", [D, 2])
        pick = l.sb("pick_pair", [D, D // 2])
        basei = l.sb("row_base_i", [SLOT2, B * NPAIR], I32)
        base = l.sb("row_base", [SLOT2, B * NPAIR])
        pt = [l.ps(f"ps_score{i}", [D, 512]) for i in range(ng)]
        pi = l.ps("ps_slots", [D, 512])
        ident, score = keep["ident"], keep["score"]
        tr, dv, iot, mm = (l.sem(n) for n in ("tk_tr", "tk_dve", "tk_iota", "tk_mm"))
        with nc.Block() as block:

            @block.gpsimd
            def _(pool):
                nc.gpsimd.iota(basei[:, :], pattern=[[SP, B], [0, NPAIR]], base=0, channel_multiplier=0).then_inc(iot, 1)

            @block.tensor
            def _(pe):
                for g in range(ng):
                    for q, n in enumerate((TP, S - TP)):
                        x = nc.tensor.transpose(pt[g][:, q * TP:q * TP + n], score[0:n, q, g * HB:(g + 1) * HB, :].rearrange("p b e -> p (b e)"), ident[0:n, 0:n])
                    x.then_inc(tr, 1)
                pe.wait_ge(dv, LAST)
                for j in range(2):
                    for g in range(ng):
                        o = j * B * NPAIR + g * HB * NPAIR
                        x = nc.tensor.matmul(pi[0:SLOT2, o:o + HB * NPAIR], spread[:, j, g, :], pick[:, :], start=True, stop=True)
                x.then_inc(mm, 1)

            @block.vector
            def _(v):
                n = [0]

                def link(x):
                    n[0] += 1
                    x.then_inc(dv, 1)
                    v.wait_ge(dv, n[0])

                v.wait_ge(iot, 1)
                nc.vector.tensor_copy(base[:, :], basei[:, :])
                for j in range(2):
                    nc.vector.tensor_reduce(odd[:, j:j + 1], ident[:, :].rearrange("p (a b) -> p b a", b=2)[:, j], AX.X, ALU.add)
                nc.vector.tensor_tensor(pick[:, :], ident[:, :].rearrange("p (a b) -> p b a", b=2)[:, 0], ident[:, :].rearrange("p (a b) -> p b a", b=2)[:, 1], ALU.add)
                for g in range(ng):
                    v.wait_ge(tr, g + 1)
                    x = nc.vector.tensor_copy(work[:, g, :], pt[g][:, 0:S])
                link(x)
                for r in range(ROUNDS):
                    w = slice(8 * r, 8 * r + 8)
                    for g in range(ng):
                        x = nc.vector.max(val[:, g, w], work[:, g, :])
                    link(x)
                    for g in range(ng):
                        x = nc.vector.max_index(idx[:, g, w], val[:, g, w], work[:, g, :])
                    if r < ROUNDS - 1:
                        link(x)
                        for g in range(ng):
                            x = nc.vector.match_replace(work[:, g, :], val[:, g, w], work[:, g, :], -1.0)
                    link(x)
                for j, src in enumerate((idx, val)):
                    for h in range(2):
                        x = nc.vector.tensor_scalar(spread[:, j, :, h * KTOP:(h + 1) * KTOP], src[:, :, 0:KTOP], odd[:, h:h + 1], None, ALU.mult)
                link(x)
                assert n[0] == LAST, n[0]
                v.wait_ge(mm, 1)
                nc.vector.tensor_copy(keep["slot_idx"][:, :], pi[0:SLOT2, 0:B * NPAIR])
                nc.vector.tensor_copy(keep["slot_gate"][:, :], pi[0:SLOT2, B * NPAIR:2 * B * NPAIR])
                link(nc.vector.tensor_tensor(keep["slot_row"][:, :], pi[0:SLOT2, 0:B * NPAIR], base[:, :], ALU.add))


LAST = 1 + 3 * ROUNDS - 1 + 1


def experts(nc, m, t, keep):
    with ExitStack() as ctx:
        l = Mem(nc, ctx)
        w1 = l.sb("e_w1", [D, E0, F0])
        w2 = l.sb("e_w2", [D, E0, 2, D])
        brow = l.sb("e_bias_rows", [E0, 3, D])
        bcol = l.sb("e_bias_cols", [D, 3, E0])
        stage = l.sb("gather_rows", [SLOT2, GI * NPAIR], I32)
        got = l.sb("gathered", [SLOT2, GI, NPAIR, D])
        ex = l.sb("expert_in", [D, E0, GI, KTOP])
        hm = l.sb("expert_hidden", [D, 2, 2, GI * KTOP])
        eo = l.sb("expert_out", [D, GI, E0, KTOP])
        vr_ = l.sb("expert_rows", [SLOT2, 2, NPAIR, D])
        hot = l.sb("gated_onehot", [SLOT2, 2, NPAIR, SP])
        toki = l.sb("token_iota_i", [SLOT2, SP], I32)
        tok = l.sb("token_iota", [SLOT2, SP])
        h1 = l.sb("h1_rows", [TP, GI, 2, D])
        h2 = l.sb("h2_rows", [TP, GI, 2, D])
        xn = l.sb("xn2_rows", [TP, GI, 2, D])
        xs = l.sb("xs_rows", [TP, GI, 2, D])
        st = l.sb("e_ln_stats", [TP, 4, 4, 6])
        mv = l.sb("e_meanvar", [TP, 4, 4, 2])
        sc = [l.sb(f"e_scale{i}", [TP, 4, 4]) for i in range(6)]
        pw = l.sb("e_powers", [TP, 5, 4])
        ring = [l.ps(f"ps_e_ring{i}", [D, 512]) for i in range(4)]
        hid = [l.ps(f"ps_e_hidden{i}", [D, 512]) for i in range(4)]
        ident = keep["ident"]
        w_in, cst, bt, bc = (l.sem(n) for n in ("e_w_in", "e_const", "e_bias_tr", "e_bias_ready"))
        gat = [l.sem(f"gathered{i}") for i in range(GI)]
        stg, full, exr, w1d, hmr, eor, rwr, hotr, h2r = (l.sem(n) for n in ("stage_ready", "e_ring_full", "ex_ready", "w1_done", "hidden_ready", "eout_ready", "erows_ready", "hot_ready", "h2_ready"))
        dv, mvr, pp, scr, xsr, rr, h1in, outd = (l.sem(n) for n in ("e_dve", "e_meanvar_ready", "e_pow", "e_scale_ready", "xs_ready", "r_ready", "h1_in", "e_stored"))
        xnd, tokr, held, pheld = (l.sem(n) for n in ("xn2_ready", "token_iota_ready", "e_dve_held", "e_pool_held"))
        NU = 4 * GI

        def u_tr(b):
            return 16 if b == 0 else 15 + 2 * b

        def u_sc(b):
            return 31 if b == GI - 1 else 18 + 2 * b

        use = {}
        for b in range(GI):
            use[b], use[GI + b], use[u_tr(b)], use[u_sc(b)] = (exr, b, 0), (eor, b, 0), (rwr, b, GI), (h2r, b, GI)

        def slot(u):
            return ring[u % 4]

        with nc.Block() as block:

            @block.sync
            def _(sp):
                for i in range(2):
                    sp.dma_start(brow[:, i, :], t["L0_ffn_b1"][:, i * D:(i + 1) * D]).then_inc(w_in, 16)
                sp.dma_start(brow[:, 2, :], t["L0_ffn_b2"]).then_inc(w_in, 16)
                sp.dma_start(w1[:, :, :], t["L0_ffn_W1"].rearrange("e h f -> h e f")).then_inc(w_in, 16)
                sp.dma_start(w2[:, :, :, :], t["L0_ffn_W2"].rearrange("e (c p) h -> p e c h", p=D)).then_inc(w_in, 16)

                with sp.Fori(0, NG) as g:
                    sp.wait_ge(h2r, 8 * g + GI)
                    sp.dma_start(h1[:, :, :, :], t["h1"][bass.ds(g * GI, GI)].rearrange("b (t p) d -> p b t d", p=TP)).then_inc(h1in, 16)
                    sp.wait_ge(rr, 4 * g + 4)
                    sp.dma_start(t["res2"][bass.ds(g * GI, GI)].rearrange("b (t p) d -> p b t d", p=TP), h2[:, :, :, :]).then_inc(outd, 16)
                    sp.wait_ge(xsr, 4 * g + 4)
                    sp.dma_start(t["xs"][bass.ds(g * GI, GI)].rearrange("b (t p) d -> p b t d", p=TP), xs[:, :, :, :]).then_inc(outd, 16)
                sp.wait_ge(outd, 32 * NG + 32)

            @block.gpsimd
            def _(pool):
                def gathers(g):
                    nc.gpsimd.tensor_copy(stage[:, :], keep["slot_row"][:, bass.ds(g * GI * NPAIR, GI * NPAIR)]).then_inc(stg, 1)
                    hold(pool, stg, g + 1, pheld)
                    for b in range(GI):
                        if not isinstance(g, int):
                            hold(pool, full, NU * (g - 1) + b + 1, pheld)
                        for j in range(NPAIR):
                            nc.gpsimd.indirect_dma_start(got[:, b, j, :], None, t["xn1"].rearrange("b s d -> (b s) d"),
                                                         bass.IndirectOffsetOnAxis(ap=stage[:, b * NPAIR + j:b * NPAIR + j + 1], axis=0)).then_inc(gat[b], 16)

                def scales(g):
                    for k in range(4):
                        n = 6 * (4 * g + k)
                        pool.wait_ge(mvr, 4 * g + k + 1)
                        vare, rstd, vr, ms, rms, inv = (s[:, k, :] for s in sc)
                        steps = [
                            (vare, mv[:, k, :, 1], pw[:, 3, :], ALU.add),
                            (rstd, vare, pw[:, 0, :], ALU.pow),
                            (vr, mv[:, k, :, 1], rstd, ALU.mult),
                            (ms, vr, rstd, ALU.mult),
                            (rms, ms, pw[:, 1, :], ALU.pow),
                            (vare, rms, pw[:, 4, :], ALU.add),
                        ]
                        for i, step in enumerate(steps):
                            nc.gpsimd.tensor_tensor(*step).then_inc(pp, 1)
                            pool.wait_ge(pp, n + i + 1)
                        nc.gpsimd.tensor_tensor(inv, vare, pw[:, 2, :], ALU.pow).then_inc(scr, 1)

                nc.gpsimd.iota(toki[:, :], pattern=[[1, SP]], base=0, channel_multiplier=0).then_inc(cst, 1)
                for i, p in enumerate((-0.5, 0.5, -1.0, EPS, 1e-8)):
                    nc.gpsimd.memset(pw[:, i, :], p).then_inc(cst, 1)
                pool.wait_ge(cst, 6)
                pool.sem_inc(outd, 32)
                gathers(0)
                with pool.Fori(0, NG - 1) as g:
                    for b in range(GI):
                        pool.wait_ge(gat[b], 64 * g + 64)
                    gathers(g + 1)
                    scales(g)
                scales(NG - 1)

            @block.tensor
            def _(pe):
                def take(g, u):
                    s, b, credit = use[(u - 4) % NU]
                    assert u >= 4 or credit
                    pe.wait_ge(s, GI * g + b + 1 + (credit if u >= 4 else 0))

                def hidden(g, e):
                    if e == 0:
                        pe.wait_ge(exr, GI * g + GI)
                    pe.wait_ge(hmr, GI * g + e + 1)
                    for c in range(2):
                        x = nc.tensor.matmul(hid[2 * (e % 2) + c][:, 0:GI * KTOP], w1[:, e, c * D:(c + 1) * D], ex[:, e, :, :].rearrange("p b k -> p (b k)"), start=True, stop=True)
                    x.then_inc(w1d, 1)

                def output(g, e):
                    take(g, GI + e)
                    pe.wait_ge(hmr, GI * g + e + 3)
                    for c in range(2):
                        x = nc.tensor.matmul(slot(GI + e)[:, 0:GI * KTOP], w2[:, e, c, :], hm[:, e % 2, c, :], start=c == 0, stop=c == 1)
                    x.then_inc(full, 1)

                def to_rows(g, b):
                    take(g, u_tr(b))
                    if b == 0:
                        pe.wait_ge(eor, GI * g + GI)
                    for j in range(NPAIR):
                        x = nc.tensor.transpose(slot(u_tr(b))[0:SLOT2, j * D:(j + 1) * D], eo[:, b, 2 * j:2 * j + 2, :].rearrange("p e k -> p (e k)"), ident[:, :])
                    x.then_inc(full, 1)

                def spread(g, b):
                    take(g, u_sc(b))
                    pe.wait_ge(rwr, GI * g + b + 1 + GI)
                    pe.wait_ge(hotr, GI * g + b + 1)
                    for q in range(2):
                        for j in range(NPAIR):
                            x = nc.tensor.matmul(slot(u_sc(b))[0:TP, q * D:(q + 1) * D], hot[:, b % 2, j, q * TP:(q + 1) * TP], vr_[:, b % 2, j, :], start=j == 0, stop=j == NPAIR - 1)
                    x.then_inc(full, 1)

                pe.wait_ge(w_in, 80)
                for i in range(3):
                    x = nc.tensor.transpose(hid[0][:, i * E0:(i + 1) * E0], brow[:, i, :], ident[0:E0, 0:E0])
                x.then_inc(bt, 1)
                pe.wait_ge(bc, 1)
                with pe.Fori(0, NG) as g:
                    for b in range(GI):
                        take(g, b)
                        pe.wait_ge(gat[b], 64 * g + 64)
                        for j in range(NPAIR):
                            x = nc.tensor.transpose(slot(b)[:, j * SLOT2:(j + 1) * SLOT2], got[:, b, j, :], ident[0:SLOT2, 0:SLOT2])
                        x.then_inc(full, 1)
                    hidden(g, 0)
                    for e in range(E0):
                        if e + 1 < E0:
                            hidden(g, e + 1)
                        output(g, e)
                    to_rows(g, 0)
                    for b in range(GI):
                        if b + 1 < GI:
                            to_rows(g, b + 1)
                        spread(g, b)

            @block.scalar
            def _(act):
                act.wait_ge(bt, 1)
                nc.scalar.copy(bcol[:, :, :].rearrange("p i e -> p (i e)"), hid[0][:, 0:3 * E0]).then_inc(bc, 1)
                act.wait_ge(bc, 1)
                act.sem_inc(hmr, 2)
                act.sem_inc(rwr, GI)

                def rescale(g, k):
                    act.wait_ge(scr, 4 * g + k + 1)
                    act.wait_ge(rr, 4 * g + k + 1)
                    if k == 0:
                        act.wait_ge(outd, 32 * g + 32)
                    for q in range(4):
                        x = nc.scalar.activation(xs[:, 2 * k + q // 2, q % 2, :], xn[:, 2 * k + q // 2, q % 2, :], ACT.Copy, scale=sc[5][:, k, q:q + 1])
                    x.then_inc(xsr, 1)

                with act.Fori(0, NG) as g:
                    for e in range(E0):
                        act.wait_ge(w1d, GI * g + e + 1)
                        if e >= 2:
                            act.wait_ge(full, NU * g + GI + e - 1)
                        for c in range(2):
                            x = nc.scalar.activation(hm[:, e % 2, c, :], hid[2 * (e % 2) + c][:, 0:GI * KTOP], ACT.Gelu, bias=bcol[:, c, e:e + 1])
                        x.then_inc(hmr, 1)
                    for b in range(GI):
                        act.wait_ge(full, NU * g + u_tr(b) + 1)
                        nc.scalar.copy(vr_[:, b % 2, :, :].rearrange("p j d -> p (j d)"), slot(u_tr(b))[0:SLOT2, :]).then_inc(rwr, 1)
                        if b >= 4 and b % 2 == 1:
                            rescale(g, b // 2 - 2)
                    rescale(g, 2)
                    rescale(g, 3)

            @block.vector
            def _(v):
                v.wait_ge(cst, 6)
                nc.vector.tensor_copy(tok[:, :], toki[:, :]).then_inc(tokr, 1)
                v.wait_ge(tokr, 1)
                v.sem_inc(h2r, GI)

                def onehots(g, b):
                    for j in range(NPAIR):
                        col = g * (GI * NPAIR) + b * NPAIR + j
                        x = nc.vector.tensor_scalar(hot[:, b % 2, j, :], tok[:, :], keep["slot_idx"][:, bass.ds(col, 1)], keep["slot_gate"][:, bass.ds(col, 1)], ALU.is_equal, ALU.mult)
                    x.then_inc(hotr, 1)

                def stats(g, k):
                    v.wait_ge(h2r, GI * g + 2 * k + 2 + GI)
                    for q in range(4):
                        x = nc.vector.bn_stats(st[:, k, q, :], h2[:, 2 * k + q // 2, q % 2, :])
                    x.then_inc(dv, 1)
                    hold(v, dv, 4 * g + k + 1, held)
                    for q in range(4):
                        x = nc.vector.bn_aggr(mv[:, k, q, :], st[:, k, q, :])
                    x.then_inc(mvr, 1)

                def normalise(g, k):
                    v.wait_ge(scr, 4 * g + k + 1)
                    for q in range(4):
                        x = nc.vector.tensor_scalar(xn[:, 2 * k + q // 2, q % 2, :], h2[:, 2 * k + q // 2, q % 2, :], mv[:, k, q, 0:1], sc[1][:, k, q:q + 1], ALU.subtract, ALU.mult)
                    x.then_inc(xnd, 1)
                    v.wait_ge(xnd, 4 * g + k + 1)
                    a = h2[:, 2 * k:2 * k + 2, :, :].rearrange("p i q d -> p (i q d)")
                    nc.vector.tensor_tensor(a, a, xn[:, 2 * k:2 * k + 2, :, :].rearrange("p i q d -> p (i q d)"), ALU.add).then_inc(rr, 1)

                v.wait_ge(bc, 1)
                with v.Fori(0, NG) as g:
                    for b in range(GI):
                        v.wait_ge(full, NU * g + b + 1)
                        nc.vector.tensor_copy(ex[:, :, b, :], slot(b)[:, 0:E0 * KTOP].rearrange("p (e k) -> p e k", k=KTOP)).then_inc(exr, 1)
                    onehots(g, 0)
                    onehots(g, 1)
                    for e in range(E0):
                        v.wait_ge(full, NU * g + GI + e + 1)
                        nc.vector.tensor_scalar(eo[:, :, e, :], slot(GI + e)[:, 0:GI * KTOP].rearrange("p (b k) -> p b k", k=KTOP), bcol[:, 2, e:e + 1], None, ALU.add).then_inc(eor, 1)
                    v.wait_ge(h1in, 16 * g + 16)
                    v.wait_ge(outd, 32 * g + 32)
                    for b in range(GI):
                        v.wait_ge(full, NU * g + u_sc(b) + 1)
                        nc.vector.tensor_tensor(h2[:, b, :, :].rearrange("p q d -> p (q d)"), slot(u_sc(b))[0:TP, 0:2 * D], h1[:, b, :, :].rearrange("p q d -> p (q d)"), ALU.add).then_inc(h2r, 1)
                        if b + 2 < GI:
                            onehots(g, b + 2)
                        if b % 2 == 1:
                            stats(g, b // 2)
                            if b >= 3:
                                normalise(g, b // 2 - 1)
                    normalise(g, 3)


E1, F1 = 8, 64
NC1 = E1 * F1 // D
CPU = 4
TU = 6
NU1 = SP // TU
NT = TU // 2
COL = TU * B


def load_layer1(sp, t, w, pick, sem):
    one = lambda v: v.rearrange("(p a) -> p a", a=1)
    row = lambda v, n: v.rearrange("(a p) -> a p", a=1).broadcast_to(n)
    pairs = [
        (w["wv"][:, :], t["L1_attn_Wv"]), (w["bv"][:, :], row(t["L1_attn_bv"], [TP, 2 * D])),
        (w["wu"][:, :], t["L1_attn_Wu"]), (w["bo"][:, :], row(t["L1_attn_bo"], [D, D])),
        (w["bu"][:, 0:1], one(t["L1_attn_bu"][0:D])), (w["bu"][:, 1:2], one(t["L1_attn_bu"][D:2 * D])),
        (w["wo"][:, :, :], t["L1_attn_Wo"].rearrange("(a p) d -> p a d", p=D)),
        (w["router"][:, :], t["L1_ffn_router"]),
        (w["gate"][:, :, :], t["L1_ffn_W_gate"].rearrange("e d h -> d e h")),
        (w["up"][:, :, :], t["L1_ffn_W_up"].rearrange("e d h -> d e h")),
        (w["sgate"][:, :], t["L1_ffn_shared_gate"]), (w["sup"][:, :], t["L1_ffn_shared_up"]),
        (w["down"][:, :, :], t["L1_ffn_W_down"].rearrange("(i a) h d -> (a h) i d", a=2)),
        (w["sdown"][:, :], t["L1_ffn_shared_down"]),
        (pick[:, :, :], t["pick"]), (w["expid"][:, :], t["expid"].broadcast_to([D, E1])),
    ]
    for dst, src in pairs:
        sp.dma_start(dst, src).then_inc(sem, 16)
    return 16 * len(pairs)


def layer1(nc, m, t, keep):
    with ExitStack() as ctx:
        l = Mem(nc, ctx)
        w = {
            "wv": l.sb("l1_wv", [D, 2 * D]), "bv": l.sb("l1_bv", [TP, 2 * D]), "wu": l.sb("l1_wu", [D, 2 * D]),
            "bo": l.sb("l1_bo", [D, D]), "bu": l.sb("l1_bu", [D, 2]), "wo": l.sb("l1_wo", [D, 2, D]),
            "router": l.sb("l1_router", [D, E1]), "gate": l.sb("l1_gate", [D, E1, F1]), "up": l.sb("l1_up", [D, E1, F1]),
            "sgate": l.sb("l1_sgate", [D, F1]), "sup": l.sb("l1_sup", [D, F1]), "down": l.sb("l1_down", [D, NC1, D]),
            "sdown": l.sb("l1_sdown", [F1, D]), "pick": l.sb("l1_pick", [D, NC1, D], BF16),
            "identb": l.sb("identb", [D, D], BF16), "expid": l.sb("expert_ids", [D, E1]),
        }
        mixer = l.sb("mixer_values", [D, D, 4 * B])
        values(nc, t, keep, w, mixer)
        mix_tokens(nc, t, keep, mixer)
        finish(nc, t, keep, w, mixer)


def values(nc, t, keep, w, mixer):
    with ExitStack() as ctx:
        l = Mem(nc, ctx)
        xs = l.sb("v_xs", [TP, 2, GI, 2, D])
        xsT = l.sb("v_xsT", [D, 2, SP])
        pre = l.sb("v_pre", [TP, 2, 2, 2 * D])
        pick = l.sb("l1_pick_fp32", [D, NC1, D])
        pT = [l.ps(f"ps_v_T{i}", [D, 512]) for i in range(2)]
        pV = [l.ps(f"ps_v{i}", [D, 512]) for i in range(2)]
        ident = keep["ident"]
        xin = [l.sem(f"v_xs_in{i}") for i in range(2)]
        w_in, turned, xtr, mm, prer, vr = (l.sem(n) for n in ("l1_w_in", "v_turned", "v_xsT_ready", "v_mm", "v_pre_ready", "v_ready"))
        with nc.Block() as block:

            @block.sync
            def _(sp):
                def load(g, par):
                    sp.dma_start(xs[:, par, :, :, :], t["xs"][bass.ds(g * GI, GI)].rearrange("b (t p) d -> p b t d", p=TP)).then_inc(xin[par], 16)

                load(0, 0)
                load(1, 1)
                n = load_layer1(sp, t, w, pick, w_in)
                with sp.Fori(1, NG // 2) as it:
                    for par in range(2):
                        sp.wait_ge(turned, GI * (2 * it + par - 1))
                        load(2 * it + par, par)
                sp.wait_ge(w_in, n)

            @block.gpsimd
            def _(pool):
                pool.wait_ge(w_in, 16 * 16)
                nc.gpsimd.tensor_copy(w["pick"][:, :, :], pick[:, :, :])
                nc.gpsimd.tensor_copy(w["identb"][:, :], ident[:, :])

            @block.tensor
            def _(pe):
                def turn(g, par, b, half):
                    if b == 0:
                        pe.wait_ge(xin[par], 16 * half + 16)
                    i = GI * g + b
                    pe.wait_ge(xtr, i + 1)
                    for q in range(2):
                        x = nc.tensor.transpose(pT[b % 2][:, q * TP:(q + 1) * TP], xs[:, par, b, q, :], ident[0:TP, 0:TP])
                    x.then_inc(turned, 1)

                def project(g, b):
                    i = GI * g + b
                    pe.wait_ge(xtr, i + 3)
                    pe.wait_ge(prer, i + 1)
                    for q in range(2):
                        x = nc.tensor.matmul(pV[b % 2][0:TP, q * 2 * D:(q + 1) * 2 * D], xsT[:, b % 2, q * TP:(q + 1) * TP], w["wv"][:, :], start=True, stop=True)
                    x.then_inc(mm, 1)

                pe.wait_ge(w_in, 16 * 16)
                with pe.Fori(0, NG // 2) as it:
                    for par in range(2):
                        g = it * 2 + par
                        turn(g, par, 0, it)
                        for b in range(GI):
                            if b + 1 < GI:
                                turn(g, par, b + 1, it)
                            project(g, b)

            @block.vector
            def _(v):
                v.sem_inc(prer, 2)
                v.wait_ge(w_in, 16 * 16)
                with v.Fori(0, NG) as g:
                    for b in range(GI):
                        i = GI * g + b
                        v.wait_ge(mm, i + 1)
                        v.wait_ge(vr, i + 1)
                        nc.vector.tensor_tensor(pre[:, b % 2, :, :], pV[b % 2][0:TP, :].rearrange("p (q c) -> p q c", q=2),
                                                w["bv"][:, :].unsqueeze(1).broadcast_to([TP, 2, 2 * D]), ALU.add).then_inc(prer, 1)

            @block.scalar
            def _(act):
                act.sem_inc(xtr, 2)
                act.sem_inc(vr, 2)

                def turned_(g, b):
                    i = GI * g + b
                    act.wait_ge(turned, i + 1)
                    if not (isinstance(g, int) and i < 2):
                        act.wait_ge(mm, i - 1)
                    src = pT[b % 2][:, 0:SP].rearrange("p (q n) -> p q n", q=2)[:, :, ::-1]
                    nc.scalar.copy(xsT[:, b % 2, :].rearrange("p (q n) -> p q n", q=2), src).then_inc(xtr, 1)

                def gate(g, b):
                    i = GI * g + b
                    act.wait_ge(prer, i + 3)
                    dst = mixer[0:TP, :, :].rearrange("p c (n b) -> p n c b", b=B)
                    for q in range(2):
                        o = dst[:, 2 * q:2 * q + 2, :, bass.ds(i, 1)]
                        x = nc.scalar.activation(o, pre[:, b % 2, q, :].rearrange("p (h c a) -> p h c a", h=2, a=1), ACT.Silu)
                    x.then_inc(vr, 1)

                def body(g):
                    for b in range(GI):
                        turned_(g, b)
                        if b:
                            gate(g, b - 1)
                    gate(g, GI - 1)

                body(0)
                with act.Fori(1, NG) as g:
                    body(g)


def mix_tokens(nc, t, keep, mixer):
    with ExitStack() as ctx:
        l = Mem(nc, ctx)
        nu = D // CPU
        toep = l.sb("toeplitz", [TP, 4, 2, CPU, SP])
        stage = l.sb("mixer_stage", [TP, 2, CPU, 4 * B])
        pm = [l.ps(f"ps_mix{i}", [D, 512]) for i in range(4)]
        tin = [l.sem(f"toeplitz_in{i}") for i in range(4)]
        stg, mm, outa, outb, held = (l.sem(n) for n in ("mix_staged", "mix_mm", "mix_out_act", "mix_out_dve", "mix_pool_held"))
        width = TP - 1 + SP
        with nc.Block() as block:

            @block.sync
            def _(sp):
                ap = t["apad"]

                def load(u, r):
                    for h in range(2):
                        src = bass.AP(ap.tensor, u * (CPU * width) + h * D * width, [[1, TP], [width, CPU], [1, SP]])
                        sp.dma_start(toep[:, r, h, :, :], src).then_inc(tin[r], 16)

                for r in range(4):
                    load(r, r)
                with sp.Fori(1, nu // 4) as it:
                    for r in range(4):
                        sp.wait_ge(mm, 2 * (4 * it + r - 3))
                        load(4 * it + r, r)

            @block.gpsimd
            def _(pool):
                def copy(u, r):
                    nc.gpsimd.tensor_copy(stage[:, r, :, :], mixer[0:TP, bass.ds(u * CPU, CPU), :]).then_inc(stg, 1)

                copy(0, 0)
                copy(1, 1)
                with pool.Fori(1, nu // 2) as it:
                    for r in range(2):
                        hold(pool, mm, 2 * (2 * it + r - 1), held)
                        copy(2 * it + r, r)

            @block.tensor
            def _(pe):
                with pe.Fori(0, nu // 4) as it:
                    for r in range(4):
                        u = it * 4 + r
                        pe.wait_ge(tin[r], 32 * it + 32)
                        pe.wait_ge(stg, u + 1)
                        for c in range(CPU // 2):
                            pe.wait_ge((outa, outb)[c], u + 1)
                            bank = pm[(r % 2) * 2 + c]
                            for k in range(2):
                                cp = 2 * c + k
                                for q in range(2):
                                    for h in range(2):
                                        o = bank[h * B:(h + 1) * B, k * SP + q * TP:(k + 1) * SP]
                                        x = nc.tensor.matmul(o, stage[:, r % 2, cp, (2 * q + h) * B:(2 * q + h + 1) * B],
                                                             toep[:, r, h, cp, 0:SP - q * TP], start=q == 0, stop=q == 1, skip_group_check=True)
                            x.then_inc(mm, 1)

            def evacuate(eng, copy, sem, c):
                eng.sem_inc(sem, 2)
                with eng.Fori(0, nu // 2) as it:
                    for r in range(2):
                        u = it * 2 + r
                        eng.wait_ge(mm, 2 * u + c + 1)
                        copy(mixer[:, bass.ds(u * CPU + 2 * c, 2), 0:SP], pm[r * 2 + c][:, 0:2 * SP].rearrange("p (k n) -> p k n", k=2)).then_inc(sem, 1)

            @block.scalar
            def _(act):
                evacuate(act, nc.scalar.copy, outa, 0)

            @block.vector
            def _(v):
                evacuate(v, nc.vector.tensor_copy, outb, 1)


def finish(nc, t, keep, w, mixer):
    order = ["xsT", "gate0", "up0", "u0", "u1", "mixT0", "mixT1", "gate1", "up1", "proj", "gate2", "up2",
             "gate3", "up3", "gate4", "up4", "combT", "bc0", "bc1", "bc2", "bc3", "down", "normT", "router"]
    count = {"xsT": 1, "gate": NC1 + 1, "up": NC1 + 1, "u": 2, "mixT": 2, "proj": 1, "combT": 1, "bc": NC1, "normT": 1, "down": 1, "router": 1}
    back = {"gate", "up", "combT", "bc", "down"}
    nb = 8
    with ExitStack() as ctx:
        l = Mem(nc, ctx)
        xs = l.sb("f_xs", [D, 3, NT, D])
        res = l.sb("f_res", [D, 3, NT, D])
        xsT = l.sb("f_xsT", [D, COL])
        us = l.sb("f_u", [D, 2, COL])
        stage = l.sb("f_mixed", [D, TU, D])
        y = l.sb("f_y", [D, 2, COL])
        h3 = l.sb("f_h3", [D, 3, NT, D])
        xn = l.sb("f_xn", [D, NT, D])
        xnT = l.sb("f_xnT", [D, COL])
        gs = l.sb("f_gate", [D, NC1 + 1, COL])
        gu = l.sb("f_hidden", [D, NC1 + 1, COL])
        st = l.sb("f_stats", [D, NT, 6])
        mv = l.sb("f_meanvar", [D, NT, 2])
        vare = l.sb("f_var_eps", [D, NT])
        rstd = l.sb("f_rstd", [D, NT])
        cons = l.sb("f_consts", [D, 4, NT * E1])
        nmean = l.sb("f_minus_mean", [D, NT])
        shift = l.sb("f_shift", [D, NT])
        lmax = l.sb("f_lmax", [D, NT])
        lsub = l.sb("f_lsub", [D, NT, E1])
        lexp = l.sb("f_lexp", [D, NT, E1])
        lsum = l.sb("f_lsum", [D, 2, NT])
        prob = l.sb("f_prob", [D, NT, E1])
        top = l.sb("f_top", [D, NT, E1])
        topi = l.sb("f_top_i", [D, NT, E1], U32)
        topf = l.sb("f_top_f", [D, NT, E1])
        eq = l.sb("f_eq", [D, 2, NT, E1])
        toppart = l.sb("f_top_part", [D, NT, 3, 2], BF16)
        toprest = l.sb("f_top_rest", [D, 2, NT, 2])
        scaled = l.sb("f_scaled", [D, 2, NT, 3, E1])
        split = l.sb("f_split", [D, NT, D], BF16)
        combT = l.sb("f_combT", [D, COL], BF16)
        bank = [l.ps(f"ps_f{i}", [D, 512]) for i in range(nb)]
        ident = keep["ident"]
        filled = {s: l.sem(f"{s}_filled") for s in count}
        read = {s: l.sem(f"{s}_read") for s in count}
        xin, rin = [l.sem(f"f_xs_in{i}") for i in range(3)], [l.sem(f"f_res_in{i}") for i in range(3)]
        staged, resb, cst, held = (l.sem(n) for n in ("f_staged", "f_res_bias", "f_const", "f_pool_held"))
        mvr, veps, rsr, xnr, lsr, expr_, cbr, hidr = (l.sem(n) for n in ("f_meanvar_ready", "f_vareps_ready", "f_rstd_ready", "f_xn_ready", "f_lsub_ready", "f_lexp_ready", "f_split_ready", "f_hidden_ready"))
        dv, dheld, stored = l.sem("f_dve"), l.sem("f_dve_held"), [l.sem(f"f_stored{i}") for i in range(3)]
        zero, sts, lmr = l.sem("f_split_zero"), l.sem("f_stats_ready"), l.sem("f_lmax_ready")

        def parts(s):
            name = s.rstrip("01234")
            return name, int(s[len(name):] or 0)

        def psum(s):
            return bank[order.index(s) % nb]

        def take(pe, n, s):
            i = order.index(s) - nb
            while isinstance(n, int) and n == NU1 and i >= 0 and parts(order[i])[0] not in back:
                i -= nb
            name, k = parts(order[i])
            unit = n - (name in back) - (i < 0)
            if not (isinstance(n, int) and unit < -1):
                pe.wait_ge(read[name], count[name] * (unit + 1) + k + 1)

        def wait(eng, sems, unit, s):
            name, k = parts(s)
            eng.wait_ge(sems[name], count[name] * (unit + (sems is read)) + k + 1)

        def each_step(eng, step):
            step(0, 0, 0, True, False)
            with eng.Fori(0, (NU1 - 3) // 3) as it:
                for r in range(3):
                    step(3 * it + r + 1, (r + 1) % 3, it + (r + 1) // 3, True, True)
            n = 3 * ((NU1 - 3) // 3) + 1
            while n <= NU1:
                step(n, n % 3, n // 3, n < NU1, True)
                n += 1

        with nc.Block() as block:

            @block.sync
            def _(sp):
                def rows(d, n, r):
                    return t[d].rearrange("b (u j r) d -> r b u j d", j=NT, r=2)[r][:, bass.ds(n, 1)].rearrange("b u j d -> b (u j) d")

                def load(n, par):
                    for r in range(2):
                        sp.dma_start(xs[r * B:(r + 1) * B, par, :, :], rows("xs", n, r)).then_inc(xin[par], 16)
                        sp.dma_start(res[r * B:(r + 1) * B, par, :, :], rows("res2", n, r)).then_inc(rin[par], 16)

                def store(n, par):
                    wait(sp, read, n, "down")
                    for r in range(2):
                        k = NT - 1 if isinstance(n, int) and n == NU1 - 1 and r == 1 else NT
                        o = bass.AP(t["out"].tensor, n * (TU * D) + r * D, [[S * D, B], [2 * D, k], [1, D]])
                        sp.dma_start(o, h3[r * B:(r + 1) * B, par, 0:k, :]).then_inc(stored[par], 16)

                for n in range(2):
                    load(n, n)

                def step(n, par, half, front, backs):
                    if front and not (isinstance(n, int) and n + 2 >= NU1):
                        if not (isinstance(n, int) and n == 0):
                            wait(sp, read, n - 1, "proj")
                        load(n + 2, (par + 2) % 3)
                    if backs:
                        store(n - 1, (par + 2) % 3)

                each_step(sp, step)
                for i in range(3):
                    sp.wait_ge(stored[i], 32 * (NU1 // 3) + 32)

            @block.gpsimd
            def _(pool):
                nc.gpsimd.memset(cons[:, 0, :], EPS).then_inc(cst, 1)
                nc.gpsimd.memset(cons[:, 1, :], -0.5).then_inc(cst, 1)
                nc.gpsimd.memset(cons[:, 2, :], 2.718281828459045).then_inc(cst, 1)
                nc.gpsimd.memset(split[:, :, :], 0.0).then_inc(zero, 1)
                for i in range(3):
                    pool.sem_inc(stored[i], 32)
                nc.gpsimd.memset(cons[:, 3, :], 0.0).then_inc(cst, 1)
                pool.wait_ge(cst, 4)

                def copy(n):
                    nc.gpsimd.tensor_copy(stage[:, :, :], mixer[:, :, bass.ds(n * TU, TU)].rearrange("p c t -> p t c")).then_inc(staged, 1)

                copy(0)

                def step(n, par, half, front, backs):
                    if not front:
                        return
                    pool.wait_ge(rin[par], 32 * half + 32)
                    nc.gpsimd.tensor_tensor(res[:, par, :, :], res[:, par, :, :], w["bo"][:, :].unsqueeze(1).broadcast_to([D, NT, D]), ALU.add).then_inc(resb, 1)
                    if not (isinstance(n, int) and n == NU1 - 1):
                        hold(pool, filled["mixT"], 2 * n + 2, held)
                        copy(n + 1)
                    pool.wait_ge(mvr, n + 1)
                    nc.gpsimd.tensor_tensor(vare[:, :], mv[:, :, 1], cons[:, 0, 0:NT], ALU.add).then_inc(veps, 1)
                    nc.gpsimd.tensor_tensor(nmean[:, :], cons[:, 3, 0:NT], mv[:, :, 0], ALU.subtract).then_inc(veps, 1)
                    pool.wait_ge(veps, 2 * n + 2)
                    nc.gpsimd.tensor_tensor(rstd[:, :], vare[:, :], cons[:, 1, 0:NT], ALU.pow).then_inc(rsr, 1)
                    pool.wait_ge(rsr, 2 * n + 1)
                    nc.gpsimd.tensor_tensor(shift[:, :], nmean[:, :], rstd[:, :], ALU.mult).then_inc(rsr, 1)
                    pool.wait_ge(read["router"], n + 2)
                    nc.gpsimd.tensor_tensor(lexp[:, :, :].rearrange("p j e -> p (j e)"), cons[:, 2, :], lsub[:, :, :].rearrange("p j e -> p (j e)"), ALU.pow).then_inc(expr_, 1)

                each_step(pool, step)

            @block.tensor
            def _(pe):
                def step(n, par, half, front, backs):
                    def gate_up(i):
                        for s, big, small in (("gate", "gate", "sgate"), ("up", "up", "sup")):
                            take(pe, n, f"{s}{i}")
                            k = D if i < NC1 else F1
                            lhs = w[big][:, 2 * i:2 * i + 2, :].rearrange("p e h -> p (e h)") if i < NC1 else w[small][:, :]
                            nc.tensor.matmul(psum(f"{s}{i}")[0:k, 0:COL], lhs, xnT[:, :], start=True, stop=True).then_inc(filled[s], 1)

                    if front:
                        take(pe, n, "xsT")
                        pe.wait_ge(xin[par], 32 * half + 32)
                        for j in range(NT):
                            x = nc.tensor.transpose(psum("xsT")[:, j * D:(j + 1) * D], xs[:, par, j, :], ident[:, :])
                        x.then_inc(filled["xsT"], 1)
                    if backs:
                        gate_up(0)
                    if front:
                        wait(pe, read, n, "xsT")
                        for h in range(2):
                            take(pe, n, f"u{h}")
                            nc.tensor.matmul(psum(f"u{h}")[:, 0:COL], w["wu"][:, h * D:(h + 1) * D], xsT[:, :], start=True, stop=True).then_inc(filled["u"], 1)
                        pe.wait_ge(staged, n + 1)
                        for h in range(2):
                            take(pe, n, f"mixT{h}")
                            for k in range(TU // 2):
                                x = nc.tensor.transpose(psum(f"mixT{h}")[:, k * D:(k + 1) * D], stage[:, h * (TU // 2) + k, :], ident[:, :])
                            x.then_inc(filled["mixT"], 1)
                    if backs:
                        gate_up(1)
                    if front:
                        take(pe, n, "proj")
                        wait(pe, read, n, "mixT1")
                        for j in range(NT):
                            for h in range(2):
                                x = nc.tensor.matmul(psum("proj")[:, j * D:(j + 1) * D], y[:, h, j * D:(j + 1) * D], w["wo"][:, h, :], start=h == 0, stop=h == 1)
                        x.then_inc(filled["proj"], 1)
                    if backs:
                        gate_up(2)
                        gate_up(3)
                        gate_up(4)
                        take(pe, n, "combT")
                        pe.wait_ge(cbr, n)
                        for j in range(NT):
                            x = nc.tensor.transpose(psum("combT")[:, j * D // 2:(j + 1) * D // 2].bitcast(BF16), split[:, j, :], w["identb"][:, :])
                        x.then_inc(filled["combT"], 1)
                        wait(pe, read, n - 1, "combT")
                        for i in range(NC1):
                            take(pe, n, f"bc{i}")
                            nc.tensor.matmul(psum(f"bc{i}")[:, 0:COL], w["pick"][:, i, :], combT[:, :], start=True, stop=True).then_inc(filled["bc"], 1)
                    def down(i):
                        wait(pe, read, n - 1, f"bc{i}")
                        for j in range(NT):
                            x = nc.tensor.matmul(psum("down")[:, j * D:(j + 1) * D], gu[:, i, j * D:(j + 1) * D], w["down"][:, i, :], start=False, stop=i == NC1 - 1, skip_group_check=True)
                        return x

                    if backs:
                        take(pe, n, "down")
                        wait(pe, read, n - 1, "up4")
                        for j in range(NT):
                            nc.tensor.matmul(psum("down")[:, j * D:(j + 1) * D], gu[0:F1, NC1, j * D:(j + 1) * D], w["sdown"][:, :], start=j == 0, stop=False, skip_group_check=True)
                        for i in range(NC1 - 1):
                            down(i)
                    if front:
                        take(pe, n, "normT")
                        pe.wait_ge(xnr, n + 1)
                        for j in range(NT):
                            x = nc.tensor.transpose(psum("normT")[:, j * D:(j + 1) * D], xn[:, j, :], ident[:, :])
                        x.then_inc(filled["normT"], 1)
                    if backs:
                        down(NC1 - 1).then_inc(filled["down"], 1)
                    if front:
                        take(pe, n, "router")
                        wait(pe, read, n, "normT")
                        for j in range(NT):
                            x = nc.tensor.matmul(psum("router")[:, j * E1:(j + 1) * E1], xnT[:, j * D:(j + 1) * D], w["router"][:, :], start=True, stop=True)
                        x.then_inc(filled["router"], 1)

                each_step(pe, step)

            @block.scalar
            def _(act):
                for s in ("xsT", "gate", "u", "combT", "normT"):
                    act.sem_inc(read[s], count[s])

                def step(n, par, half, front, backs):
                    def gate(i):
                        wait(act, filled, n - 1, f"gate{i}")
                        k = D if i < NC1 else F1
                        nc.scalar.activation(gs[0:k, i, :], psum(f"gate{i}")[0:k, 0:COL], ACT.Silu).then_inc(read["gate"], 1)

                    if front:
                        wait(act, filled, n, "xsT")
                        nc.scalar.copy(xsT[:, :], psum("xsT")[:, 0:COL]).then_inc(read["xsT"], 1)
                    if backs:
                        wait(act, read, n - 2, "up4")
                        gate(0)
                    if front:
                        wait(act, read, n - 1, "mixT1")
                        for h in range(2):
                            wait(act, filled, n, f"u{h}")
                            nc.scalar.activation(us[:, h, :], psum(f"u{h}")[:, 0:COL], ACT.Silu, bias=w["bu"][:, h:h + 1]).then_inc(read["u"], 1)
                    if backs:
                        for i in range(1, NC1 + 1):
                            gate(i)
                        wait(act, filled, n - 1, "combT")
                        nc.scalar.copy(combT[:, :], psum("combT")[:, 0:COL // 2].bitcast(BF16)).then_inc(read["combT"], 1)
                    if front:
                        act.wait_ge(rsr, 2 * n + 2)
                        wait(act, read, n - 1, "normT")
                        for j in range(NT):
                            x = nc.scalar.activation(xn[:, j, :], h3[:, par, j, :], ACT.Identity, bias=shift[:, j:j + 1], scale=rstd[:, j:j + 1])
                        x.then_inc(xnr, 1)
                        wait(act, filled, n, "normT")
                        nc.scalar.copy(xnT[:, :], psum("normT")[:, 0:COL]).then_inc(read["normT"], 1)

                each_step(act, step)

            @block.vector
            def _(v):
                for s in ("up", "mixT", "proj", "bc", "down", "router"):
                    v.sem_inc(read[s], count[s])
                v.wait_ge(zero, 1)
                NL = 13

                def step(n, par, half, front, backs):
                    u = n - 1
                    i = [0]

                    def link(x):
                        i[0] += 1
                        x.then_inc(dv, 1)

                    def linked():
                        v.wait_ge(dv, NL * u + i[0])

                    def up(i):
                        wait(v, filled, n - 1, f"up{i}")
                        wait(v, read, n - 1, f"gate{i}")
                        k = D if i < NC1 else F1
                        if i == 0:
                            wait(v, filled, n - 2, "down") if not (isinstance(n, int) and n < 2) else None
                        nc.vector.tensor_tensor(gu[0:k, i, :], psum(f"up{i}")[0:k, 0:COL], gs[0:k, i, :], ALU.mult).then_inc(read["up"], 1)

                    def softmax():
                        bc = lambda a: a.unsqueeze(2).broadcast_to([D, NT, E1])
                        v.wait_ge(expr_, u + 1)
                        link(nc.vector.tensor_reduce(lsum[:, 0, :], lexp[:, :, :], AX.X, ALU.add))
                        linked()
                        link(nc.vector.reciprocal(lsum[:, 1, :], lsum[:, 0, :]))
                        linked()
                        link(nc.vector.tensor_tensor(prob[:, :, :], lexp[:, :, :], bc(lsum[:, 1, :]), ALU.mult))

                    def best():
                        hold(v, dv, NL * u + i[0], dheld)
                        for j in range(NT):
                            x = nc.vector.max(top[:, j, :], prob[:, j, :])
                        link(x)
                        linked()
                        link(nc.vector.tensor_copy(toppart[:, :, 0, :], top[:, :, 0:2]))

                    def best_index():
                        linked()
                        link(nc.vector.tensor_tensor(toprest[:, 0, :, :], top[:, :, 0:2], toppart[:, :, 0, :], ALU.subtract))
                        for j in range(NT):
                            x = nc.vector.max_index(topi[:, j, :], top[:, j, :], prob[:, j, :])
                        link(x)
                        linked()
                        link(nc.vector.tensor_copy(toppart[:, :, 1, :], toprest[:, 0, :, :]))
                        link(nc.vector.tensor_copy(topf[:, :, 0:2], topi[:, :, 0:2]))

                    def chosen():
                        linked()
                        link(nc.vector.tensor_tensor(toprest[:, 1, :, :], toprest[:, 0, :, :], toppart[:, :, 1, :], ALU.subtract))
                        ids = w["expid"][:, :].unsqueeze(1).broadcast_to([D, NT, E1])
                        for r in range(2):
                            x = nc.vector.tensor_tensor(eq[:, r, :, :], ids, topf[:, :, r:r + 1].broadcast_to([D, NT, E1]), ALU.is_equal)
                        link(x)
                        linked()
                        link(nc.vector.tensor_copy(toppart[:, :, 2, :], toprest[:, 1, :, :]))

                    def weights():
                        linked()
                        for r in range(2):
                            x = nc.vector.tensor_tensor(scaled[:, r, :, :, :], eq[:, r, :, :].unsqueeze(2).broadcast_to([D, NT, 3, E1]),
                                                        toppart[:, :, :, r:r + 1].broadcast_to([D, NT, 3, E1]), ALU.mult)
                        link(x)
                        linked()
                        nc.vector.tensor_tensor(split[:, :, 0:3 * E1].rearrange("p j (c e) -> p j c e", e=E1), scaled[:, 0, :, :, :], scaled[:, 1, :, :, :], ALU.add).then_inc(cbr, 1)
                        assert i[0] == NL, i[0]

                    def mixed(h):
                        wait(v, filled, n, f"mixT{h}")
                        if h == 0:
                            wait(v, read, n, "u1")
                        k = TU // 2
                        a = psum(f"mixT{h}")[:, 0:k * D].rearrange("p (t h b) -> p h t b", t=k, h=2)
                        c = slice(h * k * B, (h + 1) * k * B)
                        for q in range(2):
                            x = nc.vector.tensor_tensor(y[:, q, c].rearrange("p (t b) -> p t b", b=B), a[:, q], us[:, q, c].rearrange("p (t b) -> p t b", b=B), ALU.mult)
                        x.then_inc(read["mixT"], 1)

                    if backs:
                        up(0)
                    if front:
                        mixed(0)
                        mixed(1)
                    if backs:
                        up(1)
                        softmax()
                    if front:
                        v.wait_ge(resb, n + 1)
                        v.wait_ge(stored[par], 32 * half + 32)
                        wait(v, filled, n, "proj")
                        nc.vector.tensor_tensor(h3[:, par, :, :].rearrange("p j d -> p (j d)"), psum("proj")[:, 0:COL], res[:, par, :, :].rearrange("p j d -> p (j d)"), ALU.add).then_inc(read["proj"], 1)
                    if backs:
                        best()
                    if front:
                        wait(v, read, n, "proj")
                        for j in range(NT):
                            x = nc.vector.bn_stats(st[:, j, :], h3[:, par, j, :])
                        x.then_inc(sts, 1)
                    if backs:
                        best_index()
                    if front:
                        hold(v, sts, n + 1, dheld)
                        for j in range(NT):
                            x = nc.vector.bn_aggr(mv[:, j, :], st[:, j, :])
                        x.then_inc(mvr, 1)
                    if backs:
                        chosen()
                        weights()
                        up(2)
                    if backs:
                        up(3)
                        up(4)
                        wait(v, read, n - 1, "up4")
                        for i_ in range(NC1):
                            wait(v, filled, n - 1, f"bc{i_}")
                            nc.vector.tensor_tensor(gu[:, i_, :], gu[:, i_, :], psum(f"bc{i_}")[:, 0:COL], ALU.mult).then_inc(read["bc"], 1)
                        wait(v, filled, n - 1, "down")
                        p = (par + 2) % 3
                        a = h3[:, p, :, :].rearrange("p j d -> p (j d)")
                        nc.vector.tensor_tensor(a, psum("down")[:, 0:COL], a, ALU.add).then_inc(read["down"], 1)
                    if front:
                        wait(v, filled, n, "router")
                        lg = psum("router")[:, 0:NT * E1].rearrange("p (j e) -> p j e", e=E1)
                        nc.vector.tensor_reduce(lmax[:, :], lg, AX.X, ALU.max).then_inc(lmr, 1)
                        v.wait_ge(lmr, n + 1)
                        nc.vector.tensor_tensor(lsub[:, :, :], lg, lmax[:, :].unsqueeze(2).broadcast_to([D, NT, E1]), ALU.subtract).then_inc(read["router"], 1)

                each_step(v, step)


def tower(nc, t):
    with ExitStack() as ctx:
        m = Mem(nc, ctx)
        keep = persistent(m)
        setup(nc, m, t, keep)
        embed_and_attend(nc, m, t, keep)
        choose_tokens(nc, m, t, keep)
        experts(nc, m, t, keep)
        layer1(nc, m, t, keep)


_INS = ["x", "L0_tok_W", "L0_tok_b", "L0_tok_token", "L0_tok_pos", "L0_ffn_Wg", "L0_ffn_W1", "L0_ffn_b1", "L0_ffn_W2",
        "L0_ffn_b2", "L1_attn_Wu", "L1_attn_bu", "L1_attn_Wv", "L1_attn_bv", "L1_attn_Wo", "L1_attn_bo", "L1_attn_Wp",
        "L1_attn_bp", "L1_attn_W1", "L1_attn_b1", "L1_attn_W2", "L1_attn_b2", "L1_attn_W3", "L1_attn_b3", "L1_attn_Wz",
        "L1_attn_bz", "L1_ffn_router", "L1_ffn_shared_gate", "L1_ffn_shared_up", "L1_ffn_shared_down", "L1_ffn_W_gate",
        "L1_ffn_W_up", "L1_ffn_W_down"]


def _constants():
    import numpy as np

    pick = np.zeros((D, NC1, D), np.float32)
    for i in range(NC1):
        for r in range(3 * E1):
            if (r % E1) // 2 == i:
                pick[r, i, (r % 2) * F1:(r % 2 + 1) * F1] = 1.0
    return {
        "decay": (np.float32(0.999) ** np.arange(SP, dtype=np.float32)).astype(np.float32).reshape(1, SP),
        "pick": pick,
        "expid": np.arange(E1, dtype=np.float32).reshape(1, E1),
    }


def kernel(**inputs):
    import numpy as _np
    import concourse.bacc as _bacc
    from concourse import mybir as _mybir
    from concourse.bass_utils import run_bass_kernel_spmd as _run

    nc = _bacc.Bacc("TRN2", target_bir_lowering=False, num_devices=1)
    arrays, t = {}, {}
    for name, a in {**{n: inputs[n] for n in _INS}, **_constants()}.items():
        a = _np.ascontiguousarray(a)
        arrays[f"in_{name}"] = a
        t[name] = nc.dram_tensor(f"in_{name}", a.shape, _mybir.dt.from_np(a.dtype), kind="ExternalInput").ap()
    for name, shape in (("apad", (2 * D, TP - 1 + SP)), ("h1", (B, SP, D)), ("xn1", (B, SP, D)), ("res2", (B, SP, D)), ("xs", (B, SP, D))):
        t[name] = nc.dram_tensor(f"scratch_{name}", shape, F32, kind="Internal").ap()
    t["out"] = nc.dram_tensor("out_0_dram", (B, S, D), F32, kind="ExternalOutput").ap()
    tower(nc, t)
    r = _run(nc, [arrays], core_ids=[0])
    return r.results[0]["out_0_dram"]
```

```python
from contextlib import ExitStack

import concourse.bass as bass
from concourse import mybir

F32 = mybir.dt.float32
BF16 = mybir.dt.bfloat16
I32 = mybir.dt.int32
U32 = mybir.dt.uint32
ALU = mybir.AluOpType
ACT = mybir.ActivationFunctionType
AX = mybir.AxisListType

B, C, IMG, NP = 64, 3, 196, 14
PX = IMG // NP
D = 128
KIN = C * PX * PX
S = NP * NP + 1
TP = 99
SP = 2 * TP
EPS = 1e-5
E0, F0 = 8, 256
KTOP = int(S * 2 / E0)
GI = 8
NG = B // GI
ROWS = GI * NP
CPY = C * PX
CH = [9, 9, 8, 8, 8]
CH0 = [sum(CH[:i]) for i in range(len(CH))]
JP = NP // 2


class Mem:

    def __init__(self, nc, stack):
        self.nc, self.stack = nc, stack

    def sb(self, name, shape, dt=F32):
        return self.stack.enter_context(self.nc.sbuf_tensor(name, shape, dt))

    def ps(self, name, shape, dt=F32):
        return self.stack.enter_context(self.nc.psum_tensor(name, shape, dt))

    def sem(self, name):
        return self.stack.enter_context(self.nc.semaphore(name))


def hold(eng, sem, value, passed):
    eng.wait_ge(sem, value)
    eng.sem_inc(passed, 1)


def persistent(m):
    return {
        "ident": m.sb("ident", [D, D]),
        "wT": m.sb("patch_wT", [CH[0] * PX, len(CH), D]),
        "posT": m.sb("posT", [D, SP]),
        "score": m.sb("score", [TP, 2, B, E0]),
        "slot_idx": m.sb("slot_idx", [SLOT2, B * NPAIR]),
        "slot_gate": m.sb("slot_gate", [SLOT2, B * NPAIR]),
        "slot_row": m.sb("slot_row", [SLOT2, B * NPAIR], I32),
    }


def setup(nc, m, t, keep):
    with ExitStack() as ctx:
        l = Mem(nc, ctx)
        wtok = l.sb("wtok_rows", [D, KIN])
        pos = l.sb("pos_rows", [TP, 2, D])
        btok = l.sb("btok", [D, 1])
        tokc = l.sb("tokc", [D, 1])
        w3 = l.sb("coef_w", [D, 3, D])
        wz = l.sb("coef_wz", [D, 2 * D])
        rows = l.sb("coef_rows", [TP, 5, D])
        bz = l.sb("coef_bz", [D, 2])
        decay = l.sb("decay", [D, SP])
        half = l.sb("one_half", [TP, 2])
        posi = l.sb("posi", [TP, 2], I32)
        posf = l.sb("posf", [TP, 2])
        hc = l.sb("hc", [TP, 2, D])
        hn = l.sb("hn", [TP, 2, D])
        sq = l.sb("hc_sq", [TP, 2, D])
        ss = l.sb("hc_ss", [TP, 2])
        hT = l.sb("hT", [D, SP])
        apad = l.sb("apad", [D, 2, TP - 1 + SP])
        ptr = l.ps("setup_tr", [D, 4, 512])
        pmm = l.ps("setup_mm", [D, 512])
        ident, wT, posT = keep["ident"], keep["wT"], keep["posT"]
        loads, loads2, idz, idd, iot = (l.sem(n) for n in ("su_loads", "su_loads2", "su_idz", "su_ident", "su_iota"))
        tr, ev, mm, dv = (l.sem(n) for n in ("su_tr", "su_evac", "su_mm", "su_dve"))
        apd, apz, rms = l.sem("su_apad_out"), l.sem("su_pz"), l.sem("su_rms")
        with nc.Block() as block:

            @block.sync
            def _(sp):
                sp.dma_start(wtok[:, :], t["L0_tok_W"]).then_inc(loads, 16)
                sp.dma_start(pos[:, 0, :], t["L0_tok_pos"][0:TP, :]).then_inc(loads, 16)
                sp.wait_ge(apz, 1)
                sp.dma_start(pos[0:S - TP, 1, :], t["L0_tok_pos"][TP:S, :]).then_inc(loads, 16)
                sp.dma_start(btok[:, :], t["L0_tok_b"].rearrange("(p a) -> p a", a=1)).then_inc(loads, 16)
                sp.dma_start(tokc[:, :], t["L0_tok_token"].rearrange("a p -> p a")).then_inc(loads, 16)
                for i in range(3):
                    sp.dma_start(w3[:, i, :], t[f"L1_attn_W{i + 1}"]).then_inc(loads2, 16)
                sp.dma_start(wz[:, :], t["L1_attn_Wz"]).then_inc(loads2, 16)
                for i in range(2):
                    sp.dma_start(bz[:, i:i + 1], t["L1_attn_bz"][i * D:(i + 1) * D].rearrange("(p a) -> p a", a=1)).then_inc(loads2, 16)
                sp.dma_start(decay[:, :], t["decay"].broadcast_to([D, SP])).then_inc(loads2, 16)
                for i, n in enumerate(("Wp", "bp", "b1", "b2", "b3")):
                    v = t["L1_attn_" + n]
                    v = v if n == "Wp" else v.rearrange("(a p) -> a p", a=1)
                    sp.dma_start(rows[:, i, :], v.broadcast_to([TP, D])).then_inc(loads2, 16)
                sp.wait_ge(dv, 23)
                sp.dma_start(t["apad"].rearrange("(a p) n -> p a n", p=D), apad[:, :, :]).then_inc(apd, 16)
                sp.wait_ge(apd, 16)

            @block.gpsimd
            def _(pool):
                nc.gpsimd.memset(pos[:, 1, :], 0.0).then_inc(apz, 1)
                nc.gpsimd.memset(half[:, :], 0.5)
                nc.gpsimd.memset(ident[:, :], 0.0).then_inc(idz, 1)
                pool.wait_ge(idz, 1)
                nc.gpsimd.affine_select(out=ident[:, :], in_=ident[:, :], compare_op=ALU.not_equal, fill=1.0,
                                        base=0, pattern=[[-1, D]], channel_multiplier=1).then_inc(idd, 1)
                nc.gpsimd.iota(posi[:, :], pattern=[[TP, 2]], base=0, channel_multiplier=1).then_inc(iot, 1)
                for k in range(4):
                    pool.wait_ge(dv, 3 + 5 * k)
                    nc.gpsimd.tensor_tensor(ss[:, :], ss[:, :], half[:, :], ALU.pow).then_inc(rms, 1)

            @block.tensor
            def _(pe):
                pe.wait_ge(idd, 1)
                pe.wait_ge(loads, 80)
                for i, n in enumerate(CH):
                    k0, k = CH0[i] * PX, n * PX
                    nc.tensor.transpose(ptr[0:k, i // 2, (i % 2) * D:(i % 2 + 1) * D], wtok[:, k0:k0 + k], ident[:, :])
                for i in range(2):
                    x = nc.tensor.transpose(ptr[:, 3, i * TP:(i + 1) * TP], pos[:, i, :], ident[0:TP, 0:TP])
                x.then_inc(tr, 1)
                for k in range(4):
                    pe.wait_ge(dv, 6 + 5 * k)
                    pe.wait_ge(ev, 6 + k)
                    for i in range(2):
                        x = nc.tensor.transpose(ptr[:, 3, i * TP:(i + 1) * TP], hn[:, i, :], ident[0:TP, 0:TP])
                    x.then_inc(tr, 1)
                    pe.wait_ge(ev, 7 + k)
                    if k == 0:
                        pe.wait_ge(loads2, 16 * 12)
                    for i in range(2):
                        if k < 3:
                            x = nc.tensor.matmul(pmm[0:TP, i * D:(i + 1) * D], hT[:, i * TP:(i + 1) * TP], w3[:, k, :], start=True, stop=True)
                        else:
                            x = nc.tensor.matmul(pmm[:, i * SP:(i + 1) * SP], wz[:, i * D:(i + 1) * D], hT[:, :], start=True, stop=True)
                    x.then_inc(mm, 1)

            @block.scalar
            def _(act):
                act.wait_ge(tr, 1)
                for i, n in enumerate(CH):
                    nc.scalar.copy(wT[0:n * PX, i, :], ptr[0:n * PX, i // 2, (i % 2) * D:(i % 2 + 1) * D]).then_inc(ev, 1)
                nc.scalar.activation(posT[:, 1:SP], ptr[:, 3, 1:SP], ACT.Identity, bias=btok[:, 0:1])
                nc.scalar.activation(posT[:, 0:1], ptr[:, 3, 0:1], ACT.Identity, bias=tokc[:, 0:1]).then_inc(ev, 1)
                for k in range(4):
                    act.wait_ge(tr, 2 + k)
                    if k:
                        act.wait_ge(mm, k)
                    nc.scalar.copy(hT[:, :], ptr[:, 3, 0:SP]).then_inc(ev, 1)

            @block.vector
            def _(v):
                n = [0]

                def link(x):
                    n[0] += 1
                    x.then_inc(dv, 1)
                    v.wait_ge(dv, n[0])

                v.wait_ge(iot, 1)
                nc.vector.memset(apad[:, :, :], 0.0)
                nc.vector.tensor_copy(posf[:, :], posi[:, :])
                v.wait_ge(loads2, 16 * 12)
                link(nc.vector.memset(sq[:, :, :], 0.0))
                for k in range(4):
                    for i in range(2):
                        if k == 0:
                            x = nc.vector.scalar_tensor_tensor(out=hc[:, i, :], in0=rows[:, 0, :], scalar=posf[:, i:i + 1], in1=rows[:, 1, :], op0=ALU.mult, op1=ALU.add)
                        else:
                            v.wait_ge(mm, k)
                            x = nc.vector.tensor_tensor(hc[:, i, :], pmm[0:TP, i * D:(i + 1) * D], rows[:, 1 + k, :], ALU.add)
                    link(x)
                    for i in range(2):
                        x = nc.vector.tensor_tensor_reduce(out=sq[:, i, :], in0=hc[:, i, :], in1=hc[:, i, :], scale=1.0 / D, scalar=0.0, op0=ALU.mult, op1=ALU.add, accum_out=ss[:, i:i + 1])
                    link(x)
                    v.wait_ge(rms, k + 1)
                    link(nc.vector.tensor_scalar(ss[:, :], ss[:, :], 1e-8, None, ALU.add))
                    link(nc.vector.reciprocal(ss[:, :], ss[:, :]))
                    if k:
                        v.wait_ge(tr, 1 + k)
                    for i in range(2):
                        x = nc.vector.tensor_scalar(hn[:, i, :], hc[:, i, :], ss[:, i:i + 1], 0.0, ALU.mult, ALU.max)
                    link(x)
                v.wait_ge(mm, 4)
                for i in range(2):
                    link(nc.vector.scalar_tensor_tensor(out=apad[:, i, TP - 1:TP - 1 + SP], in0=pmm[:, i * SP:(i + 1) * SP], scalar=bz[:, i:i + 1], in1=decay[:, :], op0=ALU.add, op1=ALU.mult))


def embed_and_attend(nc, m, t, keep):
    with ExitStack() as ctx:
        l = Mem(nc, ctx)
        px = l.sb("pixels", [ROWS, 2, C, PX * IMG])
        cut = l.sb("pixels_cut", [ROWS, 2, 2, KIN])
        xT = l.sb("pixelsT", [CH[0] * PX, 2, len(CH), 2 * ROWS])
        h0T = l.sb("tokensT", [D, GI, SP])
        h = l.sb("h", [TP, GI, 2, D])
        xn = l.sb("xn", [TP, GI, 2, D])
        xnT = l.sb("xnT", [D, GI, SP])
        sqT = l.sb("xnT_sq", [D, GI, SP])
        dist = l.sb("neg_half_dist", [TP, GI, 2, SP])
        wgt = l.sb("attn_weights", [TP, GI, 2, SP])
        h1 = l.sb("h1", [TP, GI, 2, D])
        xn1 = l.sb("xn1", [TP, GI, 2, D])
        xn1T = l.sb("xn1T", [D, GI, SP])
        wg = l.sb("router_w", [D, E0])
        nhalf = l.sb("minus_half", [D, TP])
        st = l.sb("ln_stats", [TP, 8, 4, 6])
        mv = l.sb("ln_meanvar", [TP, 8, 4, 2])
        rstd = l.sb("ln_rstd", [TP, 8, 4])
        vare = l.sb("ln_var_eps", [TP, 8, 4])
        mhalf = l.sb("pow_minus_half", [TP, 4])
        epst = l.sb("ln_eps", [TP, 4])
        tmp4 = l.sb("var_rstd", [TP, 4, 4])
        nhsq = l.sb("neg_half_sq", [TP, GI, 2])
        rsum = l.sb("row_sum", [TP, GI, 2])
        rinv = l.sb("row_inv", [TP, 4])
        lmax = l.sb("logit_max", [TP, 2, GI])
        lsub = l.sb("logit_sub", [TP, 2, GI, E0])
        lexp = l.sb("logit_exp", [TP, 2, GI, E0])
        lsum = l.sb("logit_sum", [TP, 2, GI])
        linv = l.sb("logit_inv", [TP, 2, GI])
        pT = [l.ps(f"ps_pixelsT{i}", [D, 512]) for i in range(3)]
        pO = l.ps("ps_tokens", [D, 512])
        ring = [l.ps(f"ps_ring{i}", [D, 512]) for i in range(3)]
        pL = l.ps("ps_logits", [D, 512])
        ident, wT, posT, score = keep["ident"], keep["wT"], keep["posT"], keep["score"]
        px_in, wg_in = [l.sem(f"px_in{i}") for i in range(2)], l.sem("wg_in")
        tokT, evAC, evB, tokM, evO = (l.sem(n) for n in ("tok_T", "tok_evacAC", "tok_evacB", "tok_M", "tok_added"))
        full = l.sem("ring_full")
        hrd, xnr, xtr, ds_r, ex_r = (l.sem(n) for n in ("h_ready", "xn_ready", "xnT_ready", "dist_ready", "weights_ready"))
        h1r, xn1r, xn1tr, lgr, lfree, scr = (l.sem(n) for n in ("h1_ready", "xn1_ready", "xn1T_ready", "logits_ready", "lsub_ready", "lexp_ready"))
        dv, ac, cst, stored = l.sem("p1_dve"), l.sem("p1_act"), l.sem("p1_const"), l.sem("h1_stored")
        score_done, sqr, cutr = l.sem("score_done"), l.sem("sq_ready"), l.sem("cut_ready")
        mvr, rsr, epsr, pgo = l.sem("meanvar_ready"), l.sem("rstd_ready"), l.sem("vareps_ready"), l.sem("p1_powers")
        held, sv = l.sem("p1_dve_held"), l.sem("p1_softmax")

        order = ([f"rows{k}" for k in range(4)] + [f"scores{k}" for k in range(4)] + [f"turn{k}" for k in range(4)]
                 + [f"dots{k}" for k in range(6)] + ["mix0", "dots6", "dots7", "mix1", "mix2", "mix3"])
        NU = len(order)
        reader = {"rows": (hrd, 4), "scores": (xn1tr, 4), "turn": (xtr, 4), "dots": (ds_r, 8), "mix": (h1r, 4)}

        def slot(s):
            return ring[order.index(s) % 3]

        def take(pe, g, s):
            i = order.index(s) - 3
            if isinstance(g, int):
                while i >= 0 and order[i][:-1] == {0: "scores", NG: "rows"}.get(g):
                    i -= 3
                if g == 0 and i < 0:
                    return
            stage, k = order[i][:-1], int(order[i][-1])
            sem, count = reader[stage]
            pe.wait_ge(sem, count * (g - (stage == "scores") - (i < 0)) + k + 1)

        def filled(eng, g, s):
            i = order.index(s) + 1
            if isinstance(g, int) and g == 0:
                i -= 4 if i > 4 else 0
            else:
                i = NU * g - 4 + i - (4 if isinstance(g, int) and g == NG else 0)
            eng.wait_ge(full, i)

        with nc.Block() as block:

            @block.sync
            def _(sp):
                def load(g, par):
                    for b in range(GI):
                        sp.dma_start(px[b * NP:(b + 1) * NP, par, :, :],
                                     t["x"][g * GI + b].rearrange("c (i y) w -> i c (y w)", i=NP)).then_inc(px_in[par], 16)

                sp.dma_start(wg[:, :], t["L0_ffn_Wg"]).then_inc(wg_in, 16)
                load(0, 0)
                load(1, 1)

                def store(g):
                    sp.wait_ge(h1r, 4 * g + 4)
                    sp.dma_start(t["h1"][bass.ds(g * GI, GI)].rearrange("b (t p) d -> p b t d", p=TP), h1[:, :, :, :]).then_inc(stored, 16)
                    sp.wait_ge(xn1r, 4 * g + 4)
                    sp.dma_start(t["xn1"][bass.ds(g * GI, GI)].rearrange("b (t p) d -> p b t d", p=TP), xn1[:, :, :, :]).then_inc(stored, 16)

                with sp.Fori(0, 3) as it:
                    for par in range(2):
                        g = it * 2 + par
                        sp.wait_ge(cutr, JP * g + JP)
                        load(g + 2, par)
                        store(g)
                store(6)
                store(7)
                sp.wait_ge(stored, 32 * NG + 32)

            @block.gpsimd
            def _(pool):
                nc.gpsimd.memset(nhalf[:, :], -0.5).then_inc(cst, 1)
                nc.gpsimd.memset(h0T[:, :, SP - 1:SP], 0.0).then_inc(cst, 1)
                nc.gpsimd.memset(wgt[:, :, :, SP - 1:SP], 1.0).then_inc(cst, 1)
                nc.gpsimd.memset(mhalf[:, :], -0.5).then_inc(pgo, 1)
                nc.gpsimd.memset(epst[:, :], EPS).then_inc(pgo, 1)
                pool.sem_inc(stored, 32)

                def rstds(g, k, first):
                    pool.wait_ge(mvr, 8 * g + k + (1 if first else 5))
                    if first and k == 0:
                        pool.wait_ge(pgo, 2)
                    j = k if first else 4 + k
                    nc.gpsimd.tensor_tensor(vare[:, j, :], mv[:, j, :, 1], epst[:, :], ALU.add).then_inc(epsr, 1)
                    pool.wait_ge(epsr, 8 * g + j + 1)
                    nc.gpsimd.tensor_tensor(rstd[:, j, :], vare[:, j, :], mhalf[:, :], ALU.pow).then_inc(rsr, 1)

                with pool.Fori(0, NG) as g:
                    for k in range(4):
                        rstds(g, k, True)
                    for k in range(4):
                        rstds(g, k, False)

            @block.tensor
            def _(pe):
                def T(g, jp):
                    u = JP * g + jp
                    pe.wait_ge(cutr, u + 1)
                    if not (isinstance(g, int) and u == 0):
                        pe.wait_ge(evAC, u * 2)
                        pe.wait_ge(evB, u)
                    for c, n in enumerate(CH):
                        for j in range(2):
                            o = (c % 2) * 2 * ROWS + j * ROWS
                            x = nc.tensor.transpose(pT[c // 2][0:n * PX, o:o + ROWS], cut[:, jp % 2, j, CH0[c] * PX:(CH0[c] + n) * PX], ident[0:ROWS, 0:ROWS])
                    x.then_inc(tokT, 1)

                def M(g, jp):
                    u = JP * g + jp
                    pe.wait_ge(evAC, u * 2 + 2)
                    pe.wait_ge(evB, u + 1)
                    if not (isinstance(g, int) and u == 0):
                        pe.wait_ge(evO, u)
                    for c, n in enumerate(CH):
                        x = nc.tensor.matmul(pO[:, 0:2 * ROWS], wT[0:n * PX, c, :], xT[0:n * PX, jp % 2, c, :], start=c == 0, stop=c == len(CH) - 1)
                    x.then_inc(tokM, 1)

                def tokens_rows(g, k):
                    take(pe, g, f"rows{k}")
                    if k == 0:
                        pe.wait_ge(evO, JP * g + JP)
                    for i in range(2):
                        for q in range(2):
                            o = (2 * i + q) * D
                            x = nc.tensor.transpose(slot(f"rows{k}")[0:TP, o:o + D], h0T[:, 2 * k + i, q * TP:(q + 1) * TP], ident[:, :])
                    x.then_inc(full, 1)

                def turn(src, ready, g, group, k, use):
                    take(pe, g, f"{use}{k}")
                    pe.wait_ge(ready, 4 * group + k + 1)
                    for i in range(2):
                        for q in range(2):
                            o = i * SP + q * TP
                            x = nc.tensor.transpose(slot(f"{use}{k}")[:, o:o + TP], src[:, 2 * k + i, q, :], ident[0:TP, 0:TP])
                    x.then_inc(full, 1)

                def dots(g, b):
                    take(pe, g, f"dots{b}")
                    pe.wait_ge(xtr, 4 * g + b // 2 + 1)
                    for q in range(2):
                        o = slot(f"dots{b}")[0:TP, q * SP:(q + 1) * SP]
                        nc.tensor.matmul(o, xnT[:, b, q * TP:(q + 1) * TP], xnT[:, b, :], start=True, stop=False)
                        x = nc.tensor.matmul(o, nhalf[:, :], sqT[:, b, :], start=False, stop=True)
                    x.then_inc(full, 1)

                def mix(g, k):
                    take(pe, g, f"mix{k}")
                    pe.wait_ge(ex_r, 8 * g + 2 * k + 2)
                    for i in range(2):
                        for q in range(2):
                            o = (2 * i + q) * D
                            for s, n in enumerate((TP, S - TP)):
                                x = nc.tensor.matmul(slot(f"mix{k}")[0:TP, o:o + D], wgt[0:n, 2 * k + i, s, q * TP:(q + 1) * TP], xn[0:n, 2 * k + i, s, :], start=s == 0, stop=s == 1)
                    x.then_inc(full, 1)

                def logits(g):
                    pe.wait_ge(xn1tr, 4 * g + 4)
                    pe.wait_ge(lfree, g + 1)
                    for b in range(GI):
                        for q in range(2):
                            o = (q * GI + b) * E0
                            x = nc.tensor.matmul(pL[0:TP, o:o + E0], xn1T[:, b, q * TP:(q + 1) * TP], wg[:, :], start=True, stop=True)
                    x.then_inc(lgr, 1)

                def scores(g):
                    for k in range(4):
                        turn(xn1, xn1r, g, g - 1, k, "scores")

                def body(g, more):
                    f = [lambda jp=jp: (M(g + 1, jp - 1) if jp else None, T(g + 1, jp) if jp < JP else None) for jp in range(JP + 1)]
                    if not more:
                        f = [lambda: None] * (JP + 1)
                    later = not (isinstance(g, int) and g == 0)
                    for k in range(4):
                        tokens_rows(g, k)
                    f[0]()
                    if later:
                        scores(g)
                    f[1]()
                    turn(xn, xnr, g, g, 0, "turn")
                    turn(xn, xnr, g, g, 1, "turn")
                    if later:
                        logits(g - 1)
                    turn(xn, xnr, g, g, 2, "turn")
                    turn(xn, xnr, g, g, 3, "turn")
                    f[2]()
                    for k in range(2):
                        dots(g, 2 * k)
                        dots(g, 2 * k + 1)
                        f[3 + k]()
                    dots(g, 4)
                    dots(g, 5)
                    mix(g, 0)
                    f[5]()
                    dots(g, 6)
                    dots(g, 7)
                    mix(g, 1)
                    f[6]()
                    mix(g, 2)
                    f[7]()
                    mix(g, 3)

                pe.wait_ge(cst, 4)
                pe.wait_ge(wg_in, 16)
                for jp in range(JP):
                    T(0, jp)
                    M(0, jp)
                body(0, True)
                with pe.Fori(0, 3) as it:
                    body(it * 2 + 1, True)
                    body(it * 2 + 2, True)
                body(NG - 1, False)
                scores(NG)
                logits(NG - 1)

            @block.scalar
            def _(act):
                def pixels(g, jp):
                    u = JP * g + jp
                    act.wait_ge(tokT, u + 1)
                    if not (isinstance(g, int) and u < 2):
                        act.wait_ge(tokM, u - 1 if jp else u)
                    k = CH[0] * PX
                    nc.scalar.copy(xT[0:k, jp % 2, 0:2, :], pT[0][0:k, 0:4 * ROWS].rearrange("p (c n) -> p c n", c=2)).then_inc(evAC, 1)
                    k = CH[4] * PX
                    nc.scalar.copy(xT[0:k, jp % 2, 4, :], pT[2][0:k, 0:2 * ROWS]).then_inc(evAC, 1)

                def cut_pair(g, jp, par, half):
                    u = JP * g + jp
                    if jp == 0:
                        act.wait_ge(px_in[par], 128 * half + 128)
                    if not (isinstance(g, int) and g == 0 and jp < 2):
                        act.wait_ge(tokT, u - 1 if jp else u)
                    rows = px[:, par, :, :].rearrange("p c (y j x) -> p j (c y) x", y=PX, j=NP)
                    nc.scalar.copy(cut[:, jp % 2, :, :].rearrange("p j (r x) -> p j r x", x=PX), rows[:, 2 * jp:2 * jp + 2]).then_inc(cutr, 1)

                def take_rows(g, k):
                    filled(act, g, f"rows{k}")
                    if not (isinstance(g, int) and g == 0):
                        act.wait_ge(h1r, 4 * g - 3 + k)
                    nc.scalar.copy(h[:, 2 * k:2 * k + 2, :, :].rearrange("p i q d -> p (i q d)"), slot(f"rows{k}")[0:TP, :]).then_inc(hrd, 1)

                def turned(g, k):
                    filled(act, g, f"turn{k}")
                    o = xnT[:, 2 * k:2 * k + 2, :].rearrange("p i n -> p (i n)")
                    nc.scalar.copy(o, slot(f"turn{k}")[:, 0:2 * SP])
                    nc.scalar.activation(sqT[:, 2 * k:2 * k + 2, :].rearrange("p i n -> p (i n)"), slot(f"turn{k}")[:, 0:2 * SP], ACT.Square).then_inc(xtr, 1)

                def weights(g, b):
                    act.wait_ge(ds_r, 8 * g + b + 1)
                    nc.scalar.activation(dist[:, b, :, :], dist[:, b, :, :], ACT.Exp, scale=2.0).then_inc(ac, 1)
                    act.wait_ge(ac, 8 * g + b + 1)
                    for q in range(2):
                        x = nc.scalar.activation(wgt[:, b, q, 0:S], dist[:, b, q, 0:S], ACT.Exp, accum_out=rsum[:, b, q:q + 1])
                    x.then_inc(ex_r, 1)

                def turned1(g, k):
                    filled(act, g, f"scores{k}")
                    nc.scalar.copy(xn1T[:, 2 * k:2 * k + 2, :].rearrange("p i n -> p (i n)"), slot(f"scores{k}")[:, 0:2 * SP]).then_inc(xn1tr, 1)

                def softmax(g):
                    act.wait_ge(lfree, g + 2)
                    nc.scalar.activation(lexp[:, :, :, :], lsub[:, :, :, :], ACT.Exp).then_inc(scr, 1)

                def body(g, par, half, more):
                    f = [lambda jp=jp: (cut_pair(g + 1, jp + 1, 1 - par, half + par) if jp + 1 < JP else None, pixels(g + 1, jp)) for jp in range(JP)]
                    later = not (isinstance(g, int) and g == 0)
                    if more:
                        cut_pair(g + 1, 0, 1 - par, half + par)
                    else:
                        f = [lambda: None] * JP
                    for k in range(4):
                        take_rows(g, k)
                    f[0]()
                    if later:
                        for k in range(4):
                            turned1(g, k)
                    f[1]()
                    for k in range(4):
                        turned(g, k)
                    f[2]()
                    for k in range(4):
                        weights(g, 2 * k)
                        weights(g, 2 * k + 1)
                        if k == 1 and later:
                            softmax(g - 1)
                        f[3 + k]()

                cut_pair(0, 0, 0, 0)
                for jp in range(JP):
                    if jp + 1 < JP:
                        cut_pair(0, jp + 1, 0, 0)
                    pixels(0, jp)
                body(0, 0, 0, True)
                with act.Fori(0, 3) as it:
                    body(it * 2 + 1, 1, it, True)
                    body(it * 2 + 2, 0, it + 1, True)
                body(NG - 1, 1, 3, False)
                for k in range(4):
                    turned1(NG, k)
                softmax(NG - 1)

            @block.vector
            def _(v):
                def pixels(g, jp):
                    u = JP * g + jp
                    v.wait_ge(tokT, u + 1)
                    if not (isinstance(g, int) and u < 2):
                        v.wait_ge(tokM, u - 1 if jp else u)
                    k = CH[2] * PX
                    nc.vector.tensor_copy(xT[0:CH[2] * PX, jp % 2, 2:4, :], pT[1][0:k, 0:4 * ROWS].rearrange("p (c n) -> p c n", c=2)).then_inc(evB, 1)

                def add_pos(g, jp):
                    u = JP * g + jp
                    v.wait_ge(tokM, u + 1)
                    if jp == 0:
                        if isinstance(g, int) and g == 0:
                            v.wait_ge(cst, 3)
                        else:
                            filled(v, g - 1, "rows3")
                    o = h0T[:, :, 1:S].rearrange("p b (i j) -> p j b i", j=NP)[:, 2 * jp:2 * jp + 2]
                    a = pO[:, 0:2 * ROWS].rearrange("p (j b i) -> p j b i", j=2, b=GI)
                    b = posT[:, 1:S].rearrange("p (i j) -> p j i", j=NP)[:, 2 * jp:2 * jp + 2].unsqueeze(2).broadcast_to([D, 2, GI, NP])
                    for j in range(2):
                        x = nc.vector.tensor_tensor(o[:, j], a[:, j], b[:, j], ALU.add)
                    x.then_inc(evO, 1)

                def link(x, base, i):
                    x.then_inc(dv, 1)
                    v.wait_ge(dv, base + i)

                NL = 2 * 4 + 4 + 4

                def body(g, more):
                    i = [0]

                    def c(x):
                        i[0] += 1
                        link(x, NL * g, i[0])

                    def stats(src, k, j):
                        for q in range(4):
                            x = nc.vector.bn_stats(st[:, j, q, :], src[:, 2 * k + q // 2, q % 2, :])
                        i[0] += 1
                        x.then_inc(dv, 1)
                        hold(v, dv, NL * g + i[0], held)
                        for q in range(4):
                            x = nc.vector.bn_aggr(mv[:, j, q, :], st[:, j, q, :])
                        x.then_inc(mvr, 1)

                    def apply(src, out, k, j, ready, g=g):
                        v.wait_ge(rsr, 8 * g + j + 1)
                        for q in range(4):
                            x = nc.vector.tensor_scalar(out[:, 2 * k + q // 2, q % 2, :], src[:, 2 * k + q // 2, q % 2, :], mv[:, j, q, 0:1], rstd[:, j, q:q + 1], ALU.subtract, ALU.mult)
                        x.then_inc(ready, 1)

                    def first(k):
                        v.wait_ge(hrd, 4 * g + k + 1)
                        stats(h, k, k)

                    def second(k):
                        apply(h, xn, k, k, xnr)
                        c(nc.vector.tensor_tensor(tmp4[:, k, :], mv[:, k, :, 1], rstd[:, k, :], ALU.mult))
                        nc.vector.scalar_tensor_tensor(out=nhsq[:, 2 * k:2 * k + 2, :].rearrange("p i q -> p (i q)"), in0=tmp4[:, k, :], scalar=-D / 2, in1=rstd[:, k, :], op0=ALU.mult, op1=ALU.mult).then_inc(sqr, 1)

                    def distance(b):
                        filled(v, g, f"dots{b}")
                        if b % 2 == 0:
                            v.wait_ge(sqr, 4 * g + b // 2 + 1)
                        for q in range(2):
                            x = nc.vector.tensor_scalar(dist[:, b, q, :], slot(f"dots{b}")[0:TP, q * SP:(q + 1) * SP], nhsq[:, b, q:q + 1], 0.0, ALU.add, ALU.min)
                        x.then_inc(ds_r, 1)

                    def residual(k):
                        filled(v, g, f"mix{k}")
                        if k == 0:
                            v.wait_ge(stored, 32 * g + 32)
                        c(nc.vector.reciprocal(rinv[:, :], rsum[:, 2 * k:2 * k + 2, :].rearrange("p i q -> p (i q)")))
                        for q in range(4):
                            x = nc.vector.scalar_tensor_tensor(out=h1[:, 2 * k + q // 2, q % 2, :], in0=slot(f"mix{k}")[0:TP, q * D:(q + 1) * D], scalar=rinv[:, q:q + 1], in1=h[:, 2 * k + q // 2, q % 2, :], op0=ALU.mult, op1=ALU.add)
                        x.then_inc(h1r, 1)
                        v.wait_ge(h1r, 4 * g + k + 1)
                        stats(h1, k, 4 + k)

                    f = [lambda jp=jp: (add_pos(g + 1, jp - 1) if jp else None, pixels(g + 1, jp) if jp < JP else None) for jp in range(JP + 1)]
                    if not more:
                        f = [lambda: None] * (JP + 1)
                    later = not (isinstance(g, int) and g == 0)
                    if later:
                        apply(h1, xn1, 2, 6, xn1r, g - 1)
                    first(0)
                    if later:
                        apply(h1, xn1, 3, 7, xn1r, g - 1)
                    f[0]()
                    first(1)
                    first(2)
                    second(0)
                    first(3)
                    second(1)
                    f[1]()
                    second(2)
                    second(3)
                    f[2]()
                    distance(0)
                    distance(1)
                    if later:
                        centre(g - 1)
                    f[3]()
                    distance(2)
                    distance(3)
                    if later:
                        scores(g - 1)
                    f[4]()
                    distance(4)
                    distance(5)
                    residual(0)
                    f[5]()
                    distance(6)
                    distance(7)
                    apply(h1, xn1, 0, 4, xn1r)
                    residual(1)
                    f[6]()
                    residual(2)
                    apply(h1, xn1, 1, 5, xn1r)
                    f[7]()
                    residual(3)
                    assert i[0] == NL, i[0]
                    return apply

                def centre(g):
                    v.wait_ge(lgr, g + 1)
                    lg = pL[0:TP, 0:2 * GI * E0].rearrange("p (q b e) -> p q b e", q=2, b=GI)
                    nc.vector.tensor_reduce(lmax[:, :, :], lg, AX.X, ALU.max).then_inc(sv, 1)
                    v.wait_ge(sv, 3 * g + 1)
                    nc.vector.tensor_tensor(lsub[:, :, :, :], lg, lmax[:, :, :].unsqueeze(3).broadcast_to([TP, 2, GI, E0]), ALU.subtract).then_inc(lfree, 1)

                def scores(g):
                    v.wait_ge(scr, g + 1)
                    nc.vector.tensor_reduce(lsum[:, :, :], lexp[:, :, :, :], AX.X, ALU.add).then_inc(sv, 1)
                    v.wait_ge(sv, 3 * g + 2)
                    nc.vector.reciprocal(linv[:, :, :], lsum[:, :, :]).then_inc(sv, 1)
                    v.wait_ge(sv, 3 * g + 3)
                    nc.vector.tensor_tensor(score[:, :, bass.ds(g * GI, GI), :], lexp[:, :, :, :], linv[:, :, :].unsqueeze(3).broadcast_to([TP, 2, GI, E0]), ALU.mult).then_inc(score_done, 1)

                v.sem_inc(lfree, 1)
                nc.vector.tensor_copy(h0T[:, :, 0:1], posT[:, 0:1].unsqueeze(1).broadcast_to([D, GI, 1])).then_inc(cst, 1)
                for jp in range(JP):
                    pixels(0, jp)
                    add_pos(0, jp)
                body(0, True)
                with v.Fori(0, 3) as it:
                    body(it * 2 + 1, True)
                    body(it * 2 + 2, True)
                apply = body(NG - 1, False)
                apply(h1, xn1, 2, 6, xn1r)
                apply(h1, xn1, 3, 7, xn1r)
                centre(NG - 1)
                scores(NG - 1)
                v.wait_ge(score_done, NG)


HB = 16
NPAIR = E0 // 2
SLOT2 = 2 * KTOP
ROUNDS = -(-KTOP // 8)


def choose_tokens(nc, m, t, keep):
    with ExitStack() as ctx:
        l = Mem(nc, ctx)
        ng = B // HB
        work = l.sb("topk_work", [D, ng, S])
        val = l.sb("topk_val", [D, ng, ROUNDS * 8])
        idx = l.sb("topk_idx", [D, ng, ROUNDS * 8], U32)
        spread = l.sb("topk_spread", [D, 2, ng, SLOT2])
        odd = l.sb("odd_even", [D, 2])
        pick = l.sb("pick_pair", [D, D // 2])
        basei = l.sb("row_base_i", [SLOT2, B * NPAIR], I32)
        base = l.sb("row_base", [SLOT2, B * NPAIR])
        pt = [l.ps(f"ps_score{i}", [D, 512]) for i in range(ng)]
        pi = l.ps("ps_slots", [D, 512])
        ident, score = keep["ident"], keep["score"]
        tr, dv, iot, mm = (l.sem(n) for n in ("tk_tr", "tk_dve", "tk_iota", "tk_mm"))
        with nc.Block() as block:

            @block.gpsimd
            def _(pool):
                nc.gpsimd.iota(basei[:, :], pattern=[[SP, B], [0, NPAIR]], base=0, channel_multiplier=0).then_inc(iot, 1)

            @block.tensor
            def _(pe):
                for g in range(ng):
                    for q, n in enumerate((TP, S - TP)):
                        x = nc.tensor.transpose(pt[g][:, q * TP:q * TP + n], score[0:n, q, g * HB:(g + 1) * HB, :].rearrange("p b e -> p (b e)"), ident[0:n, 0:n])
                    x.then_inc(tr, 1)
                pe.wait_ge(dv, LAST)
                for j in range(2):
                    for g in range(ng):
                        o = j * B * NPAIR + g * HB * NPAIR
                        x = nc.tensor.matmul(pi[0:SLOT2, o:o + HB * NPAIR], spread[:, j, g, :], pick[:, :], start=True, stop=True)
                x.then_inc(mm, 1)

            @block.vector
            def _(v):
                n = [0]

                def link(x):
                    n[0] += 1
                    x.then_inc(dv, 1)
                    v.wait_ge(dv, n[0])

                v.wait_ge(iot, 1)
                nc.vector.tensor_copy(base[:, :], basei[:, :])
                for j in range(2):
                    nc.vector.tensor_reduce(odd[:, j:j + 1], ident[:, :].rearrange("p (a b) -> p b a", b=2)[:, j], AX.X, ALU.add)
                nc.vector.tensor_tensor(pick[:, :], ident[:, :].rearrange("p (a b) -> p b a", b=2)[:, 0], ident[:, :].rearrange("p (a b) -> p b a", b=2)[:, 1], ALU.add)
                for g in range(ng):
                    v.wait_ge(tr, g + 1)
                    x = nc.vector.tensor_copy(work[:, g, :], pt[g][:, 0:S])
                link(x)
                for r in range(ROUNDS):
                    w = slice(8 * r, 8 * r + 8)
                    for g in range(ng):
                        x = nc.vector.max(val[:, g, w], work[:, g, :])
                    link(x)
                    for g in range(ng):
                        x = nc.vector.max_index(idx[:, g, w], val[:, g, w], work[:, g, :])
                    if r < ROUNDS - 1:
                        link(x)
                        for g in range(ng):
                            x = nc.vector.match_replace(work[:, g, :], val[:, g, w], work[:, g, :], -1.0)
                    link(x)
                for j, src in enumerate((idx, val)):
                    for h in range(2):
                        x = nc.vector.tensor_scalar(spread[:, j, :, h * KTOP:(h + 1) * KTOP], src[:, :, 0:KTOP], odd[:, h:h + 1], None, ALU.mult)
                link(x)
                assert n[0] == LAST, n[0]
                v.wait_ge(mm, 1)
                nc.vector.tensor_copy(keep["slot_idx"][:, :], pi[0:SLOT2, 0:B * NPAIR])
                nc.vector.tensor_copy(keep["slot_gate"][:, :], pi[0:SLOT2, B * NPAIR:2 * B * NPAIR])
                link(nc.vector.tensor_tensor(keep["slot_row"][:, :], pi[0:SLOT2, 0:B * NPAIR], base[:, :], ALU.add))


LAST = 1 + 3 * ROUNDS - 1 + 1


def experts(nc, m, t, keep):
    with ExitStack() as ctx:
        l = Mem(nc, ctx)
        w1 = l.sb("e_w1", [D, E0, F0])
        w2 = l.sb("e_w2", [D, E0, 2, D])
        brow = l.sb("e_bias_rows", [E0, 3, D])
        bcol = l.sb("e_bias_cols", [D, 3, E0])
        stage = l.sb("gather_rows", [SLOT2, GI * NPAIR], I32)
        got = l.sb("gathered", [SLOT2, GI, NPAIR, D])
        ex = l.sb("expert_in", [D, E0, GI, KTOP])
        hm = l.sb("expert_hidden", [D, 2, 2, GI * KTOP])
        eo = l.sb("expert_out", [D, GI, E0, KTOP])
        vr_ = l.sb("expert_rows", [SLOT2, 2, NPAIR, D])
        hot = l.sb("gated_onehot", [SLOT2, 2, NPAIR, SP])
        toki = l.sb("token_iota_i", [SLOT2, SP], I32)
        tok = l.sb("token_iota", [SLOT2, SP])
        h1 = l.sb("h1_rows", [TP, GI, 2, D])
        h2 = l.sb("h2_rows", [TP, GI, 2, D])
        xn = l.sb("xn2_rows", [TP, GI, 2, D])
        xs = l.sb("xs_rows", [TP, GI, 2, D])
        st = l.sb("e_ln_stats", [TP, 4, 4, 6])
        mv = l.sb("e_meanvar", [TP, 4, 4, 2])
        base = l.sb("e_pow_base", [TP, 4, 2, 4])
        root = l.sb("e_pow_root", [TP, 4, 2, 4])
        rms = l.sb("e_rms", [TP, 2, 4, 4])
        inv = l.sb("e_inv_rms", [TP, 4, 4])
        pw = l.sb("e_powers", [TP, 2, 4])
        ring = [l.ps(f"ps_e_ring{i}", [D, 512]) for i in range(4)]
        hid = [l.ps(f"ps_e_hidden{i}", [D, 512]) for i in range(4)]
        ident = keep["ident"]
        w_in, cst, bt, bc = (l.sem(n) for n in ("e_w_in", "e_const", "e_bias_tr", "e_bias_ready"))
        gat = [l.sem(f"gathered{i}") for i in range(GI)]
        stg, full, exr, w1d, hmr, eor, rwr, hotr, h2r = (l.sem(n) for n in ("stage_ready", "e_ring_full", "ex_ready", "w1_done", "hidden_ready", "eout_ready", "erows_ready", "hot_ready", "h2_ready"))
        dv, mvr, pp, scr, xsr, rr, h1in, outd = (l.sem(n) for n in ("e_dve", "e_meanvar_ready", "e_pow", "e_root_ready", "xs_ready", "r_ready", "h1_in", "e_stored"))
        prer, invr, nv = (l.sem(n) for n in ("e_base_ready", "e_inv_ready", "e_norm"))
        xnd, tokr, held, pheld = (l.sem(n) for n in ("xn2_ready", "token_iota_ready", "e_dve_held", "e_pool_held"))
        order = [f"out{e}" for e in range(E0)] + ["rows0"]
        for b in range(GI):
            order += ([f"rows{b + 1}"] if b + 1 < GI else []) + [f"spread{b}", f"fetch{b}"]
        NU = len(order)
        reader = {"out": eor, "rows": rwr, "spread": h2r, "fetch": exr}

        def slot(s):
            return ring[order.index(s) % 4]

        def take(pe, g, s):
            i = order.index(s) - 4
            fixed = isinstance(g, int)
            while i >= 0 and fixed and (order[i][:-1] != "fetch" if g < 0 else g == NG - 1 and order[i][:-1] == "fetch"):
                i -= 4
            if fixed and g < 0 and i < 0:
                return
            stage, k = order[i % NU][:-1], int(order[i % NU][-1])
            pe.wait_ge(reader[stage], GI * (g - (i < 0) + 1) + k + 1)

        def filled(eng, g, s):
            i = order.index(s) + 1
            if isinstance(g, int) and g < 0:
                eng.wait_ge(full, int(s[-1]) + 1)
            else:
                if isinstance(g, int) and g == NG - 1:
                    i -= sum(x[:-1] == "fetch" for x in order[:i])
                eng.wait_ge(full, GI + NU * g + i)

        with nc.Block() as block:

            @block.sync
            def _(sp):
                for i in range(2):
                    sp.dma_start(brow[:, i, :], t["L0_ffn_b1"][:, i * D:(i + 1) * D]).then_inc(w_in, 16)
                sp.dma_start(brow[:, 2, :], t["L0_ffn_b2"]).then_inc(w_in, 16)
                sp.dma_start(w1[:, :, :], t["L0_ffn_W1"].rearrange("e h f -> h e f")).then_inc(w_in, 16)
                sp.dma_start(w2[:, :, :, :], t["L0_ffn_W2"].rearrange("e (c p) h -> p e c h", p=D)).then_inc(w_in, 16)

                with sp.Fori(0, NG) as g:
                    sp.wait_ge(h2r, 8 * g + GI)
                    sp.dma_start(h1[:, :, :, :], t["h1"][bass.ds(g * GI, GI)].rearrange("b (t p) d -> p b t d", p=TP)).then_inc(h1in, 16)
                    sp.wait_ge(rr, 4 * g + 4)
                    sp.dma_start(t["res2"][bass.ds(g * GI, GI)].rearrange("b (t p) d -> p b t d", p=TP), h2[:, :, :, :]).then_inc(outd, 16)
                    sp.wait_ge(xsr, 4 * g + 4)
                    sp.dma_start(t["xs"][bass.ds(g * GI, GI)].rearrange("b (t p) d -> p b t d", p=TP), xs[:, :, :, :]).then_inc(outd, 16)
                sp.wait_ge(outd, 32 * NG + 32)

            @block.gpsimd
            def _(pool):
                def indices(g, half):
                    n = GI * NPAIR // 2
                    c = slice(half * n, (half + 1) * n)
                    if not isinstance(g, int):
                        for b in range(half * GI // 2, (half + 1) * GI // 2):
                            pool.wait_ge(gat[b], 64 * g)
                        hold(pool, gat[half * GI // 2], 64 * g, pheld)
                    nc.gpsimd.tensor_copy(stage[:, c], keep["slot_row"][:, bass.ds(g * GI * NPAIR + half * n, n)]).then_inc(stg, 1)
                    hold(pool, stg, 2 * g + half + 1, pheld)

                def gather(g, b):
                    if not isinstance(g, int):
                        hold(pool, exr, GI * (g - 1) + b + 1, pheld)
                    for j in range(NPAIR):
                        nc.gpsimd.indirect_dma_start(got[:, b, j, :], None, t["xn1"].rearrange("b s d -> (b s) d"),
                                                     bass.IndirectOffsetOnAxis(ap=stage[:, b * NPAIR + j:b * NPAIR + j + 1], axis=0)).then_inc(gat[b], 16)

                def roots(g, k):
                    pool.wait_ge(prer, 4 * g + k + 1)
                    nc.gpsimd.tensor_tensor(root[:, k, :, :], base[:, k, :, :], pw[:, :, :], ALU.pow).then_inc(scr, 1)

                nc.gpsimd.iota(toki[:, :], pattern=[[1, SP]], base=0, channel_multiplier=0).then_inc(cst, 1)
                for i, p in enumerate((-0.5, 0.5)):
                    nc.gpsimd.memset(pw[:, i, :], p).then_inc(cst, 1)
                pool.wait_ge(cst, 3)
                pool.sem_inc(outd, 32)
                for half in range(2):
                    indices(0, half)
                    for b in range(half * 4, half * 4 + 4):
                        gather(0, b)
                with pool.Fori(0, NG - 1) as g:
                    indices(g + 1, 0)
                    for b in range(4):
                        gather(g + 1, b)
                    indices(g + 1, 1)
                    gather(g + 1, 4)
                    gather(g + 1, 5)
                    roots(g, 0)
                    gather(g + 1, 6)
                    roots(g, 1)
                    gather(g + 1, 7)
                    roots(g, 2)
                    roots(g, 3)
                for k in range(4):
                    roots(NG - 1, k)

            @block.tensor
            def _(pe):
                def hidden(g, e):
                    if e == 0:
                        pe.wait_ge(exr, GI * g + GI)
                    pe.wait_ge(hmr, GI * g + e + 1)
                    for c in range(2):
                        x = nc.tensor.matmul(hid[2 * (e % 2) + c][:, 0:GI * KTOP], w1[:, e, c * D:(c + 1) * D], ex[:, e, :, :].rearrange("p b k -> p (b k)"), start=True, stop=True)
                    x.then_inc(w1d, 1)

                def output(g, e):
                    take(pe, g, f"out{e}")
                    pe.wait_ge(hmr, GI * g + e + 3)
                    for c in range(2):
                        x = nc.tensor.matmul(slot(f"out{e}")[:, 0:GI * KTOP], w2[:, e, c, :], hm[:, e % 2, c, :], start=c == 0, stop=c == 1)
                    x.then_inc(full, 1)

                def to_rows(g, b):
                    take(pe, g, f"rows{b}")
                    if b == 0:
                        pe.wait_ge(eor, GI * g + 2 * GI)
                    for j in range(NPAIR):
                        x = nc.tensor.transpose(slot(f"rows{b}")[0:SLOT2, j * D:(j + 1) * D], eo[:, b, 2 * j:2 * j + 2, :].rearrange("p e k -> p (e k)"), ident[:, :])
                    x.then_inc(full, 1)

                def spread(g, b):
                    take(pe, g, f"spread{b}")
                    pe.wait_ge(rwr, GI * g + b + 1 + GI)
                    pe.wait_ge(hotr, GI * g + b + 1)
                    for q in range(2):
                        for j in range(NPAIR):
                            x = nc.tensor.matmul(slot(f"spread{b}")[0:TP, q * D:(q + 1) * D], hot[:, b % 2, j, q * TP:(q + 1) * TP], vr_[:, b % 2, j, :], start=j == 0, stop=j == NPAIR - 1)
                    x.then_inc(full, 1)

                pe.wait_ge(w_in, 80)
                for i in range(3):
                    x = nc.tensor.transpose(hid[0][:, i * E0:(i + 1) * E0], brow[:, i, :], ident[0:E0, 0:E0])
                x.then_inc(bt, 1)
                pe.wait_ge(bc, 1)

                def fetch(g, b):
                    take(pe, g, f"fetch{b}")
                    pe.wait_ge(gat[b], 64 * (g + 1) + 64)
                    for j in range(NPAIR):
                        x = nc.tensor.transpose(slot(f"fetch{b}")[:, j * SLOT2:(j + 1) * SLOT2], got[:, b, j, :], ident[0:SLOT2, 0:SLOT2])
                    x.then_inc(full, 1)

                def body(g, more):
                    hidden(g, 0)
                    for e in range(E0):
                        if e + 1 < E0:
                            hidden(g, e + 1)
                        output(g, e)
                    to_rows(g, 0)
                    for b in range(GI):
                        if b + 1 < GI:
                            to_rows(g, b + 1)
                        spread(g, b)
                        if more:
                            fetch(g, b)

                for b in range(GI):
                    fetch(-1, b)
                with pe.Fori(0, NG - 1) as g:
                    body(g, True)
                body(NG - 1, False)

            @block.scalar
            def _(act):
                act.wait_ge(bt, 1)
                nc.scalar.copy(bcol[:, :, :].rearrange("p i e -> p (i e)"), hid[0][:, 0:3 * E0]).then_inc(bc, 1)
                act.wait_ge(bc, 1)
                act.sem_inc(hmr, 2)
                act.sem_inc(rwr, GI)

                def rescale(g, k):
                    act.wait_ge(invr, 4 * g + k + 1)
                    act.wait_ge(rr, 4 * g + k + 1)
                    if k == 0:
                        act.wait_ge(outd, 32 * g + 32)
                    for q in range(4):
                        x = nc.scalar.activation(xs[:, 2 * k + q // 2, q % 2, :], xn[:, 2 * k + q // 2, q % 2, :], ACT.Copy, scale=inv[:, k, q:q + 1])
                    x.then_inc(xsr, 1)

                def body(g):
                    for e in range(E0):
                        act.wait_ge(w1d, GI * g + e + 1)
                        if e >= 2:
                            filled(act, g, f"out{e - 2}")
                        for c in range(2):
                            x = nc.scalar.activation(hm[:, e % 2, c, :], hid[2 * (e % 2) + c][:, 0:GI * KTOP], ACT.Gelu, bias=bcol[:, c, e:e + 1])
                        x.then_inc(hmr, 1)
                        if not (isinstance(g, int) and g == 0) and e in (2, 4):
                            rescale(g - 1, 1 + e // 2)
                    for b in range(GI):
                        filled(act, g, f"rows{b}")
                        nc.scalar.copy(vr_[:, b % 2, :, :].rearrange("p j d -> p (j d)"), slot(f"rows{b}")[0:SLOT2, :]).then_inc(rwr, 1)
                        if b >= 6:
                            rescale(g, b - 6)

                body(0)
                with act.Fori(1, NG - 1) as g:
                    body(g)
                body(NG - 1)
                rescale(NG - 1, 2)
                rescale(NG - 1, 3)

            @block.vector
            def _(v):
                v.wait_ge(cst, 3)
                nc.vector.tensor_copy(tok[:, :], toki[:, :]).then_inc(tokr, 1)
                v.wait_ge(tokr, 1)
                v.sem_inc(h2r, GI)
                v.sem_inc(eor, GI)

                def onehots(g, b):
                    for j in range(NPAIR):
                        col = g * (GI * NPAIR) + b * NPAIR + j
                        x = nc.vector.tensor_scalar(hot[:, b % 2, j, :], tok[:, :], keep["slot_idx"][:, bass.ds(col, 1)], keep["slot_gate"][:, bass.ds(col, 1)], ALU.is_equal, ALU.mult)
                    x.then_inc(hotr, 1)

                def stats(g, k):
                    v.wait_ge(h2r, GI * g + 2 * k + 2 + GI)
                    for q in range(4):
                        x = nc.vector.bn_stats(st[:, k, q, :], h2[:, 2 * k + q // 2, q % 2, :])
                    x.then_inc(dv, 1)
                    hold(v, dv, 2 * (4 * g + k) + 1, held)
                    for q in range(4):
                        x = nc.vector.bn_aggr(mv[:, k, q, :], st[:, k, q, :])
                    x.then_inc(dv, 1)
                    v.wait_ge(dv, 2 * (4 * g + k) + 2)
                    nc.vector.tensor_scalar(base[:, k, 0, :], mv[:, k, :, 1], EPS, None, ALU.add)
                    nc.vector.tensor_copy(base[:, k, 1, :], mv[:, k, :, 1]).then_inc(prer, 1)

                def normalise(g, k):
                    v.wait_ge(scr, 4 * g + k + 1)
                    for q in range(4):
                        x = nc.vector.tensor_scalar(xn[:, 2 * k + q // 2, q % 2, :], h2[:, 2 * k + q // 2, q % 2, :], mv[:, k, q, 0:1], root[:, k, 0, q:q + 1], ALU.subtract, ALU.mult)
                    x.then_inc(xnd, 1)
                    nc.vector.tensor_tensor(rms[:, 0, k, :], root[:, k, 0, :], root[:, k, 1, :], ALU.mult).then_inc(nv, 1)
                    v.wait_ge(nv, 2 * (4 * g + k) + 1)
                    nc.vector.tensor_scalar(rms[:, 1, k, :], rms[:, 0, k, :], 1e-8, None, ALU.add).then_inc(nv, 1)
                    v.wait_ge(nv, 2 * (4 * g + k) + 2)
                    nc.vector.reciprocal(inv[:, k, :], rms[:, 1, k, :]).then_inc(invr, 1)
                    v.wait_ge(xnd, 4 * g + k + 1)
                    a = h2[:, 2 * k:2 * k + 2, :, :].rearrange("p i q d -> p (i q d)")
                    nc.vector.tensor_tensor(a, a, xn[:, 2 * k:2 * k + 2, :, :].rearrange("p i q d -> p (i q d)"), ALU.add).then_inc(rr, 1)

                def fetched(g, b):
                    filled(v, g, f"fetch{b}")
                    nc.vector.tensor_copy(ex[:, :, b, :], slot(f"fetch{b}")[:, 0:E0 * KTOP].rearrange("p (e k) -> p e k", k=KTOP)).then_inc(exr, 1)

                def body(g, more):
                    onehots(g, 0)
                    onehots(g, 1)
                    for e in range(E0):
                        filled(v, g, f"out{e}")
                        nc.vector.tensor_scalar(eo[:, :, e, :], slot(f"out{e}")[:, 0:GI * KTOP].rearrange("p (b k) -> p b k", k=KTOP), bcol[:, 2, e:e + 1], None, ALU.add).then_inc(eor, 1)
                    v.wait_ge(h1in, 16 * g + 16)
                    v.wait_ge(outd, 32 * g + 32)
                    for b in range(GI):
                        filled(v, g, f"spread{b}")
                        nc.vector.tensor_tensor(h2[:, b, :, :].rearrange("p q d -> p (q d)"), slot(f"spread{b}")[0:TP, 0:2 * D], h1[:, b, :, :].rearrange("p q d -> p (q d)"), ALU.add).then_inc(h2r, 1)
                        if b + 2 < GI:
                            onehots(g, b + 2)
                        if more:
                            fetched(g, b)
                        if b % 2 == 1:
                            stats(g, b // 2)
                        if b in (4, 6, 7):
                            normalise(g, {4: 0, 6: 1, 7: 2}[b])
                    normalise(g, 3)

                v.wait_ge(bc, 1)
                for b in range(GI):
                    fetched(-1, b)
                with v.Fori(0, NG - 1) as g:
                    body(g, True)
                body(NG - 1, False)


E1, F1 = 8, 64
NC1 = E1 * F1 // D
CPU = 4
TU = 6
NU1 = SP // TU
NT = TU // 2
COL = TU * B


def load_layer1(sp, t, w, pick, sem):
    one = lambda v: v.rearrange("(p a) -> p a", a=1)
    row = lambda v, n: v.rearrange("(a p) -> a p", a=1).broadcast_to(n)
    pairs = [
        (w["wv"][:, :], t["L1_attn_Wv"]), (w["bv"][:, :], row(t["L1_attn_bv"], [TP, 2 * D])),
        (w["wu"][:, :], t["L1_attn_Wu"]), (w["bo"][:, :], row(t["L1_attn_bo"], [D, D])),
        (w["bu"][:, 0:1], one(t["L1_attn_bu"][0:D])), (w["bu"][:, 1:2], one(t["L1_attn_bu"][D:2 * D])),
        (w["wo"][:, :, :], t["L1_attn_Wo"].rearrange("(a p) d -> p a d", p=D)),
        (w["router"][:, :], t["L1_ffn_router"]),
        (w["gate"][:, :, :], t["L1_ffn_W_gate"].rearrange("e d h -> d e h")),
        (w["up"][:, :, :], t["L1_ffn_W_up"].rearrange("e d h -> d e h")),
        (w["sgate"][:, :], t["L1_ffn_shared_gate"]), (w["sup"][:, :], t["L1_ffn_shared_up"]),
        (w["down"][:, :, :], t["L1_ffn_W_down"].rearrange("(i a) h d -> (a h) i d", a=2)),
        (w["sdown"][:, :], t["L1_ffn_shared_down"]),
        (pick[:, :, :], t["pick"]), (w["expid"][:, :], t["expid"].broadcast_to([D, E1])),
    ]
    for dst, src in pairs:
        sp.dma_start(dst, src).then_inc(sem, 16)
    return 16 * len(pairs)


def layer1(nc, m, t, keep):
    with ExitStack() as ctx:
        l = Mem(nc, ctx)
        w = {
            "wv": l.sb("l1_wv", [D, 2 * D]), "bv": l.sb("l1_bv", [TP, 2 * D]), "wu": l.sb("l1_wu", [D, 2 * D]),
            "bo": l.sb("l1_bo", [D, D]), "bu": l.sb("l1_bu", [D, 2]), "wo": l.sb("l1_wo", [D, 2, D]),
            "router": l.sb("l1_router", [D, E1]), "gate": l.sb("l1_gate", [D, E1, F1]), "up": l.sb("l1_up", [D, E1, F1]),
            "sgate": l.sb("l1_sgate", [D, F1]), "sup": l.sb("l1_sup", [D, F1]), "down": l.sb("l1_down", [D, NC1, D]),
            "sdown": l.sb("l1_sdown", [F1, D]), "pick": l.sb("l1_pick", [D, NC1, D], BF16),
            "identb": l.sb("identb", [D, D], BF16), "expid": l.sb("expert_ids", [D, E1]),
        }
        mixer = l.sb("mixer_values", [D, D, 4 * B])
        values(nc, t, keep, w, mixer)
        mix_tokens(nc, t, keep, mixer)
        finish(nc, t, keep, w, mixer)


def values(nc, t, keep, w, mixer):
    with ExitStack() as ctx:
        l = Mem(nc, ctx)
        xs = l.sb("v_xs", [TP, 2, GI, 2, D])
        xsT = l.sb("v_xsT", [D, 2, SP])
        pre = l.sb("v_pre", [TP, 2, 2, 2 * D])
        pick = l.sb("l1_pick_fp32", [D, NC1, D])
        pT = [l.ps(f"ps_v_T{i}", [D, 512]) for i in range(2)]
        pV = [l.ps(f"ps_v{i}", [D, 512]) for i in range(2)]
        ident = keep["ident"]
        xin = [l.sem(f"v_xs_in{i}") for i in range(2)]
        w_in, turned, xtr, mm, prer, vr = (l.sem(n) for n in ("l1_w_in", "v_turned", "v_xsT_ready", "v_mm", "v_pre_ready", "v_ready"))
        with nc.Block() as block:

            @block.sync
            def _(sp):
                def load(g, par):
                    sp.dma_start(xs[:, par, :, :, :], t["xs"][bass.ds(g * GI, GI)].rearrange("b (t p) d -> p b t d", p=TP)).then_inc(xin[par], 16)

                load(0, 0)
                load(1, 1)
                n = load_layer1(sp, t, w, pick, w_in)
                with sp.Fori(1, NG // 2) as it:
                    for par in range(2):
                        sp.wait_ge(turned, GI * (2 * it + par - 1))
                        load(2 * it + par, par)
                sp.wait_ge(w_in, n)

            @block.gpsimd
            def _(pool):
                pool.wait_ge(w_in, 16 * 16)
                nc.gpsimd.tensor_copy(w["pick"][:, :, :], pick[:, :, :])
                nc.gpsimd.tensor_copy(w["identb"][:, :], ident[:, :])

            @block.tensor
            def _(pe):
                def turn(g, par, b, half):
                    if b == 0:
                        pe.wait_ge(xin[par], 16 * half + 16)
                    i = GI * g + b
                    pe.wait_ge(xtr, i + 1)
                    for q in range(2):
                        x = nc.tensor.transpose(pT[b % 2][:, q * TP:(q + 1) * TP], xs[:, par, b, q, :], ident[0:TP, 0:TP])
                    x.then_inc(turned, 1)

                def project(g, b):
                    i = GI * g + b
                    pe.wait_ge(xtr, i + 3)
                    pe.wait_ge(prer, i + 1)
                    for q in range(2):
                        x = nc.tensor.matmul(pV[b % 2][0:TP, q * 2 * D:(q + 1) * 2 * D], xsT[:, b % 2, q * TP:(q + 1) * TP], w["wv"][:, :], start=True, stop=True)
                    x.then_inc(mm, 1)

                pe.wait_ge(w_in, 16 * 16)
                with pe.Fori(0, NG // 2) as it:
                    for par in range(2):
                        g = it * 2 + par
                        turn(g, par, 0, it)
                        for b in range(GI):
                            if b + 1 < GI:
                                turn(g, par, b + 1, it)
                            project(g, b)

            @block.vector
            def _(v):
                v.sem_inc(prer, 2)
                v.wait_ge(w_in, 16 * 16)
                with v.Fori(0, NG) as g:
                    for b in range(GI):
                        i = GI * g + b
                        v.wait_ge(mm, i + 1)
                        v.wait_ge(vr, i + 1)
                        nc.vector.tensor_tensor(pre[:, b % 2, :, :], pV[b % 2][0:TP, :].rearrange("p (q c) -> p q c", q=2),
                                                w["bv"][:, :].unsqueeze(1).broadcast_to([TP, 2, 2 * D]), ALU.add).then_inc(prer, 1)

            @block.scalar
            def _(act):
                act.sem_inc(xtr, 2)
                act.sem_inc(vr, 2)

                def turned_(g, b):
                    i = GI * g + b
                    act.wait_ge(turned, i + 1)
                    if not (isinstance(g, int) and i < 2):
                        act.wait_ge(mm, i - 1)
                    src = pT[b % 2][:, 0:SP].rearrange("p (q n) -> p q n", q=2)[:, :, ::-1]
                    nc.scalar.copy(xsT[:, b % 2, :].rearrange("p (q n) -> p q n", q=2), src).then_inc(xtr, 1)

                def gate(g, b):
                    i = GI * g + b
                    act.wait_ge(prer, i + 3)
                    dst = mixer[0:TP, :, :].rearrange("p c (n b) -> p n c b", b=B)
                    for q in range(2):
                        o = dst[:, 2 * q:2 * q + 2, :, bass.ds(i, 1)]
                        x = nc.scalar.activation(o, pre[:, b % 2, q, :].rearrange("p (h c a) -> p h c a", h=2, a=1), ACT.Silu)
                    x.then_inc(vr, 1)

                def body(g):
                    for b in range(GI):
                        turned_(g, b)
                        if b:
                            gate(g, b - 1)
                    gate(g, GI - 1)

                body(0)
                with act.Fori(1, NG) as g:
                    body(g)


def mix_tokens(nc, t, keep, mixer):
    with ExitStack() as ctx:
        l = Mem(nc, ctx)
        nu = D // CPU
        toep = l.sb("toeplitz", [TP, 4, 2, CPU, SP])
        stage = l.sb("mixer_stage", [TP, 2, CPU, 4 * B])
        pm = [l.ps(f"ps_mix{i}", [D, 512]) for i in range(4)]
        tin = [l.sem(f"toeplitz_in{i}") for i in range(4)]
        stg, mm, outa, outb, held = (l.sem(n) for n in ("mix_staged", "mix_mm", "mix_out_act", "mix_out_dve", "mix_pool_held"))
        width = TP - 1 + SP
        with nc.Block() as block:

            @block.sync
            def _(sp):
                ap = t["apad"]

                def load(u, r):
                    for h in range(2):
                        src = bass.AP(ap.tensor, u * (CPU * width) + h * D * width, [[1, TP], [width, CPU], [1, SP]])
                        sp.dma_start(toep[:, r, h, :, :], src).then_inc(tin[r], 16)

                for r in range(4):
                    load(r, r)
                with sp.Fori(1, nu // 4) as it:
                    for r in range(4):
                        sp.wait_ge(mm, 2 * (4 * it + r - 3))
                        load(4 * it + r, r)

            @block.gpsimd
            def _(pool):
                def copy(u, r):
                    nc.gpsimd.tensor_copy(stage[:, r, :, :], mixer[0:TP, bass.ds(u * CPU, CPU), :]).then_inc(stg, 1)

                copy(0, 0)
                copy(1, 1)
                with pool.Fori(1, nu // 2) as it:
                    for r in range(2):
                        hold(pool, mm, 2 * (2 * it + r - 1), held)
                        copy(2 * it + r, r)

            @block.tensor
            def _(pe):
                with pe.Fori(0, nu // 4) as it:
                    for r in range(4):
                        u = it * 4 + r
                        pe.wait_ge(tin[r], 32 * it + 32)
                        pe.wait_ge(stg, u + 1)
                        for c in range(CPU // 2):
                            pe.wait_ge((outa, outb)[c], u + 1)
                            bank = pm[(r % 2) * 2 + c]
                            for k in range(2):
                                cp = 2 * c + k
                                for q in range(2):
                                    for h in range(2):
                                        o = bank[h * B:(h + 1) * B, k * SP + q * TP:(k + 1) * SP]
                                        x = nc.tensor.matmul(o, stage[:, r % 2, cp, (2 * q + h) * B:(2 * q + h + 1) * B],
                                                             toep[:, r, h, cp, 0:SP - q * TP], start=q == 0, stop=q == 1, skip_group_check=True)
                            x.then_inc(mm, 1)

            def evacuate(eng, copy, sem, c):
                eng.sem_inc(sem, 2)
                with eng.Fori(0, nu // 2) as it:
                    for r in range(2):
                        u = it * 2 + r
                        eng.wait_ge(mm, 2 * u + c + 1)
                        copy(mixer[:, bass.ds(u * CPU + 2 * c, 2), 0:SP], pm[r * 2 + c][:, 0:2 * SP].rearrange("p (k n) -> p k n", k=2)).then_inc(sem, 1)

            @block.scalar
            def _(act):
                evacuate(act, nc.scalar.copy, outa, 0)

            @block.vector
            def _(v):
                evacuate(v, nc.vector.tensor_copy, outb, 1)


def finish(nc, t, keep, w, mixer):
    order = ["xsT", "gate0", "up0", "u0", "u1", "mixT0", "mixT1", "gate1", "up1", "proj", "gate2", "up2",
             "gate3", "up3", "gate4", "up4", "combT", "bc0", "bc1", "bc2", "bc3", "down", "normT", "router"]
    count = {"xsT": 1, "gate": NC1 + 1, "up": NC1 + 1, "u": 2, "mixT": 2, "proj": 1, "combT": 1, "bc": NC1, "normT": 1, "down": 1, "router": 1}
    back = {"gate", "up", "combT", "bc", "down"}
    nb = 8
    with ExitStack() as ctx:
        l = Mem(nc, ctx)
        xs = l.sb("f_xs", [D, 3, NT, D])
        res = l.sb("f_res", [D, 3, NT, D])
        xsT = l.sb("f_xsT", [D, COL])
        us = l.sb("f_u", [D, 2, COL])
        stage = l.sb("f_mixed", [D, TU, D])
        y = l.sb("f_y", [D, 2, COL])
        h3 = l.sb("f_h3", [D, 3, NT, D])
        xn = l.sb("f_xn", [D, NT, D])
        xnT = l.sb("f_xnT", [D, COL])
        gs = l.sb("f_gate", [D, NC1 + 1, COL])
        gu = l.sb("f_hidden", [D, NC1 + 1, COL])
        st = l.sb("f_stats", [D, NT, 6])
        mv = l.sb("f_meanvar", [D, NT, 2])
        vare = l.sb("f_var_eps", [D, NT])
        rstd = l.sb("f_rstd", [D, NT])
        cons = l.sb("f_consts", [D, 4, NT * E1])
        nmean = l.sb("f_minus_mean", [D, NT])
        shift = l.sb("f_shift", [D, NT])
        lmax = l.sb("f_lmax", [D, NT])
        lsub = l.sb("f_lsub", [D, NT, E1])
        lexp = l.sb("f_lexp", [D, NT, E1])
        lsum = l.sb("f_lsum", [D, 2, NT])
        prob = l.sb("f_prob", [D, NT, E1])
        top = l.sb("f_top", [D, NT, E1])
        topi = l.sb("f_top_i", [D, NT, E1], U32)
        topf = l.sb("f_top_f", [D, NT, E1])
        eq = l.sb("f_eq", [D, 2, NT, E1])
        toppart = l.sb("f_top_part", [D, NT, 3, 2], BF16)
        toprest = l.sb("f_top_rest", [D, 2, NT, 2])
        scaled = l.sb("f_scaled", [D, 2, NT, 3, E1])
        split = l.sb("f_split", [D, NT, D], BF16)
        combT = l.sb("f_combT", [D, COL], BF16)
        bank = [l.ps(f"ps_f{i}", [D, 512]) for i in range(nb)]
        ident = keep["ident"]
        filled = {s: l.sem(f"{s}_filled") for s in count}
        read = {s: l.sem(f"{s}_read") for s in count}
        xin, rin = [l.sem(f"f_xs_in{i}") for i in range(3)], [l.sem(f"f_res_in{i}") for i in range(3)]
        staged, resb, cst, held = (l.sem(n) for n in ("f_staged", "f_res_bias", "f_const", "f_pool_held"))
        mvr, veps, rsr, xnr, lsr, expr_, cbr, hidr = (l.sem(n) for n in ("f_meanvar_ready", "f_vareps_ready", "f_rstd_ready", "f_xn_ready", "f_lsub_ready", "f_lexp_ready", "f_split_ready", "f_hidden_ready"))
        dv, dheld, stored = l.sem("f_dve"), l.sem("f_dve_held"), [l.sem(f"f_stored{i}") for i in range(3)]
        zero, sts, lmr = l.sem("f_split_zero"), l.sem("f_stats_ready"), l.sem("f_lmax_ready")

        def parts(s):
            name = s.rstrip("01234")
            return name, int(s[len(name):] or 0)

        def psum(s):
            return bank[order.index(s) % nb]

        def take(pe, n, s):
            i = order.index(s) - nb
            while isinstance(n, int) and n == NU1 and i >= 0 and parts(order[i])[0] not in back:
                i -= nb
            name, k = parts(order[i])
            unit = n - (name in back) - (i < 0)
            if not (isinstance(n, int) and unit < -1):
                pe.wait_ge(read[name], count[name] * (unit + 1) + k + 1)

        def wait(eng, sems, unit, s):
            name, k = parts(s)
            eng.wait_ge(sems[name], count[name] * (unit + (sems is read)) + k + 1)

        def each_step(eng, step):
            step(0, 0, 0, True, False)
            with eng.Fori(0, (NU1 - 3) // 3) as it:
                for r in range(3):
                    step(3 * it + r + 1, (r + 1) % 3, it + (r + 1) // 3, True, True)
            n = 3 * ((NU1 - 3) // 3) + 1
            while n <= NU1:
                step(n, n % 3, n // 3, n < NU1, True)
                n += 1

        with nc.Block() as block:

            @block.sync
            def _(sp):
                def rows(d, n, r):
                    return t[d].rearrange("b (u j r) d -> r b u j d", j=NT, r=2)[r][:, bass.ds(n, 1)].rearrange("b u j d -> b (u j) d")

                def load(n, par):
                    for r in range(2):
                        sp.dma_start(xs[r * B:(r + 1) * B, par, :, :], rows("xs", n, r)).then_inc(xin[par], 16)
                        sp.dma_start(res[r * B:(r + 1) * B, par, :, :], rows("res2", n, r)).then_inc(rin[par], 16)

                def store(n, par):
                    wait(sp, read, n, "down")
                    for r in range(2):
                        k = NT - 1 if isinstance(n, int) and n == NU1 - 1 and r == 1 else NT
                        o = bass.AP(t["out"].tensor, n * (TU * D) + r * D, [[S * D, B], [2 * D, k], [1, D]])
                        sp.dma_start(o, h3[r * B:(r + 1) * B, par, 0:k, :]).then_inc(stored[par], 16)

                for n in range(2):
                    load(n, n)

                def step(n, par, half, front, backs):
                    if front and not (isinstance(n, int) and n + 2 >= NU1):
                        if not (isinstance(n, int) and n == 0):
                            wait(sp, read, n - 1, "proj")
                        load(n + 2, (par + 2) % 3)
                    if backs:
                        store(n - 1, (par + 2) % 3)

                each_step(sp, step)
                for i in range(3):
                    sp.wait_ge(stored[i], 32 * (NU1 // 3) + 32)

            @block.gpsimd
            def _(pool):
                nc.gpsimd.memset(cons[:, 0, :], EPS).then_inc(cst, 1)
                nc.gpsimd.memset(cons[:, 1, :], -0.5).then_inc(cst, 1)
                nc.gpsimd.memset(cons[:, 2, :], 2.718281828459045).then_inc(cst, 1)
                nc.gpsimd.memset(split[:, :, :], 0.0).then_inc(zero, 1)
                for i in range(3):
                    pool.sem_inc(stored[i], 32)
                nc.gpsimd.memset(cons[:, 3, :], 0.0).then_inc(cst, 1)
                pool.wait_ge(cst, 4)

                def copy(n):
                    nc.gpsimd.tensor_copy(stage[:, :, :], mixer[:, :, bass.ds(n * TU, TU)].rearrange("p c t -> p t c")).then_inc(staged, 1)

                copy(0)

                def step(n, par, half, front, backs):
                    if not front:
                        return
                    pool.wait_ge(rin[par], 32 * half + 32)
                    nc.gpsimd.tensor_tensor(res[:, par, :, :], res[:, par, :, :], w["bo"][:, :].unsqueeze(1).broadcast_to([D, NT, D]), ALU.add).then_inc(resb, 1)
                    if not (isinstance(n, int) and n == NU1 - 1):
                        hold(pool, filled["mixT"], 2 * n + 2, held)
                        copy(n + 1)
                    pool.wait_ge(mvr, n + 1)
                    nc.gpsimd.tensor_tensor(vare[:, :], mv[:, :, 1], cons[:, 0, 0:NT], ALU.add).then_inc(veps, 1)
                    nc.gpsimd.tensor_tensor(nmean[:, :], cons[:, 3, 0:NT], mv[:, :, 0], ALU.subtract).then_inc(veps, 1)
                    pool.wait_ge(veps, 2 * n + 2)
                    nc.gpsimd.tensor_tensor(rstd[:, :], vare[:, :], cons[:, 1, 0:NT], ALU.pow).then_inc(rsr, 1)
                    pool.wait_ge(rsr, 2 * n + 1)
                    nc.gpsimd.tensor_tensor(shift[:, :], nmean[:, :], rstd[:, :], ALU.mult).then_inc(rsr, 1)
                    pool.wait_ge(read["router"], n + 2)
                    nc.gpsimd.tensor_tensor(lexp[:, :, :].rearrange("p j e -> p (j e)"), cons[:, 2, :], lsub[:, :, :].rearrange("p j e -> p (j e)"), ALU.pow).then_inc(expr_, 1)

                each_step(pool, step)

            @block.tensor
            def _(pe):
                def step(n, par, half, front, backs):
                    def gate_up(i):
                        for s, big, small in (("gate", "gate", "sgate"), ("up", "up", "sup")):
                            take(pe, n, f"{s}{i}")
                            k = D if i < NC1 else F1
                            lhs = w[big][:, 2 * i:2 * i + 2, :].rearrange("p e h -> p (e h)") if i < NC1 else w[small][:, :]
                            nc.tensor.matmul(psum(f"{s}{i}")[0:k, 0:COL], lhs, xnT[:, :], start=True, stop=True).then_inc(filled[s], 1)

                    if front:
                        take(pe, n, "xsT")
                        pe.wait_ge(xin[par], 32 * half + 32)
                        for j in range(NT):
                            x = nc.tensor.transpose(psum("xsT")[:, j * D:(j + 1) * D], xs[:, par, j, :], ident[:, :])
                        x.then_inc(filled["xsT"], 1)
                    if backs:
                        gate_up(0)
                    if front:
                        wait(pe, read, n, "xsT")
                        for h in range(2):
                            take(pe, n, f"u{h}")
                            nc.tensor.matmul(psum(f"u{h}")[:, 0:COL], w["wu"][:, h * D:(h + 1) * D], xsT[:, :], start=True, stop=True).then_inc(filled["u"], 1)
                        pe.wait_ge(staged, n + 1)
                        for h in range(2):
                            take(pe, n, f"mixT{h}")
                            for k in range(TU // 2):
                                x = nc.tensor.transpose(psum(f"mixT{h}")[:, k * D:(k + 1) * D], stage[:, h * (TU // 2) + k, :], ident[:, :])
                            x.then_inc(filled["mixT"], 1)
                    if backs:
                        gate_up(1)
                    if front:
                        take(pe, n, "proj")
                        wait(pe, read, n, "mixT1")
                        for j in range(NT):
                            for h in range(2):
                                x = nc.tensor.matmul(psum("proj")[:, j * D:(j + 1) * D], y[:, h, j * D:(j + 1) * D], w["wo"][:, h, :], start=h == 0, stop=h == 1)
                        x.then_inc(filled["proj"], 1)
                    if backs:
                        gate_up(2)
                        gate_up(3)
                        gate_up(4)
                        take(pe, n, "combT")
                        pe.wait_ge(cbr, n)
                        for j in range(NT):
                            x = nc.tensor.transpose(psum("combT")[:, j * D // 2:(j + 1) * D // 2].bitcast(BF16), split[:, j, :], w["identb"][:, :])
                        x.then_inc(filled["combT"], 1)
                        wait(pe, read, n - 1, "combT")
                        for i in range(NC1):
                            take(pe, n, f"bc{i}")
                            nc.tensor.matmul(psum(f"bc{i}")[:, 0:COL], w["pick"][:, i, :], combT[:, :], start=True, stop=True).then_inc(filled["bc"], 1)
                    def down(i):
                        wait(pe, read, n - 1, f"bc{i}")
                        for j in range(NT):
                            x = nc.tensor.matmul(psum("down")[:, j * D:(j + 1) * D], gu[:, i, j * D:(j + 1) * D], w["down"][:, i, :], start=False, stop=i == NC1 - 1, skip_group_check=True)
                        return x

                    if backs:
                        take(pe, n, "down")
                        wait(pe, read, n - 1, "up4")
                        for j in range(NT):
                            nc.tensor.matmul(psum("down")[:, j * D:(j + 1) * D], gu[0:F1, NC1, j * D:(j + 1) * D], w["sdown"][:, :], start=j == 0, stop=False, skip_group_check=True)
                        for i in range(NC1 - 1):
                            down(i)
                    if front:
                        take(pe, n, "normT")
                        pe.wait_ge(xnr, n + 1)
                        for j in range(NT):
                            x = nc.tensor.transpose(psum("normT")[:, j * D:(j + 1) * D], xn[:, j, :], ident[:, :])
                        x.then_inc(filled["normT"], 1)
                    if backs:
                        down(NC1 - 1).then_inc(filled["down"], 1)
                    if front:
                        take(pe, n, "router")
                        wait(pe, read, n, "normT")
                        for j in range(NT):
                            x = nc.tensor.matmul(psum("router")[:, j * E1:(j + 1) * E1], xnT[:, j * D:(j + 1) * D], w["router"][:, :], start=True, stop=True)
                        x.then_inc(filled["router"], 1)

                each_step(pe, step)

            @block.scalar
            def _(act):
                for s in ("xsT", "gate", "u", "combT", "normT"):
                    act.sem_inc(read[s], count[s])

                def step(n, par, half, front, backs):
                    def gate(i):
                        wait(act, filled, n - 1, f"gate{i}")
                        k = D if i < NC1 else F1
                        nc.scalar.activation(gs[0:k, i, :], psum(f"gate{i}")[0:k, 0:COL], ACT.Silu).then_inc(read["gate"], 1)

                    if front:
                        wait(act, filled, n, "xsT")
                        nc.scalar.copy(xsT[:, :], psum("xsT")[:, 0:COL]).then_inc(read["xsT"], 1)
                    if backs:
                        wait(act, read, n - 2, "up4")
                        gate(0)
                    if front:
                        wait(act, read, n - 1, "mixT1")
                        for h in range(2):
                            wait(act, filled, n, f"u{h}")
                            nc.scalar.activation(us[:, h, :], psum(f"u{h}")[:, 0:COL], ACT.Silu, bias=w["bu"][:, h:h + 1]).then_inc(read["u"], 1)
                    if backs:
                        for i in range(1, NC1 + 1):
                            gate(i)
                        wait(act, filled, n - 1, "combT")
                        nc.scalar.copy(combT[:, :], psum("combT")[:, 0:COL // 2].bitcast(BF16)).then_inc(read["combT"], 1)
                    if front:
                        act.wait_ge(rsr, 2 * n + 2)
                        wait(act, read, n - 1, "normT")
                        for j in range(NT):
                            x = nc.scalar.activation(xn[:, j, :], h3[:, par, j, :], ACT.Identity, bias=shift[:, j:j + 1], scale=rstd[:, j:j + 1])
                        x.then_inc(xnr, 1)
                        wait(act, filled, n, "normT")
                        nc.scalar.copy(xnT[:, :], psum("normT")[:, 0:COL]).then_inc(read["normT"], 1)

                each_step(act, step)

            @block.vector
            def _(v):
                for s in ("up", "mixT", "proj", "bc", "down", "router"):
                    v.sem_inc(read[s], count[s])
                v.wait_ge(zero, 1)
                NL = 13

                def step(n, par, half, front, backs):
                    u = n - 1
                    i = [0]

                    def link(x):
                        i[0] += 1
                        x.then_inc(dv, 1)

                    def linked():
                        v.wait_ge(dv, NL * u + i[0])

                    def up(i):
                        wait(v, filled, n - 1, f"up{i}")
                        wait(v, read, n - 1, f"gate{i}")
                        k = D if i < NC1 else F1
                        if i == 0:
                            wait(v, filled, n - 2, "down") if not (isinstance(n, int) and n < 2) else None
                        nc.vector.tensor_tensor(gu[0:k, i, :], psum(f"up{i}")[0:k, 0:COL], gs[0:k, i, :], ALU.mult).then_inc(read["up"], 1)

                    def softmax():
                        bc = lambda a: a.unsqueeze(2).broadcast_to([D, NT, E1])
                        v.wait_ge(expr_, u + 1)
                        link(nc.vector.tensor_reduce(lsum[:, 0, :], lexp[:, :, :], AX.X, ALU.add))
                        linked()
                        link(nc.vector.reciprocal(lsum[:, 1, :], lsum[:, 0, :]))
                        linked()
                        link(nc.vector.tensor_tensor(prob[:, :, :], lexp[:, :, :], bc(lsum[:, 1, :]), ALU.mult))

                    def best():
                        hold(v, dv, NL * u + i[0], dheld)
                        for j in range(NT):
                            x = nc.vector.max(top[:, j, :], prob[:, j, :])
                        link(x)
                        linked()
                        link(nc.vector.tensor_copy(toppart[:, :, 0, :], top[:, :, 0:2]))

                    def best_index():
                        linked()
                        link(nc.vector.tensor_tensor(toprest[:, 0, :, :], top[:, :, 0:2], toppart[:, :, 0, :], ALU.subtract))
                        for j in range(NT):
                            x = nc.vector.max_index(topi[:, j, :], top[:, j, :], prob[:, j, :])
                        link(x)
                        linked()
                        link(nc.vector.tensor_copy(toppart[:, :, 1, :], toprest[:, 0, :, :]))
                        link(nc.vector.tensor_copy(topf[:, :, 0:2], topi[:, :, 0:2]))

                    def chosen():
                        linked()
                        link(nc.vector.tensor_tensor(toprest[:, 1, :, :], toprest[:, 0, :, :], toppart[:, :, 1, :], ALU.subtract))
                        ids = w["expid"][:, :].unsqueeze(1).broadcast_to([D, NT, E1])
                        for r in range(2):
                            x = nc.vector.tensor_tensor(eq[:, r, :, :], ids, topf[:, :, r:r + 1].broadcast_to([D, NT, E1]), ALU.is_equal)
                        link(x)
                        linked()
                        link(nc.vector.tensor_copy(toppart[:, :, 2, :], toprest[:, 1, :, :]))

                    def weights():
                        linked()
                        for r in range(2):
                            x = nc.vector.tensor_tensor(scaled[:, r, :, :, :], eq[:, r, :, :].unsqueeze(2).broadcast_to([D, NT, 3, E1]),
                                                        toppart[:, :, :, r:r + 1].broadcast_to([D, NT, 3, E1]), ALU.mult)
                        link(x)
                        linked()
                        nc.vector.tensor_tensor(split[:, :, 0:3 * E1].rearrange("p j (c e) -> p j c e", e=E1), scaled[:, 0, :, :, :], scaled[:, 1, :, :, :], ALU.add).then_inc(cbr, 1)
                        assert i[0] == NL, i[0]

                    def mixed(h):
                        wait(v, filled, n, f"mixT{h}")
                        if h == 0:
                            wait(v, read, n, "u1")
                        k = TU // 2
                        a = psum(f"mixT{h}")[:, 0:k * D].rearrange("p (t h b) -> p h t b", t=k, h=2)
                        c = slice(h * k * B, (h + 1) * k * B)
                        for q in range(2):
                            x = nc.vector.tensor_tensor(y[:, q, c].rearrange("p (t b) -> p t b", b=B), a[:, q], us[:, q, c].rearrange("p (t b) -> p t b", b=B), ALU.mult)
                        x.then_inc(read["mixT"], 1)

                    if backs:
                        up(0)
                    if front:
                        mixed(0)
                        mixed(1)
                    if backs:
                        up(1)
                        softmax()
                    if front:
                        v.wait_ge(resb, n + 1)
                        v.wait_ge(stored[par], 32 * half + 32)
                        wait(v, filled, n, "proj")
                        nc.vector.tensor_tensor(h3[:, par, :, :].rearrange("p j d -> p (j d)"), psum("proj")[:, 0:COL], res[:, par, :, :].rearrange("p j d -> p (j d)"), ALU.add).then_inc(read["proj"], 1)
                    if backs:
                        best()
                    if front:
                        wait(v, read, n, "proj")
                        for j in range(NT):
                            x = nc.vector.bn_stats(st[:, j, :], h3[:, par, j, :])
                        x.then_inc(sts, 1)
                    if backs:
                        best_index()
                    if front:
                        hold(v, sts, n + 1, dheld)
                        for j in range(NT):
                            x = nc.vector.bn_aggr(mv[:, j, :], st[:, j, :])
                        x.then_inc(mvr, 1)
                    if backs:
                        chosen()
                        weights()
                        up(2)
                    if backs:
                        up(3)
                        up(4)
                        wait(v, read, n - 1, "up4")
                        for i_ in range(NC1):
                            wait(v, filled, n - 1, f"bc{i_}")
                            nc.vector.tensor_tensor(gu[:, i_, :], gu[:, i_, :], psum(f"bc{i_}")[:, 0:COL], ALU.mult).then_inc(read["bc"], 1)
                        wait(v, filled, n - 1, "down")
                        p = (par + 2) % 3
                        a = h3[:, p, :, :].rearrange("p j d -> p (j d)")
                        nc.vector.tensor_tensor(a, psum("down")[:, 0:COL], a, ALU.add).then_inc(read["down"], 1)
                    if front:
                        wait(v, filled, n, "router")
                        lg = psum("router")[:, 0:NT * E1].rearrange("p (j e) -> p j e", e=E1)
                        nc.vector.tensor_reduce(lmax[:, :], lg, AX.X, ALU.max).then_inc(lmr, 1)
                        v.wait_ge(lmr, n + 1)
                        nc.vector.tensor_tensor(lsub[:, :, :], lg, lmax[:, :].unsqueeze(2).broadcast_to([D, NT, E1]), ALU.subtract).then_inc(read["router"], 1)

                each_step(v, step)


def tower(nc, t):
    with ExitStack() as ctx:
        m = Mem(nc, ctx)
        keep = persistent(m)
        setup(nc, m, t, keep)
        embed_and_attend(nc, m, t, keep)
        choose_tokens(nc, m, t, keep)
        experts(nc, m, t, keep)
        layer1(nc, m, t, keep)


_INS = ["x", "L0_tok_W", "L0_tok_b", "L0_tok_token", "L0_tok_pos", "L0_ffn_Wg", "L0_ffn_W1", "L0_ffn_b1", "L0_ffn_W2",
        "L0_ffn_b2", "L1_attn_Wu", "L1_attn_bu", "L1_attn_Wv", "L1_attn_bv", "L1_attn_Wo", "L1_attn_bo", "L1_attn_Wp",
        "L1_attn_bp", "L1_attn_W1", "L1_attn_b1", "L1_attn_W2", "L1_attn_b2", "L1_attn_W3", "L1_attn_b3", "L1_attn_Wz",
        "L1_attn_bz", "L1_ffn_router", "L1_ffn_shared_gate", "L1_ffn_shared_up", "L1_ffn_shared_down", "L1_ffn_W_gate",
        "L1_ffn_W_up", "L1_ffn_W_down"]


def _constants():
    import numpy as np

    pick = np.zeros((D, NC1, D), np.float32)
    for i in range(NC1):
        for r in range(3 * E1):
            if (r % E1) // 2 == i:
                pick[r, i, (r % 2) * F1:(r % 2 + 1) * F1] = 1.0
    return {
        "decay": (np.float32(0.999) ** np.arange(SP, dtype=np.float32)).astype(np.float32).reshape(1, SP),
        "pick": pick,
        "expid": np.arange(E1, dtype=np.float32).reshape(1, E1),
    }


def kernel(**inputs):
    import numpy as _np
    import concourse.bacc as _bacc
    from concourse import mybir as _mybir
    from concourse.bass_utils import run_bass_kernel_spmd as _run

    nc = _bacc.Bacc("TRN2", target_bir_lowering=False, num_devices=1)
    arrays, t = {}, {}
    for name, a in {**{n: inputs[n] for n in _INS}, **_constants()}.items():
        a = _np.ascontiguousarray(a)
        arrays[f"in_{name}"] = a
        t[name] = nc.dram_tensor(f"in_{name}", a.shape, _mybir.dt.from_np(a.dtype), kind="ExternalInput").ap()
    for name, shape in (("apad", (2 * D, TP - 1 + SP)), ("h1", (B, SP, D)), ("xn1", (B, SP, D)), ("res2", (B, SP, D)), ("xs", (B, SP, D))):
        t[name] = nc.dram_tensor(f"scratch_{name}", shape, F32, kind="Internal").ap()
    t["out"] = nc.dram_tensor("out_0_dram", (B, S, D), F32, kind="ExternalOutput").ap()
    tower(nc, t)
    r = _run(nc, [arrays], core_ids=[0])
    return r.results[0]["out_0_dram"]
```

```python
from contextlib import ExitStack

import concourse.bass as bass
from concourse import mybir

F32 = mybir.dt.float32
BF16 = mybir.dt.bfloat16
I32 = mybir.dt.int32
U32 = mybir.dt.uint32
F32R = mybir.dt.float32r
ALU = mybir.AluOpType
ACT = mybir.ActivationFunctionType
AX = mybir.AxisListType

B, C, IMG, NP = 64, 3, 196, 14
PX = IMG // NP
D = 128
KIN = C * PX * PX
S = NP * NP + 1
TP = 99
SP = 2 * TP
EPS = 1e-5
E0, F0 = 8, 256
KTOP = int(S * 2 / E0)
GI = 8
NG = B // GI
ROWS = GI * NP
CPY = C * PX
CH = [9, 9, 8, 8, 8]
CH0 = [sum(CH[:i]) for i in range(len(CH))]
JP = NP // 2


class Mem:

    def __init__(self, nc, stack):
        self.nc, self.stack = nc, stack

    def sb(self, name, shape, dt=F32):
        return self.stack.enter_context(self.nc.sbuf_tensor(name, shape, dt))

    def ps(self, name, shape, dt=F32):
        return self.stack.enter_context(self.nc.psum_tensor(name, shape, dt))

    def sem(self, name):
        return self.stack.enter_context(self.nc.semaphore(name))


def hold(eng, sem, value, passed):
    eng.wait_ge(sem, value)
    eng.sem_inc(passed, 1)


def persistent(m):
    return {
        "ident": m.sb("ident", [D, D]),
        "wT": m.sb("patch_wT", [CH[0] * PX, len(CH), D]),
        "posT": m.sb("posT", [D, SP]),
        "score": m.sb("score", [TP, 2, B, E0]),
        "slot_idx": m.sb("slot_idx", [SLOT2, B * NPAIR]),
        "slot_gate": m.sb("slot_gate", [SLOT2, B * NPAIR]),
        "slot_row": m.sb("slot_row", [SLOT2, B * NPAIR], I32),
    }


def pixel_buffers(m):
    return {"px": m.sb("pixels", [ROWS, 2, C, PX * IMG]), "in": [m.sem(f"px_in{i}") for i in range(2)]}


def load_pixels(sp, t, pixels, g, par):
    for b in range(GI):
        sp.dma_start(pixels["px"][b * NP:(b + 1) * NP, par, :, :],
                     t["x"][g * GI + b].rearrange("c (i y) w -> i c (y w)", i=NP)).then_inc(pixels["in"][par], 16)


def setup(nc, m, t, keep, pixels):
    with ExitStack() as ctx:
        l = Mem(nc, ctx)
        wtok = l.sb("wtok_rows", [D, KIN])
        pos = l.sb("pos_rows", [TP, 2, D])
        btok = l.sb("btok", [D, 1])
        tokc = l.sb("tokc", [D, 1])
        w3 = l.sb("coef_w", [D, 3, D])
        wz = l.sb("coef_wz", [D, 2 * D])
        rows = l.sb("coef_rows", [TP, 5, D])
        bz = l.sb("coef_bz", [D, 2])
        decay = l.sb("decay", [D, SP])
        half = l.sb("one_half", [TP, 2])
        posi = l.sb("posi", [TP, 2], I32)
        posf = l.sb("posf", [TP, 2])
        hc = l.sb("hc", [TP, 2, D])
        hn = l.sb("hn", [TP, 2, D])
        sq = l.sb("hc_sq", [TP, 2, D])
        ss = l.sb("hc_ss", [TP, 2])
        hT = l.sb("hT", [D, SP])
        apad = l.sb("apad", [D, 2, TP - 1 + SP])
        ptr = l.ps("setup_tr", [D, 4, 512])
        pmm = l.ps("setup_mm", [D, 512])
        ident, wT, posT = keep["ident"], keep["wT"], keep["posT"]
        loads, loads2, idz, idd, iot = (l.sem(n) for n in ("su_loads", "su_loads2", "su_idz", "su_ident", "su_iota"))
        tr, ev, mm, dv = (l.sem(n) for n in ("su_tr", "su_evac", "su_mm", "su_dve"))
        apd, apz, rms = l.sem("su_apad_out"), l.sem("su_pz"), l.sem("su_rms")
        with nc.Block() as block:

            @block.sync
            def _(sp):
                sp.dma_start(wtok[:, :], t["L0_tok_W"]).then_inc(loads, 16)
                sp.dma_start(pos[:, 0, :], t["L0_tok_pos"][0:TP, :]).then_inc(loads, 16)
                sp.wait_ge(apz, 1)
                sp.dma_start(pos[0:S - TP, 1, :], t["L0_tok_pos"][TP:S, :]).then_inc(loads, 16)
                sp.dma_start(btok[:, :], t["L0_tok_b"].rearrange("(p a) -> p a", a=1)).then_inc(loads, 16)
                sp.dma_start(tokc[:, :], t["L0_tok_token"].rearrange("a p -> p a")).then_inc(loads, 16)
                for i in range(3):
                    sp.dma_start(w3[:, i, :], t[f"L1_attn_W{i + 1}"]).then_inc(loads2, 16)
                sp.dma_start(wz[:, :], t["L1_attn_Wz"]).then_inc(loads2, 16)
                for i in range(2):
                    sp.dma_start(bz[:, i:i + 1], t["L1_attn_bz"][i * D:(i + 1) * D].rearrange("(p a) -> p a", a=1)).then_inc(loads2, 16)
                sp.dma_start(decay[:, :], t["decay"].broadcast_to([D, SP])).then_inc(loads2, 16)
                for i, n in enumerate(("Wp", "bp", "b1", "b2", "b3")):
                    v = t["L1_attn_" + n]
                    v = v if n == "Wp" else v.rearrange("(a p) -> a p", a=1)
                    sp.dma_start(rows[:, i, :], v.broadcast_to([TP, D])).then_inc(loads2, 16)
                for g in range(2):
                    load_pixels(sp, t, pixels, g, g)
                sp.wait_ge(dv, 23)
                sp.dma_start(t["apad"].rearrange("(a p) n -> p a n", p=D), apad[:, :, :]).then_inc(apd, 16)
                sp.wait_ge(apd, 16)

            @block.gpsimd
            def _(pool):
                nc.gpsimd.memset(pos[:, 1, :], 0.0).then_inc(apz, 1)
                nc.gpsimd.memset(half[:, :], 0.5)
                nc.gpsimd.memset(ident[:, :], 0.0).then_inc(idz, 1)
                pool.wait_ge(idz, 1)
                nc.gpsimd.affine_select(out=ident[:, :], in_=ident[:, :], compare_op=ALU.not_equal, fill=1.0,
                                        base=0, pattern=[[-1, D]], channel_multiplier=1).then_inc(idd, 1)
                nc.gpsimd.iota(posi[:, :], pattern=[[TP, 2]], base=0, channel_multiplier=1).then_inc(iot, 1)
                for k in range(4):
                    pool.wait_ge(dv, 3 + 5 * k)
                    nc.gpsimd.tensor_tensor(ss[:, :], ss[:, :], half[:, :], ALU.pow).then_inc(rms, 1)

            @block.tensor
            def _(pe):
                pe.wait_ge(idd, 1)
                pe.wait_ge(loads, 80)
                for i, n in enumerate(CH):
                    k0, k = CH0[i] * PX, n * PX
                    nc.tensor.transpose(ptr[0:k, i // 2, (i % 2) * D:(i % 2 + 1) * D], wtok[:, k0:k0 + k], ident[:, :])
                for i in range(2):
                    x = nc.tensor.transpose(ptr[:, 3, i * TP:(i + 1) * TP], pos[:, i, :], ident[0:TP, 0:TP])
                x.then_inc(tr, 1)
                for k in range(4):
                    pe.wait_ge(dv, 6 + 5 * k)
                    pe.wait_ge(ev, 6 + k)
                    for i in range(2):
                        x = nc.tensor.transpose(ptr[:, 3, i * TP:(i + 1) * TP], hn[:, i, :], ident[0:TP, 0:TP])
                    x.then_inc(tr, 1)
                    pe.wait_ge(ev, 7 + k)
                    if k == 0:
                        pe.wait_ge(loads2, 16 * 12)
                    for i in range(2):
                        if k < 3:
                            x = nc.tensor.matmul(pmm[0:TP, i * D:(i + 1) * D], hT[:, i * TP:(i + 1) * TP], w3[:, k, :], start=True, stop=True)
                        else:
                            x = nc.tensor.matmul(pmm[:, i * SP:(i + 1) * SP], wz[:, i * D:(i + 1) * D], hT[:, :], start=True, stop=True)
                    x.then_inc(mm, 1)

            @block.scalar
            def _(act):
                act.wait_ge(tr, 1)
                for i, n in enumerate(CH):
                    nc.scalar.copy(wT[0:n * PX, i, :], ptr[0:n * PX, i // 2, (i % 2) * D:(i % 2 + 1) * D]).then_inc(ev, 1)
                nc.scalar.activation(posT[:, 1:SP], ptr[:, 3, 1:SP], ACT.Identity, bias=btok[:, 0:1])
                nc.scalar.activation(posT[:, 0:1], ptr[:, 3, 0:1], ACT.Identity, bias=tokc[:, 0:1]).then_inc(ev, 1)
                for k in range(4):
                    act.wait_ge(tr, 2 + k)
                    if k:
                        act.wait_ge(mm, k)
                    nc.scalar.copy(hT[:, :], ptr[:, 3, 0:SP]).then_inc(ev, 1)

            @block.vector
            def _(v):
                n = [0]

                def link(x):
                    n[0] += 1
                    x.then_inc(dv, 1)
                    v.wait_ge(dv, n[0])

                v.wait_ge(iot, 1)
                nc.vector.memset(apad[:, :, :], 0.0)
                nc.vector.tensor_copy(posf[:, :], posi[:, :])
                v.wait_ge(loads2, 16 * 12)
                link(nc.vector.memset(sq[:, :, :], 0.0))
                for k in range(4):
                    for i in range(2):
                        if k == 0:
                            x = nc.vector.scalar_tensor_tensor(out=hc[:, i, :], in0=rows[:, 0, :], scalar=posf[:, i:i + 1], in1=rows[:, 1, :], op0=ALU.mult, op1=ALU.add)
                        else:
                            v.wait_ge(mm, k)
                            x = nc.vector.tensor_tensor(hc[:, i, :], pmm[0:TP, i * D:(i + 1) * D], rows[:, 1 + k, :], ALU.add)
                    link(x)
                    for i in range(2):
                        x = nc.vector.tensor_tensor_reduce(out=sq[:, i, :], in0=hc[:, i, :], in1=hc[:, i, :], scale=1.0 / D, scalar=0.0, op0=ALU.mult, op1=ALU.add, accum_out=ss[:, i:i + 1])
                    link(x)
                    v.wait_ge(rms, k + 1)
                    link(nc.vector.tensor_scalar(ss[:, :], ss[:, :], 1e-8, None, ALU.add))
                    link(nc.vector.reciprocal(ss[:, :], ss[:, :]))
                    if k:
                        v.wait_ge(tr, 1 + k)
                    for i in range(2):
                        x = nc.vector.tensor_scalar(hn[:, i, :], hc[:, i, :], ss[:, i:i + 1], 0.0, ALU.mult, ALU.max)
                    link(x)
                v.wait_ge(mm, 4)
                for i in range(2):
                    link(nc.vector.scalar_tensor_tensor(out=apad[:, i, TP - 1:TP - 1 + SP], in0=pmm[:, i * SP:(i + 1) * SP], scalar=bz[:, i:i + 1], in1=decay[:, :], op0=ALU.add, op1=ALU.mult))


def embed_and_attend(nc, m, t, keep, pixels):
    with ExitStack() as ctx:
        l = Mem(nc, ctx)
        cut = l.sb("pixels_cut", [ROWS, 2, 2, KIN])
        xT = l.sb("pixelsT", [CH[0] * PX, 2, len(CH), 2 * ROWS])
        h0T = l.sb("tokensT", [D, GI, SP])
        h = l.sb("h", [TP, GI, 2, D])
        xn = l.sb("xn", [TP, GI, 2, D])
        xnT = l.sb("xnT", [D, GI, SP])
        sqT = l.sb("xnT_sq", [D, GI, SP])
        dist = l.sb("neg_half_dist", [TP, GI, 2, SP])
        wgt = l.sb("attn_weights", [TP, GI, 2, SP])
        h1 = l.sb("h1", [TP, GI, 2, D])
        xn1 = l.sb("xn1", [TP, GI, 2, D])
        xn1T = l.sb("xn1T", [D, GI, SP])
        wg = l.sb("router_w", [D, E0])
        nhalf = l.sb("minus_half", [D, TP])
        st = l.sb("ln_stats", [TP, 8, 4, 6])
        mv = l.sb("ln_meanvar", [TP, 8, 4, 2])
        rstd = l.sb("ln_rstd", [TP, 8, 4])
        vare = l.sb("ln_var_eps", [TP, 8, 4])
        mhalf = l.sb("pow_minus_half", [TP, 4])
        epst = l.sb("ln_eps", [TP, 4])
        tmp4 = l.sb("var_rstd", [TP, 4, 4])
        zerot = l.sb("zeros", [TP, 4])
        nmean = l.sb("minus_mean", [TP, 4, 4])
        shift = l.sb("shift", [TP, 4, 4])
        nhsq = l.sb("neg_half_sq", [TP, GI, 2])
        rsum = l.sb("row_sum", [TP, GI, 2])
        rinv = l.sb("row_inv", [TP, 4])
        lmax = l.sb("logit_max", [TP, 2, GI])
        lsub = l.sb("logit_sub", [TP, 2, GI, E0])
        lexp = l.sb("logit_exp", [TP, 2, GI, E0])
        lsum = l.sb("logit_sum", [TP, 2, GI])
        linv = l.sb("logit_inv", [TP, 2, GI])
        pT = [l.ps(f"ps_pixelsT{i}", [D, 512]) for i in range(3)]
        pO = l.ps("ps_tokens", [D, 512])
        ring = [l.ps(f"ps_ring{i}", [D, 512]) for i in range(3)]
        pL = l.ps("ps_logits", [D, 512])
        ident, wT, posT, score = keep["ident"], keep["wT"], keep["posT"], keep["score"]
        px, px_in, wg_in = pixels["px"], pixels["in"], l.sem("wg_in")
        tokT, evAC, evB, tokM, evO = (l.sem(n) for n in ("tok_T", "tok_evacAC", "tok_evacB", "tok_M", "tok_added"))
        full = l.sem("ring_full")
        hrd, xnr, xtr, ds_r, ex_r = (l.sem(n) for n in ("h_ready", "xn_ready", "xnT_ready", "dist_ready", "weights_ready"))
        h1r, xn1r, xn1tr, lgr, lfree, scr = (l.sem(n) for n in ("h1_ready", "xn1_ready", "xn1T_ready", "logits_ready", "lsub_ready", "lexp_ready"))
        dv, ac, cst, stored = l.sem("p1_dve"), l.sem("p1_act"), l.sem("p1_const"), l.sem("h1_stored")
        score_done, sqr, cutr = l.sem("score_done"), l.sem("sq_ready"), l.sem("cut_ready")
        mvr, rsr, epsr, pgo = l.sem("meanvar_ready"), l.sem("rstd_ready"), l.sem("vareps_ready"), l.sem("p1_powers")
        held, sv, shr = l.sem("p1_dve_held"), l.sem("p1_softmax"), l.sem("shift_ready")

        order = ([f"rows{k}" for k in range(4)] + [f"scores{k}" for k in range(4)] + [f"turn{k}" for k in range(4)]
                 + [f"dots{k}" for k in range(6)] + ["mix0", "dots6", "dots7", "mix1", "mix2", "mix3"])
        NU = len(order)
        reader = {"rows": (hrd, 4), "scores": (xn1tr, 4), "turn": (xtr, 4), "dots": (ds_r, 8), "mix": (h1r, 4)}

        def slot(s):
            return ring[order.index(s) % 3]

        def take(pe, g, s):
            i = order.index(s) - 3
            if isinstance(g, int):
                while i >= 0 and order[i][:-1] == {0: "scores", NG: "rows"}.get(g):
                    i -= 3
                if g == 0 and i < 0:
                    return
            stage, k = order[i][:-1], int(order[i][-1])
            sem, count = reader[stage]
            pe.wait_ge(sem, count * (g - (stage == "scores") - (i < 0)) + k + 1)

        def filled(eng, g, s):
            i = order.index(s) + 1
            if isinstance(g, int) and g == 0:
                i -= 4 if i > 4 else 0
            else:
                i = NU * g - 4 + i - (4 if isinstance(g, int) and g == NG else 0)
            eng.wait_ge(full, i)

        with nc.Block() as block:

            @block.sync
            def _(sp):
                sp.dma_start(wg[:, :], t["L0_ffn_Wg"]).then_inc(wg_in, 16)

                def store(g):
                    sp.wait_ge(h1r, 4 * g + 4)
                    sp.dma_start(t["h1"][bass.ds(g * GI, GI)].rearrange("b (t p) d -> p b t d", p=TP), h1[:, :, :, :]).then_inc(stored, 16)
                    sp.wait_ge(xn1r, 4 * g + 4)
                    sp.dma_start(t["xn1"][bass.ds(g * GI, GI)].rearrange("b (t p) d -> p b t d", p=TP), xn1[:, :, :, :]).then_inc(stored, 16)

                with sp.Fori(0, 3) as it:
                    for par in range(2):
                        g = it * 2 + par
                        sp.wait_ge(cutr, JP * g + JP)
                        load_pixels(sp, t, pixels, g + 2, par)
                        store(g)
                store(6)
                store(7)
                sp.wait_ge(stored, 32 * NG + 32)

            @block.gpsimd
            def _(pool):
                nc.gpsimd.memset(nhalf[:, :], -0.5).then_inc(cst, 1)
                nc.gpsimd.memset(h0T[:, :, SP - 1:SP], 0.0).then_inc(cst, 1)
                nc.gpsimd.memset(wgt[:, :, :, SP - 1:SP], 1.0).then_inc(cst, 1)
                nc.gpsimd.memset(mhalf[:, :], -0.5).then_inc(pgo, 1)
                nc.gpsimd.memset(epst[:, :], EPS).then_inc(pgo, 1)
                nc.gpsimd.memset(zerot[:, :], 0.0).then_inc(pgo, 1)
                pool.sem_inc(stored, 32)

                def rstds(g, k, first):
                    pool.wait_ge(mvr, 8 * g + k + (1 if first else 5))
                    if first and k == 0:
                        pool.wait_ge(pgo, 3)
                    j = k if first else 4 + k
                    nc.gpsimd.tensor_tensor(vare[:, j, :], mv[:, j, :, 1], epst[:, :], ALU.add).then_inc(epsr, 1)
                    pool.wait_ge(epsr, 8 * g + j + 1)
                    nc.gpsimd.tensor_tensor(rstd[:, j, :], vare[:, j, :], mhalf[:, :], ALU.pow).then_inc(rsr, 1)
                    if not first:
                        nc.gpsimd.tensor_tensor(nmean[:, k, :], zerot[:, :], mv[:, j, :, 0], ALU.subtract).then_inc(shr, 1)
                        pool.wait_ge(rsr, 8 * g + j + 1)
                        pool.wait_ge(shr, 8 * g + 2 * k + 1)
                        nc.gpsimd.tensor_tensor(shift[:, k, :], nmean[:, k, :], rstd[:, j, :], ALU.mult).then_inc(shr, 1)

                with pool.Fori(0, NG) as g:
                    for k in range(4):
                        rstds(g, k, True)
                    for k in range(4):
                        rstds(g, k, False)

            @block.tensor
            def _(pe):
                def T(g, jp):
                    u = JP * g + jp
                    pe.wait_ge(cutr, u + 1)
                    if not (isinstance(g, int) and u == 0):
                        pe.wait_ge(evAC, u * 2)
                        pe.wait_ge(evB, u)
                    for c, n in enumerate(CH):
                        for j in range(2):
                            o = (c % 2) * 2 * ROWS + j * ROWS
                            x = nc.tensor.transpose(pT[c // 2][0:n * PX, o:o + ROWS], cut[:, jp % 2, j, CH0[c] * PX:(CH0[c] + n) * PX], ident[0:ROWS, 0:ROWS])
                    x.then_inc(tokT, 1)

                def M(g, jp):
                    u = JP * g + jp
                    pe.wait_ge(evAC, u * 2 + 2)
                    pe.wait_ge(evB, u + 1)
                    if not (isinstance(g, int) and u == 0):
                        pe.wait_ge(evO, u)
                    for c, n in enumerate(CH):
                        x = nc.tensor.matmul(pO[:, 0:2 * ROWS], wT[0:n * PX, c, :], xT[0:n * PX, jp % 2, c, :], start=c == 0, stop=c == len(CH) - 1)
                    x.then_inc(tokM, 1)

                def tokens_rows(g, k):
                    take(pe, g, f"rows{k}")
                    if k == 0:
                        pe.wait_ge(evO, JP * g + JP)
                    for i in range(2):
                        for q in range(2):
                            o = (2 * i + q) * D
                            x = nc.tensor.transpose(slot(f"rows{k}")[0:TP, o:o + D], h0T[:, 2 * k + i, q * TP:(q + 1) * TP], ident[:, :])
                    x.then_inc(full, 1)

                def turn(src, ready, g, group, k, use):
                    take(pe, g, f"{use}{k}")
                    pe.wait_ge(ready, 4 * group + k + 1)
                    for i in range(2):
                        for q in range(2):
                            o = i * SP + q * TP
                            x = nc.tensor.transpose(slot(f"{use}{k}")[:, o:o + TP], src[:, 2 * k + i, q, :], ident[0:TP, 0:TP])
                    x.then_inc(full, 1)

                def dots(g, b):
                    take(pe, g, f"dots{b}")
                    pe.wait_ge(xtr, 4 * g + b // 2 + 1)
                    for q in range(2):
                        o = slot(f"dots{b}")[0:TP, q * SP:(q + 1) * SP]
                        nc.tensor.matmul(o, xnT[:, b, q * TP:(q + 1) * TP], xnT[:, b, :], start=True, stop=False)
                        x = nc.tensor.matmul(o, nhalf[:, :], sqT[:, b, :], start=False, stop=True)
                    x.then_inc(full, 1)

                def mix(g, k):
                    take(pe, g, f"mix{k}")
                    pe.wait_ge(ex_r, 8 * g + 2 * k + 2)
                    for i in range(2):
                        for q in range(2):
                            o = (2 * i + q) * D
                            for s, n in enumerate((TP, S - TP)):
                                x = nc.tensor.matmul(slot(f"mix{k}")[0:TP, o:o + D], wgt[0:n, 2 * k + i, s, q * TP:(q + 1) * TP], xn[0:n, 2 * k + i, s, :], start=s == 0, stop=s == 1)
                    x.then_inc(full, 1)

                def logits(g):
                    pe.wait_ge(xn1tr, 4 * g + 4)
                    pe.wait_ge(lfree, g + 1)
                    for b in range(GI):
                        for q in range(2):
                            o = (q * GI + b) * E0
                            x = nc.tensor.matmul(pL[0:TP, o:o + E0], xn1T[:, b, q * TP:(q + 1) * TP], wg[:, :], start=True, stop=True)
                    x.then_inc(lgr, 1)

                def scores(g):
                    for k in range(4):
                        turn(xn1, xn1r, g, g - 1, k, "scores")

                def body(g, more):
                    f = [lambda jp=jp: (M(g + 1, jp - 1) if jp else None, T(g + 1, jp) if jp < JP else None) for jp in range(JP + 1)]
                    if not more:
                        f = [lambda: None] * (JP + 1)
                    later = not (isinstance(g, int) and g == 0)
                    for k in range(4):
                        tokens_rows(g, k)
                    f[0]()
                    if later:
                        scores(g)
                    f[1]()
                    turn(xn, xnr, g, g, 0, "turn")
                    turn(xn, xnr, g, g, 1, "turn")
                    if later:
                        logits(g - 1)
                    turn(xn, xnr, g, g, 2, "turn")
                    turn(xn, xnr, g, g, 3, "turn")
                    f[2]()
                    for k in range(2):
                        dots(g, 2 * k)
                        dots(g, 2 * k + 1)
                        f[3 + k]()
                    dots(g, 4)
                    dots(g, 5)
                    mix(g, 0)
                    f[5]()
                    dots(g, 6)
                    dots(g, 7)
                    mix(g, 1)
                    f[6]()
                    mix(g, 2)
                    f[7]()
                    mix(g, 3)

                pe.wait_ge(cst, 4)
                pe.wait_ge(wg_in, 16)
                for jp in range(JP):
                    T(0, jp)
                    M(0, jp)
                body(0, True)
                with pe.Fori(0, 3) as it:
                    body(it * 2 + 1, True)
                    body(it * 2 + 2, True)
                body(NG - 1, False)
                scores(NG)
                logits(NG - 1)

            @block.scalar
            def _(act):
                def pixels(g, jp):
                    u = JP * g + jp
                    act.wait_ge(tokT, u + 1)
                    if not (isinstance(g, int) and u < 2):
                        act.wait_ge(tokM, u - 1 if jp else u)
                    k = CH[0] * PX
                    nc.scalar.copy(xT[0:k, jp % 2, 0:2, :], pT[0][0:k, 0:4 * ROWS].rearrange("p (c n) -> p c n", c=2)).then_inc(evAC, 1)
                    k = CH[4] * PX
                    nc.scalar.copy(xT[0:k, jp % 2, 4, :], pT[2][0:k, 0:2 * ROWS]).then_inc(evAC, 1)

                def cut_pair(g, jp, par, half):
                    u = JP * g + jp
                    if jp == 0:
                        act.wait_ge(px_in[par], 128 * half + 128)
                    if not (isinstance(g, int) and g == 0 and jp < 2):
                        act.wait_ge(tokT, u - 1 if jp else u)
                    rows = px[:, par, :, :].rearrange("p c (y j x) -> p j (c y) x", y=PX, j=NP)
                    nc.scalar.copy(cut[:, jp % 2, :, :].rearrange("p j (r x) -> p j r x", x=PX), rows[:, 2 * jp:2 * jp + 2]).then_inc(cutr, 1)

                def take_rows(g, k):
                    filled(act, g, f"rows{k}")
                    if not (isinstance(g, int) and g == 0):
                        act.wait_ge(h1r, 4 * g - 3 + k)
                    nc.scalar.copy(h[:, 2 * k:2 * k + 2, :, :].rearrange("p i q d -> p (i q d)"), slot(f"rows{k}")[0:TP, :]).then_inc(hrd, 1)

                def turned(g, k):
                    filled(act, g, f"turn{k}")
                    o = xnT[:, 2 * k:2 * k + 2, :].rearrange("p i n -> p (i n)")
                    nc.scalar.copy(o, slot(f"turn{k}")[:, 0:2 * SP])
                    nc.scalar.activation(sqT[:, 2 * k:2 * k + 2, :].rearrange("p i n -> p (i n)"), slot(f"turn{k}")[:, 0:2 * SP], ACT.Square).then_inc(xtr, 1)

                def weights(g, b):
                    act.wait_ge(ds_r, 8 * g + b + 1)
                    nc.scalar.activation(dist[:, b, :, :], dist[:, b, :, :], ACT.Exp, scale=2.0).then_inc(ac, 1)
                    act.wait_ge(ac, 8 * g + b + 1)
                    for q in range(2):
                        x = nc.scalar.activation(wgt[:, b, q, 0:S], dist[:, b, q, 0:S], ACT.Exp, accum_out=rsum[:, b, q:q + 1])
                    x.then_inc(ex_r, 1)

                def turned1(g, k):
                    filled(act, g, f"scores{k}")
                    nc.scalar.copy(xn1T[:, 2 * k:2 * k + 2, :].rearrange("p i n -> p (i n)"), slot(f"scores{k}")[:, 0:2 * SP]).then_inc(xn1tr, 1)

                def normalise(g, k):
                    act.wait_ge(shr, 8 * g + 2 * k + 2)
                    for q in range(4):
                        x = nc.scalar.activation(xn1[:, 2 * k + q // 2, q % 2, :], h1[:, 2 * k + q // 2, q % 2, :], ACT.Identity, bias=shift[:, k, q:q + 1], scale=rstd[:, 4 + k, q:q + 1])
                    x.then_inc(xn1r, 1)

                def softmax(g):
                    act.wait_ge(lfree, g + 2)
                    nc.scalar.activation(lexp[:, :, :, :], lsub[:, :, :, :], ACT.Exp).then_inc(scr, 1)

                def body(g, par, half, more):
                    f = [lambda jp=jp: (pixels(g + 1, jp), cut_pair(g + 1, jp + 1, 1 - par, half + par) if jp + 1 < JP else None) for jp in range(JP)]
                    later = not (isinstance(g, int) and g == 0)
                    if not more:
                        f = [lambda: None] * JP
                    take_rows(g, 0)
                    take_rows(g, 1)
                    if later:
                        normalise(g - 1, 2)
                    take_rows(g, 2)
                    take_rows(g, 3)
                    if more:
                        pixels(g + 1, 0)
                    if more:
                        cut_pair(g + 1, 1, 1 - par, half + par)
                    if later:
                        normalise(g - 1, 3)
                    if later:
                        for k in range(4):
                            turned1(g, k)
                    f[1]()
                    for k in range(4):
                        turned(g, k)
                    f[2]()
                    for k in range(4):
                        weights(g, 2 * k)
                        weights(g, 2 * k + 1)
                        if k == 1 and later:
                            softmax(g - 1)
                        if k == 3:
                            normalise(g, 0)
                        f[3 + k]()
                    if not (isinstance(g, int) and g + 2 >= NG):
                        cut_pair(g + 2, 0, par, half + 1)
                    normalise(g, 1)

                cut_pair(0, 0, 0, 0)
                for jp in range(JP):
                    if jp + 1 < JP:
                        cut_pair(0, jp + 1, 0, 0)
                    pixels(0, jp)
                cut_pair(1, 0, 1, 0)
                body(0, 0, 0, True)
                with act.Fori(0, 2) as it:
                    body(it * 2 + 1, 1, it, True)
                    body(it * 2 + 2, 0, it + 1, True)
                for g in range(5, NG):
                    body(g, g % 2, g // 2, g + 1 < NG)
                normalise(NG - 1, 2)
                normalise(NG - 1, 3)
                for k in range(4):
                    turned1(NG, k)
                softmax(NG - 1)

            @block.vector
            def _(v):
                def pixels(g, jp):
                    u = JP * g + jp
                    v.wait_ge(tokT, u + 1)
                    if not (isinstance(g, int) and u < 2):
                        v.wait_ge(tokM, u - 1 if jp else u)
                    k = CH[2] * PX
                    nc.vector.tensor_copy(xT[0:CH[2] * PX, jp % 2, 2:4, :], pT[1][0:k, 0:4 * ROWS].rearrange("p (c n) -> p c n", c=2)).then_inc(evB, 1)

                def add_pos(g, jp):
                    u = JP * g + jp
                    v.wait_ge(tokM, u + 1)
                    if jp == 0:
                        if isinstance(g, int) and g == 0:
                            v.wait_ge(cst, 3)
                        else:
                            filled(v, g - 1, "rows3")
                    o = h0T[:, :, 1:S].rearrange("p b (i j) -> p j b i", j=NP)[:, 2 * jp:2 * jp + 2]
                    a = pO[:, 0:2 * ROWS].rearrange("p (j b i) -> p j b i", j=2, b=GI)
                    b = posT[:, 1:S].rearrange("p (i j) -> p j i", j=NP)[:, 2 * jp:2 * jp + 2].unsqueeze(2).broadcast_to([D, 2, GI, NP])
                    for j in range(2):
                        x = nc.vector.tensor_tensor(o[:, j], a[:, j], b[:, j], ALU.add)
                    x.then_inc(evO, 1)

                def link(x, base, i):
                    x.then_inc(dv, 1)
                    v.wait_ge(dv, base + i)

                NL = 2 * 4 + 4 + 4

                def body(g, more):
                    i = [0]

                    def c(x):
                        i[0] += 1
                        link(x, NL * g, i[0])

                    def stats(src, k, j):
                        for q in range(4):
                            x = nc.vector.bn_stats(st[:, j, q, :], src[:, 2 * k + q // 2, q % 2, :])
                        i[0] += 1
                        x.then_inc(dv, 1)
                        hold(v, dv, NL * g + i[0], held)
                        for q in range(4):
                            x = nc.vector.bn_aggr(mv[:, j, q, :], st[:, j, q, :])
                        x.then_inc(mvr, 1)

                    def first(k):
                        v.wait_ge(hrd, 4 * g + k + 1)
                        stats(h, k, k)

                    def second(k):
                        v.wait_ge(rsr, 8 * g + k + 1)
                        for q in range(4):
                            x = nc.vector.tensor_scalar(xn[:, 2 * k + q // 2, q % 2, :], h[:, 2 * k + q // 2, q % 2, :], mv[:, k, q, 0:1], rstd[:, k, q:q + 1], ALU.subtract, ALU.mult)
                        x.then_inc(xnr, 1)
                        c(nc.vector.tensor_tensor(tmp4[:, k, :], mv[:, k, :, 1], rstd[:, k, :], ALU.mult))
                        nc.vector.scalar_tensor_tensor(out=nhsq[:, 2 * k:2 * k + 2, :].rearrange("p i q -> p (i q)"), in0=tmp4[:, k, :], scalar=-D / 2, in1=rstd[:, k, :], op0=ALU.mult, op1=ALU.mult).then_inc(sqr, 1)

                    def distance(b):
                        filled(v, g, f"dots{b}")
                        if b % 2 == 0:
                            v.wait_ge(sqr, 4 * g + b // 2 + 1)
                        for q in range(2):
                            x = nc.vector.tensor_scalar(dist[:, b, q, :], slot(f"dots{b}")[0:TP, q * SP:(q + 1) * SP], nhsq[:, b, q:q + 1], 0.0, ALU.add, ALU.min)
                        x.then_inc(ds_r, 1)

                    def residual(k):
                        filled(v, g, f"mix{k}")
                        if k == 0:
                            v.wait_ge(stored, 32 * g + 32)
                        c(nc.vector.reciprocal(rinv[:, :], rsum[:, 2 * k:2 * k + 2, :].rearrange("p i q -> p (i q)")))
                        for q in range(4):
                            x = nc.vector.scalar_tensor_tensor(out=h1[:, 2 * k + q // 2, q % 2, :], in0=slot(f"mix{k}")[0:TP, q * D:(q + 1) * D], scalar=rinv[:, q:q + 1], in1=h[:, 2 * k + q // 2, q % 2, :], op0=ALU.mult, op1=ALU.add)
                        x.then_inc(h1r, 1)
                        v.wait_ge(h1r, 4 * g + k + 1)
                        stats(h1, k, 4 + k)

                    f = [lambda jp=jp: (add_pos(g + 1, jp - 1) if jp else None, pixels(g + 1, jp) if jp < JP else None) for jp in range(JP + 1)]
                    if not more:
                        f = [lambda: None] * (JP + 1)
                    later = not (isinstance(g, int) and g == 0)
                    first(0)
                    f[0]()
                    first(1)
                    first(2)
                    second(0)
                    first(3)
                    second(1)
                    f[1]()
                    second(2)
                    second(3)
                    f[2]()
                    distance(0)
                    distance(1)
                    if later:
                        centre(g - 1)
                    f[3]()
                    distance(2)
                    distance(3)
                    if later:
                        scores(g - 1)
                    f[4]()
                    distance(4)
                    distance(5)
                    residual(0)
                    f[5]()
                    distance(6)
                    distance(7)
                    residual(1)
                    f[6]()
                    residual(2)
                    f[7]()
                    residual(3)
                    assert i[0] == NL, i[0]

                def centre(g):
                    v.wait_ge(lgr, g + 1)
                    lg = pL[0:TP, 0:2 * GI * E0].rearrange("p (q b e) -> p q b e", q=2, b=GI)
                    nc.vector.tensor_reduce(lmax[:, :, :], lg, AX.X, ALU.max).then_inc(sv, 1)
                    v.wait_ge(sv, 3 * g + 1)
                    nc.vector.tensor_tensor(lsub[:, :, :, :], lg, lmax[:, :, :].unsqueeze(3).broadcast_to([TP, 2, GI, E0]), ALU.subtract).then_inc(lfree, 1)

                def scores(g):
                    v.wait_ge(scr, g + 1)
                    nc.vector.tensor_reduce(lsum[:, :, :], lexp[:, :, :, :], AX.X, ALU.add).then_inc(sv, 1)
                    v.wait_ge(sv, 3 * g + 2)
                    nc.vector.reciprocal(linv[:, :, :], lsum[:, :, :]).then_inc(sv, 1)
                    v.wait_ge(sv, 3 * g + 3)
                    nc.vector.tensor_tensor(score[:, :, bass.ds(g * GI, GI), :], lexp[:, :, :, :], linv[:, :, :].unsqueeze(3).broadcast_to([TP, 2, GI, E0]), ALU.mult).then_inc(score_done, 1)

                v.sem_inc(lfree, 1)
                nc.vector.tensor_copy(h0T[:, :, 0:1], posT[:, 0:1].unsqueeze(1).broadcast_to([D, GI, 1])).then_inc(cst, 1)
                for jp in range(JP):
                    pixels(0, jp)
                    add_pos(0, jp)
                body(0, True)
                with v.Fori(0, 3) as it:
                    body(it * 2 + 1, True)
                    body(it * 2 + 2, True)
                body(NG - 1, False)
                centre(NG - 1)
                scores(NG - 1)
                v.wait_ge(score_done, NG)


HB = 16
NPAIR = E0 // 2
SLOT2 = 2 * KTOP
ROUNDS = -(-KTOP // 8)


def expert_inputs(m):
    return {
        "w1": m.sb("e_w1", [D, E0, F0]), "w2": m.sb("e_w2", [D, E0, 2, D]), "rows": m.sb("e_bias_rows", [E0, 3, D]), "in": m.sem("e_w_in"),
        "got": m.sb("gathered", [SLOT2, GI, NPAIR, D]), "stage": m.sb("gather_rows", [SLOT2, GI * NPAIR], I32),
        "gathered": [m.sem(f"gathered{i}") for i in range(GI)], "staged": m.sem("stage_ready"), "held": m.sem("e_pool_held"),
    }


def stage_indices(nc, pool, keep, we, g, half):
    n = GI * NPAIR // 2
    nc.gpsimd.tensor_copy(we["stage"][:, half * n:(half + 1) * n], keep["slot_row"][:, bass.ds(g * GI * NPAIR + half * n, n)]).then_inc(we["staged"], 1)
    hold(pool, we["staged"], 2 * g + half + 1, we["held"])


def gather_image(nc, t, we, b):
    for j in range(NPAIR):
        nc.gpsimd.indirect_dma_start(we["got"][:, b, j, :], None, t["xn1"].rearrange("b s d -> (b s) d"),
                                     bass.IndirectOffsetOnAxis(ap=we["stage"][:, b * NPAIR + j:b * NPAIR + j + 1], axis=0)).then_inc(we["gathered"][b], 16)


def layer1_weights(m):
    return {
        "wv": m.sb("l1_wv", [D, 2 * D]), "bv": m.sb("l1_bv", [TP, 2 * D]), "wu": m.sb("l1_wu", [D, 2 * D]),
        "bo": m.sb("l1_bo", [D, D]), "bu": m.sb("l1_bu", [D, 2]), "wo": m.sb("l1_wo", [D, 2, D]),
        "router": m.sb("l1_router", [D, E1]), 
        "wide": m.sb("l1_wide", [D, 2, 2, (E1 + 1) * F1], F32R), "down": m.sb("l1_down", [D, NC1, D]),
        "sdown": m.sb("l1_sdown", [F1, D]), "pick": m.sb("l1_pick", [D, NC1, D], BF16),
        "identb": m.sb("identb", [D, D], BF16), "expid": m.sb("expert_ids", [D, E1]), "in": m.sem("l1_w_in"),
    }


def choose_tokens(nc, m, t, keep, we, w):
    with ExitStack() as ctx:
        l = Mem(nc, ctx)
        ng = B // HB
        work = l.sb("topk_work", [D, ng, S])
        val = l.sb("topk_val", [D, ng, ROUNDS * 8])
        idx = l.sb("topk_idx", [D, ng, ROUNDS * 8], U32)
        spread = l.sb("topk_spread", [D, 2, ng, SLOT2])
        odd = l.sb("odd_even", [D, 2])
        pick = l.sb("pick_pair", [D, D // 2])
        basei = l.sb("row_base_i", [SLOT2, B * NPAIR], I32)
        base = l.sb("row_base", [SLOT2, B * NPAIR])
        pt = [l.ps(f"ps_score{i}", [D, 512]) for i in range(ng)]
        pi = [l.ps(f"ps_slots{i}", [D, 512]) for i in range(2)]
        ident, score = keep["ident"], keep["score"]
        tr, dv, iot, mm, rowr = (l.sem(n) for n in ("tk_tr", "tk_dve", "tk_iota", "tk_mm", "tk_rows_ready"))
        parts = [range(1), range(1, ng)]
        with nc.Block() as block:

            @block.sync
            def _(sp):
                for i in range(2):
                    sp.dma_start(we["rows"][:, i, :], t["L0_ffn_b1"][:, i * D:(i + 1) * D]).then_inc(we["in"], 16)
                sp.dma_start(we["rows"][:, 2, :], t["L0_ffn_b2"]).then_inc(we["in"], 16)
                sp.dma_start(we["w1"][:, :, :], t["L0_ffn_W1"].rearrange("e h f -> h e f")).then_inc(we["in"], 16)
                sp.dma_start(we["w2"][:, :, :, :], t["L0_ffn_W2"].rearrange("e (c p) h -> p e c h", p=D)).then_inc(we["in"], 16)
                load_layer1(sp, t, w)

            @block.gpsimd
            def _(pool):
                nc.gpsimd.iota(basei[:, :], pattern=[[SP, B], [0, NPAIR]], base=0, channel_multiplier=0).then_inc(iot, 1)
                pool.wait_ge(rowr, 1)
                for half in range(2):
                    stage_indices(nc, pool, keep, we, 0, half)
                for b in range(GI):
                    gather_image(nc, t, we, b)

            @block.tensor
            def _(pe):
                for g in range(ng):
                    for q, n in enumerate((TP, S - TP)):
                        x = nc.tensor.transpose(pt[g][:, q * TP:q * TP + n], score[0:n, q, g * HB:(g + 1) * HB, :].rearrange("p b e -> p (b e)"), ident[0:n, 0:n])
                    x.then_inc(tr, 1)
                for part, gs in enumerate(parts):
                    pe.wait_ge(dv, (part + 1) * LAST)
                    for j in range(2):
                        for g in gs:
                            o = j * B * NPAIR + g * HB * NPAIR
                            x = nc.tensor.matmul(pi[part][0:SLOT2, o:o + HB * NPAIR], spread[:, j, g, :], pick[:, :], start=True, stop=True)
                    x.then_inc(mm, 1)

            @block.vector
            def _(v):
                n = [0]

                def link(x):
                    n[0] += 1
                    x.then_inc(dv, 1)
                    v.wait_ge(dv, n[0])

                v.wait_ge(iot, 1)
                nc.vector.tensor_copy(base[:, :], basei[:, :])
                for j in range(2):
                    nc.vector.tensor_reduce(odd[:, j:j + 1], ident[:, :].rearrange("p (a b) -> p b a", b=2)[:, j], AX.X, ALU.add)
                nc.vector.tensor_tensor(pick[:, :], ident[:, :].rearrange("p (a b) -> p b a", b=2)[:, 0], ident[:, :].rearrange("p (a b) -> p b a", b=2)[:, 1], ALU.add)

                def slots(part):
                    gs = parts[part]
                    a, b = gs[0] * HB * NPAIR, (gs[-1] + 1) * HB * NPAIR
                    p = pi[part][0:SLOT2, :]
                    v.wait_ge(mm, part + 1)
                    nc.vector.tensor_copy(keep["slot_idx"][:, a:b], p[:, a:b])
                    nc.vector.tensor_copy(keep["slot_gate"][:, a:b], p[:, B * NPAIR + a:B * NPAIR + b])
                    nc.vector.tensor_tensor(keep["slot_row"][:, a:b], p[:, a:b], base[:, a:b], ALU.add).then_inc(rowr, 1)

                for part, gs in enumerate(parts):
                    for g in gs:
                        v.wait_ge(tr, g + 1)
                        x = nc.vector.tensor_copy(work[:, g, :], pt[g][:, 0:S])
                    link(x)
                    for r in range(ROUNDS):
                        w = slice(8 * r, 8 * r + 8)
                        for g in gs:
                            x = nc.vector.max(val[:, g, w], work[:, g, :])
                        link(x)
                        for g in gs:
                            x = nc.vector.max_index(idx[:, g, w], val[:, g, w], work[:, g, :])
                        if r < ROUNDS - 1:
                            link(x)
                            for g in gs:
                                x = nc.vector.match_replace(work[:, g, :], val[:, g, w], work[:, g, :], -1.0)
                        link(x)
                        if part and r == 0:
                            slots(0)
                    for j, src in enumerate((idx, val)):
                        for h in range(2):
                            c = slice(gs[0], gs[-1] + 1)
                            x = nc.vector.tensor_scalar(spread[:, j, c, h * KTOP:(h + 1) * KTOP], src[:, c, 0:KTOP], odd[:, h:h + 1], None, ALU.mult)
                    link(x)
                    assert n[0] == (part + 1) * LAST, n[0]
                slots(1)
                v.wait_ge(rowr, 2)


LAST = 1 + 3 * ROUNDS - 1 + 1


def experts(nc, m, t, keep, we):
    with ExitStack() as ctx:
        l = Mem(nc, ctx)
        w1, w2, brow, w_in, got, gat = (we[n] for n in ("w1", "w2", "rows", "in", "got", "gathered"))
        bcol = l.sb("e_bias_cols", [D, 3, E0])
        ex = l.sb("expert_in", [D, E0, GI, KTOP])
        hm = l.sb("expert_hidden", [D, 2, 2, GI * KTOP])
        eo = l.sb("expert_out", [D, GI, E0, KTOP])
        vr_ = l.sb("expert_rows", [SLOT2, 2, NPAIR, D])
        hot = l.sb("gated_onehot", [SLOT2, GI, NPAIR, SP])
        toki = l.sb("token_iota_i", [SLOT2, SP], I32)
        tok = l.sb("token_iota", [SLOT2, SP])
        h1 = l.sb("h1_rows", [TP, GI, 2, D])
        h2 = l.sb("h2_rows", [TP, GI, 2, D])
        xn = l.sb("xn2_rows", [TP, GI, 2, D])
        xs = l.sb("xs_rows", [TP, GI, 2, D])
        st = l.sb("e_ln_stats", [TP, 4, 4, 6])
        mv = l.sb("e_meanvar", [TP, 4, 4, 2])
        base = l.sb("e_pow_base", [TP, 4, 2, 4])
        root = l.sb("e_pow_root", [TP, 4, 2, 4])
        rms = l.sb("e_rms", [TP, 2, 4, 4])
        inv = l.sb("e_inv_rms", [TP, 4, 4])
        pw = l.sb("e_powers", [TP, 2, 4])
        ring = [l.ps(f"ps_e_ring{i}", [D, 512]) for i in range(4)]
        hid = [l.ps(f"ps_e_hidden{i}", [D, 512]) for i in range(4)]
        ident = keep["ident"]
        cst, bt, bc = (l.sem(n) for n in ("e_const", "e_bias_tr", "e_bias_ready"))
        full, exr, w1d, hmr, eor, rwr, hotr, h2r = (l.sem(n) for n in ("e_ring_full", "ex_ready", "w1_done", "hidden_ready", "eout_ready", "erows_ready", "hot_ready", "h2_ready"))
        dv, scr, xsr, rr, h1in, outd = (l.sem(n) for n in ("e_dve", "e_root_ready", "xs_ready", "r_ready", "h1_in", "e_stored"))
        prer, invr, nv = (l.sem(n) for n in ("e_base_ready", "e_inv_ready", "e_norm"))
        xnd, tokr, held = (l.sem(n) for n in ("xn2_ready", "token_iota_ready", "e_dve_held"))
        order = [f"out{e}" for e in range(E0)] + ["rows0"]
        for b in range(GI):
            order += [f"rows{b + 1}", f"spread{b}", f"fetch{b}"] if b + 1 < GI else [f"fetch{b}", f"spread{b}"]
        NU = len(order)
        reader = {"out": eor, "rows": rwr, "spread": h2r, "fetch": exr}

        def slot(s):
            return ring[order.index(s) % 4]

        def take(pe, g, s):
            i = order.index(s) - 4
            fixed = isinstance(g, int)
            while i >= 0 and fixed and (order[i][:-1] != "fetch" if g < 0 else g == NG - 1 and order[i][:-1] == "fetch"):
                i -= 4
            if fixed and g < 0 and i < 0:
                return
            stage, k = order[i % NU][:-1], int(order[i % NU][-1])
            pe.wait_ge(reader[stage], GI * (g - (i < 0) + 1) + k + 1)

        def filled(eng, g, s):
            i = order.index(s) + 1
            if isinstance(g, int) and g < 0:
                eng.wait_ge(full, int(s[-1]) + 1)
            else:
                if isinstance(g, int) and g == NG - 1:
                    i -= sum(x[:-1] == "fetch" for x in order[:i])
                eng.wait_ge(full, GI + NU * g + i)

        with nc.Block() as block:

            @block.sync
            def _(sp):
                def residual(g):
                    sp.dma_start(h1[:, :, :, :], t["h1"][bass.ds(g * GI, GI)].rearrange("b (t p) d -> p b t d", p=TP)).then_inc(h1in, 16)

                def store(g):
                    sp.wait_ge(rr, 4 * g + 4)
                    sp.dma_start(t["res2"][bass.ds(g * GI, GI)].rearrange("b (t p) d -> p b t d", p=TP), h2[:, :, :, :]).then_inc(outd, 16)
                    sp.wait_ge(xsr, 4 * g + 4)
                    sp.dma_start(t["xs"][bass.ds(g * GI, GI)].rearrange("b (t p) d -> p b t d", p=TP), xs[:, :, :, :]).then_inc(outd, 16)

                residual(0)
                with sp.Fori(0, NG - 1) as g:
                    sp.wait_ge(h2r, GI * g + 2 * GI)
                    residual(g + 1)
                    store(g)
                store(NG - 1)
                sp.wait_ge(outd, 32 * NG + 32)

            @block.gpsimd
            def _(pool):
                def indices(g, half):
                    for b in range(half * GI // 2, (half + 1) * GI // 2):
                        pool.wait_ge(gat[b], 64 * g)
                    hold(pool, gat[half * GI // 2], 64 * g, we["held"])
                    stage_indices(nc, pool, keep, we, g, half)

                def gather(g, b):
                    hold(pool, exr, GI * (g - 1) + b + 1, we["held"])
                    gather_image(nc, t, we, b)

                def roots(g, k):
                    pool.wait_ge(prer, 4 * g + k + 1)
                    nc.gpsimd.tensor_tensor(root[:, k, :, :], base[:, k, :, :], pw[:, :, :], ALU.pow).then_inc(scr, 1)

                nc.gpsimd.iota(toki[:, :], pattern=[[1, SP]], base=0, channel_multiplier=0).then_inc(cst, 1)
                for i, p in enumerate((-0.5, 0.5)):
                    nc.gpsimd.memset(pw[:, i, :], p).then_inc(cst, 1)
                pool.wait_ge(cst, 3)
                pool.sem_inc(outd, 32)
                with pool.Fori(0, NG - 1) as g:
                    indices(g + 1, 0)
                    for b in range(4):
                        gather(g + 1, b)
                    indices(g + 1, 1)
                    for b in range(4, 7):
                        gather(g + 1, b)
                    roots(g, 0)
                    gather(g + 1, 7)
                    roots(g, 1)
                    roots(g, 2)
                    roots(g, 3)
                for k in range(4):
                    roots(NG - 1, k)

            @block.tensor
            def _(pe):
                def hidden(g, e):
                    if e == 0:
                        pe.wait_ge(exr, GI * g + GI)
                    pe.wait_ge(hmr, GI * g + e + 1)
                    for c in range(2):
                        x = nc.tensor.matmul(hid[2 * (e % 2) + c][:, 0:GI * KTOP], w1[:, e, c * D:(c + 1) * D], ex[:, e, :, :].rearrange("p b k -> p (b k)"), start=True, stop=True)
                    x.then_inc(w1d, 1)

                def output(g, e):
                    take(pe, g, f"out{e}")
                    pe.wait_ge(hmr, GI * g + e + 3)
                    for c in range(2):
                        x = nc.tensor.matmul(slot(f"out{e}")[:, 0:GI * KTOP], w2[:, e, c, :], hm[:, e % 2, c, :], start=c == 0, stop=c == 1)
                    x.then_inc(full, 1)

                def to_rows(g, b):
                    take(pe, g, f"rows{b}")
                    if b == 0:
                        pe.wait_ge(eor, GI * g + 2 * GI)
                    for j in range(NPAIR):
                        x = nc.tensor.transpose(slot(f"rows{b}")[0:SLOT2, j * D:(j + 1) * D], eo[:, b, 2 * j:2 * j + 2, :].rearrange("p e k -> p (e k)"), ident[:, :])
                    x.then_inc(full, 1)

                def spread(g, b):
                    take(pe, g, f"spread{b}")
                    pe.wait_ge(rwr, GI * g + b + 1 + GI)
                    pe.wait_ge(hotr, GI * g + b + 1)
                    for q in range(2):
                        for j in range(NPAIR):
                            x = nc.tensor.matmul(slot(f"spread{b}")[0:TP, q * D:(q + 1) * D], hot[:, b, j, q * TP:(q + 1) * TP], vr_[:, b % 2, j, :], start=j == 0, stop=j == NPAIR - 1)
                    x.then_inc(full, 1)

                pe.wait_ge(w_in, 80)
                for i in range(3):
                    x = nc.tensor.transpose(hid[0][:, i * E0:(i + 1) * E0], brow[:, i, :], ident[0:E0, 0:E0])
                x.then_inc(bt, 1)
                pe.wait_ge(bc, 1)

                def fetch(g, b):
                    take(pe, g, f"fetch{b}")
                    pe.wait_ge(gat[b], 64 * (g + 1) + 64)
                    for j in range(NPAIR):
                        x = nc.tensor.transpose(slot(f"fetch{b}")[:, j * SLOT2:(j + 1) * SLOT2], got[:, b, j, :], ident[0:SLOT2, 0:SLOT2])
                    x.then_inc(full, 1)

                def body(g, more):
                    hidden(g, 0)
                    for e in range(E0):
                        if e + 1 < E0:
                            hidden(g, e + 1)
                        output(g, e)
                    to_rows(g, 0)
                    for b in range(GI):
                        if b + 1 < GI:
                            to_rows(g, b + 1)
                        if more and b + 1 == GI:
                            fetch(g, b)
                        spread(g, b)
                        if more and b + 1 < GI:
                            fetch(g, b)

                for b in range(GI):
                    fetch(-1, b)
                with pe.Fori(0, NG - 1) as g:
                    body(g, True)
                body(NG - 1, False)

            @block.scalar
            def _(act):
                act.wait_ge(bt, 1)
                nc.scalar.copy(bcol[:, :, :].rearrange("p i e -> p (i e)"), hid[0][:, 0:3 * E0]).then_inc(bc, 1)
                act.wait_ge(bc, 1)
                act.sem_inc(hmr, 2)
                act.sem_inc(rwr, GI)

                def rescale(g, k):
                    act.wait_ge(invr, 4 * g + k + 1)
                    act.wait_ge(rr, 4 * g + k + 1)
                    if k == 0:
                        act.wait_ge(outd, 32 * g + 32)
                    for q in range(4):
                        x = nc.scalar.activation(xs[:, 2 * k + q // 2, q % 2, :], xn[:, 2 * k + q // 2, q % 2, :], ACT.Copy, scale=inv[:, k, q:q + 1])
                    x.then_inc(xsr, 1)

                def body(g):
                    for e in range(E0):
                        act.wait_ge(w1d, GI * g + e + 1)
                        if e >= 2:
                            filled(act, g, f"out{e - 2}")
                        for c in range(2):
                            x = nc.scalar.activation(hm[:, e % 2, c, :], hid[2 * (e % 2) + c][:, 0:GI * KTOP], ACT.Gelu, bias=bcol[:, c, e:e + 1])
                        x.then_inc(hmr, 1)
                        if not (isinstance(g, int) and g == 0) and e in (4, 6):
                            rescale(g - 1, e // 2)
                    for b in range(GI):
                        filled(act, g, f"rows{b}")
                        nc.scalar.copy(vr_[:, b % 2, :, :].rearrange("p j d -> p (j d)"), slot(f"rows{b}")[0:SLOT2, :]).then_inc(rwr, 1)
                        if b >= 6:
                            rescale(g, b - 6)

                body(0)
                with act.Fori(1, NG - 1) as g:
                    body(g)
                body(NG - 1)
                rescale(NG - 1, 2)
                rescale(NG - 1, 3)

            @block.vector
            def _(v):
                v.wait_ge(cst, 3)
                nc.vector.tensor_copy(tok[:, :], toki[:, :]).then_inc(tokr, 1)
                v.wait_ge(tokr, 1)
                v.sem_inc(h2r, GI)
                v.sem_inc(eor, GI)

                def onehots(g, b):
                    for j in range(NPAIR):
                        col = g * (GI * NPAIR) + b * NPAIR + j
                        x = nc.vector.tensor_scalar(hot[:, b, j, :], tok[:, :], keep["slot_idx"][:, bass.ds(col, 1)], keep["slot_gate"][:, bass.ds(col, 1)], ALU.is_equal, ALU.mult)
                    x.then_inc(hotr, 1)

                def stats(g, k):
                    v.wait_ge(h2r, GI * g + 2 * k + 2 + GI)
                    for q in range(4):
                        x = nc.vector.bn_stats(st[:, k, q, :], h2[:, 2 * k + q // 2, q % 2, :])
                    x.then_inc(dv, 1)
                    hold(v, dv, 2 * (4 * g + k) + 1, held)
                    for q in range(4):
                        x = nc.vector.bn_aggr(mv[:, k, q, :], st[:, k, q, :])
                    x.then_inc(dv, 1)
                    v.wait_ge(dv, 2 * (4 * g + k) + 2)
                    nc.vector.tensor_scalar(base[:, k, 0, :], mv[:, k, :, 1], EPS, None, ALU.add)
                    nc.vector.tensor_copy(base[:, k, 1, :], mv[:, k, :, 1]).then_inc(prer, 1)

                def normalise(g, k):
                    v.wait_ge(scr, 4 * g + k + 1)
                    for q in range(4):
                        x = nc.vector.tensor_scalar(xn[:, 2 * k + q // 2, q % 2, :], h2[:, 2 * k + q // 2, q % 2, :], mv[:, k, q, 0:1], root[:, k, 0, q:q + 1], ALU.subtract, ALU.mult)
                    x.then_inc(xnd, 1)
                    nc.vector.tensor_tensor(rms[:, 0, k, :], root[:, k, 0, :], root[:, k, 1, :], ALU.mult).then_inc(nv, 1)
                    v.wait_ge(nv, 2 * (4 * g + k) + 1)
                    nc.vector.tensor_scalar(rms[:, 1, k, :], rms[:, 0, k, :], 1e-8, None, ALU.add).then_inc(nv, 1)
                    v.wait_ge(nv, 2 * (4 * g + k) + 2)
                    nc.vector.reciprocal(inv[:, k, :], rms[:, 1, k, :]).then_inc(invr, 1)
                    v.wait_ge(xnd, 4 * g + k + 1)
                    a = h2[:, 2 * k:2 * k + 2, :, :].rearrange("p i q d -> p (i q d)")
                    nc.vector.tensor_tensor(a, a, xn[:, 2 * k:2 * k + 2, :, :].rearrange("p i q d -> p (i q d)"), ALU.add).then_inc(rr, 1)

                def fetched(g, b):
                    filled(v, g, f"fetch{b}")
                    nc.vector.tensor_copy(ex[:, :, b, :], slot(f"fetch{b}")[:, 0:E0 * KTOP].rearrange("p (e k) -> p e k", k=KTOP)).then_inc(exr, 1)

                def body(g, more):
                    for e in range(E0):
                        onehots(g, e)
                        filled(v, g, f"out{e}")
                        nc.vector.tensor_scalar(eo[:, :, e, :], slot(f"out{e}")[:, 0:GI * KTOP].rearrange("p (b k) -> p b k", k=KTOP), bcol[:, 2, e:e + 1], None, ALU.add).then_inc(eor, 1)
                        if e in (1, 3) and not (isinstance(g, int) and g == 0):
                            normalise(g - 1, 2 + e // 2)
                    v.wait_ge(h1in, 16 * g + 16)
                    v.wait_ge(outd, 32 * g + 32)
                    for b in range(GI):
                        if more and b + 1 == GI:
                            fetched(g, b)
                        filled(v, g, f"spread{b}")
                        nc.vector.tensor_tensor(h2[:, b, :, :].rearrange("p q d -> p (q d)"), slot(f"spread{b}")[0:TP, 0:2 * D], h1[:, b, :, :].rearrange("p q d -> p (q d)"), ALU.add).then_inc(h2r, 1)
                        if more and b + 1 < GI:
                            fetched(g, b)
                        if b % 2 == 1:
                            stats(g, b // 2)
                        if b in (4, 6):
                            normalise(g, b // 2 - 2)

                v.wait_ge(bc, 1)
                for b in range(GI):
                    fetched(-1, b)
                body(0, True)
                with v.Fori(1, NG - 1) as g:
                    body(g, True)
                body(NG - 1, False)
                normalise(NG - 1, 2)
                normalise(NG - 1, 3)


E1, F1 = 8, 64
NC1 = E1 * F1 // D
CPU = 4
TU = 6
NU1 = SP // TU
NT = TU // 2
COL = TU * B


def load_layer1(sp, t, w):
    one = lambda v: v.rearrange("(p a) -> p a", a=1)
    row = lambda v, n: v.rearrange("(a p) -> a p", a=1).broadcast_to(n)
    pairs = [
        (w["wv"][:, :], t["L1_attn_Wv"]), (w["bv"][:, :], row(t["L1_attn_bv"], [TP, 2 * D])),
        (w["wu"][:, :], t["L1_attn_Wu"]), (w["bo"][:, :], row(t["L1_attn_bo"], [D, D])),
        (w["bu"][:, 0:1], one(t["L1_attn_bu"][0:D])), (w["bu"][:, 1:2], one(t["L1_attn_bu"][D:2 * D])),
        (w["wo"][:, :, :], t["L1_attn_Wo"].rearrange("(a p) d -> p a d", p=D)),
        (w["router"][:, :], t["L1_ffn_router"]),
        (w["down"][:, :, :], t["L1_ffn_W_down"].rearrange("(i a) h d -> (a h) i d", a=2)),
        (w["sdown"][:, :], t["L1_ffn_shared_down"]),
        (w["expid"][:, :], t["expid"].broadcast_to([D, E1])),
    ]
    for dst, src in pairs:
        sp.dma_start(dst, src).then_inc(w["in"], 16)
    assert len(pairs) == 11


def layer1(nc, m, t, keep, w):
    with ExitStack() as ctx:
        l = Mem(nc, ctx)
        mixer = l.sb("mixer_values", [D, D, 4 * B])
        values(nc, t, keep, w, mixer)
        mix_tokens(nc, t, keep, mixer)
        finish(nc, t, keep, w, mixer)


def values(nc, t, keep, w, mixer):
    with ExitStack() as ctx:
        l = Mem(nc, ctx)
        nb = 4
        xs = l.sb("v_xs", [TP, 2, nb, 2, D])
        xsT = l.sb("v_xsT", [D, nb, SP])
        pre = l.sb("v_pre", [TP, nb, 2, 2 * D])
        pick = l.sb("l1_pick_fp32", [D, NC1, D])
        raw = l.sb("l1_wide_raw", [D, 2, (E1 + 1) * F1])
        pT = [l.ps(f"ps_v_T{i}", [D, 512]) for i in range(nb)]
        pV = [l.ps(f"ps_v{i}", [D, 512]) for i in range(nb)]
        ident, w_in = keep["ident"], w["in"]
        xin = [l.sem(f"v_xs_in{i}") for i in range(2)]
        turned, xtr, mm, prer, vr, pick_in, high, raw_in = (l.sem(n) for n in ("v_turned", "v_xsT_ready", "v_mm", "v_pre_ready", "v_ready", "v_pick_in", "l1_rounded", "l1_wide_in"))
        with nc.Block() as block:

            @block.sync
            def _(sp):
                def load(g, par):
                    sp.dma_start(xs[:, par, :, :, :], t["xs"][bass.ds(g * nb, nb)].rearrange("b (t p) d -> p b t d", p=TP)).then_inc(xin[par], 16)

                load(0, 0)
                load(1, 1)
                sp.dma_start(pick[:, :, :], t["pick"]).then_inc(pick_in, 16)
                for i, n in enumerate(("gate", "up")):
                    sp.dma_start(raw[:, i, 0:E1 * F1].rearrange("d (e h) -> d e h", h=F1), t["L1_ffn_W_" + n].rearrange("e d h -> d e h")).then_inc(raw_in, 16)
                    sp.dma_start(raw[:, i, E1 * F1:], t["L1_ffn_shared_" + n]).then_inc(raw_in, 16)
                with sp.Fori(1, B // (2 * nb)) as it:
                    for par in range(2):
                        sp.wait_ge(turned, nb * (2 * it + par - 1))
                        load(2 * it + par, par)

            @block.gpsimd
            def _(pool):
                pool.wait_ge(pick_in, 16)
                nc.gpsimd.tensor_copy(w["pick"][:, :, :], pick[:, :, :])
                nc.gpsimd.tensor_copy(w["identb"][:, :], ident[:, :])

            @block.tensor
            def _(pe):
                def turn(i, b, half):
                    k = b % nb
                    if k == 0:
                        pe.wait_ge(xin[b // nb], 16 * half + 16)
                    pe.wait_ge(xtr, i + 1)
                    for q in range(2):
                        x = nc.tensor.transpose(pT[k][:, q * TP:(q + 1) * TP], xs[:, b // nb, k, q, :], ident[0:TP, 0:TP])
                    x.then_inc(turned, 1)

                def project(i, b):
                    k = b % nb
                    pe.wait_ge(xtr, i + 1 + nb)
                    pe.wait_ge(prer, i + 1)
                    for q in range(2):
                        x = nc.tensor.matmul(pV[k][0:TP, q * 2 * D:(q + 1) * 2 * D], xsT[:, k, q * TP:(q + 1) * TP], w["wv"][:, :], start=True, stop=True)
                    x.then_inc(mm, 1)

                pe.wait_ge(w_in, 16 * 11)
                for b in range(2):
                    turn(b, b, 0)
                with pe.Fori(0, B // (2 * nb) - 1) as it:
                    for b in range(2 * nb):
                        turn(2 * nb * it + b + 2, (b + 2) % (2 * nb), it + (b + 2) // (2 * nb))
                        project(2 * nb * it + b, b)
                for b in range(2 * nb):
                    i = B - 2 * nb + b
                    if i + 2 < B:
                        turn(i + 2, b + 2, B // (2 * nb) - 1)
                    project(i, b)

            @block.vector
            def _(v):
                v.sem_inc(prer, nb)
                v.wait_ge(w_in, 16 * 11)
                with v.Fori(0, B // nb) as g:
                    for b in range(nb):
                        i = nb * g + b
                        v.wait_ge(mm, i + 1)
                        v.wait_ge(vr, i + 1)
                        nc.vector.tensor_tensor(pre[:, b, :, :], pV[b][0:TP, :].rearrange("p (q c) -> p q c", q=2),
                                                w["bv"][:, :].unsqueeze(1).broadcast_to([TP, 2, 2 * D]), ALU.add).then_inc(prer, 1)
                wide = w["wide"]
                v.wait_ge(raw_in, 64)
                nc.vector.tensor_copy(wide[:, 1, :, :], raw[:, :, :]).then_inc(high, 1)
                v.wait_ge(high, 1)
                nc.vector.tensor_tensor(wide[:, 0, :, :], raw[:, :, :], wide[:, 1, :, :].bitcast(F32), ALU.subtract)

            @block.scalar
            def _(act):
                act.sem_inc(xtr, nb)
                act.sem_inc(vr, nb)

                def turned_(i, b):
                    act.wait_ge(turned, i + 1)
                    if not (isinstance(i, int) and i < nb):
                        act.wait_ge(mm, i + 1 - nb)
                    src = pT[b][:, 0:SP].rearrange("p (q n) -> p q n", q=2)[:, :, ::-1]
                    nc.scalar.copy(xsT[:, b, :].rearrange("p (q n) -> p q n", q=2), src).then_inc(xtr, 1)

                def gate(i, b):
                    act.wait_ge(prer, i + 1 + nb)
                    dst = mixer[0:TP, :, :].rearrange("p c (n b) -> p n c b", b=B)
                    for q in range(2):
                        o = dst[:, 2 * q:2 * q + 2, :, bass.ds(i, 1)]
                        x = nc.scalar.activation(o, pre[:, b, q, :].rearrange("p (h c a) -> p h c a", h=2, a=1), ACT.Silu)
                    x.then_inc(vr, 1)

                turned_(0, 0)
                turned_(1, 1)
                turned_(2, 2)
                gate(0, 0)
                turned_(3, 3)
                gate(1, 1)
                with act.Fori(1, B // nb) as g:
                    for b in range(nb):
                        turned_(nb * g + b, b)
                        gate(nb * g + b - 2, (b - 2) % nb)
                gate(B - 2, (B - 2) % nb)
                gate(B - 1, (B - 1) % nb)


def mix_tokens(nc, t, keep, mixer):
    with ExitStack() as ctx:
        l = Mem(nc, ctx)
        nu = D // CPU
        toep = l.sb("toeplitz", [TP, 4, 2, CPU, SP])
        stage = l.sb("mixer_stage", [TP, 2, CPU, 4 * B])
        pm = [l.ps(f"ps_mix{i}", [D, 512]) for i in range(4)]
        tin = [l.sem(f"toeplitz_in{i}") for i in range(4)]
        stg, mm, outa, outb, held = (l.sem(n) for n in ("mix_staged", "mix_mm", "mix_out_act", "mix_out_dve", "mix_pool_held"))
        width = TP - 1 + SP
        with nc.Block() as block:

            @block.sync
            def _(sp):
                ap = t["apad"]

                def load(u, r):
                    for h in range(2):
                        src = bass.AP(ap.tensor, u * (CPU * width) + h * D * width, [[1, TP], [width, CPU], [1, SP]])
                        sp.dma_start(toep[:, r, h, :, :], src).then_inc(tin[r], 16)

                for r in range(4):
                    load(r, r)
                with sp.Fori(1, nu // 4) as it:
                    for r in range(4):
                        sp.wait_ge(mm, 2 * (4 * it + r - 3))
                        load(4 * it + r, r)

            @block.gpsimd
            def _(pool):
                def copy(u, r):
                    nc.gpsimd.tensor_copy(stage[:, r, :, :], mixer[0:TP, bass.ds(u * CPU, CPU), :]).then_inc(stg, 1)

                copy(0, 0)
                copy(1, 1)
                with pool.Fori(1, nu // 2) as it:
                    for r in range(2):
                        hold(pool, mm, 2 * (2 * it + r - 1), held)
                        copy(2 * it + r, r)

            @block.tensor
            def _(pe):
                with pe.Fori(0, nu // 4) as it:
                    for r in range(4):
                        u = it * 4 + r
                        pe.wait_ge(tin[r], 32 * it + 32)
                        pe.wait_ge(stg, u + 1)
                        for c in range(CPU // 2):
                            pe.wait_ge((outa, outb)[c], u + 1)
                            bank = pm[(r % 2) * 2 + c]
                            for k in range(2):
                                cp = 2 * c + k
                                for q in range(2):
                                    for h in range(2):
                                        o = bank[h * B:(h + 1) * B, k * SP + q * TP:(k + 1) * SP]
                                        x = nc.tensor.matmul(o, stage[:, r % 2, cp, (2 * q + h) * B:(2 * q + h + 1) * B],
                                                             toep[:, r, h, cp, 0:SP - q * TP], start=q == 0, stop=q == 1, skip_group_check=True)
                            x.then_inc(mm, 1)

            def evacuate(eng, copy, sem, c):
                eng.sem_inc(sem, 2)
                with eng.Fori(0, nu // 2) as it:
                    for r in range(2):
                        u = it * 2 + r
                        eng.wait_ge(mm, 2 * u + c + 1)
                        copy(mixer[:, bass.ds(u * CPU + 2 * c, 2), 0:SP], pm[r * 2 + c][:, 0:2 * SP].rearrange("p (k n) -> p k n", k=2)).then_inc(sem, 1)

            @block.scalar
            def _(act):
                evacuate(act, nc.scalar.copy, outa, 0)

            @block.vector
            def _(v):
                evacuate(v, nc.vector.tensor_copy, outb, 1)


def finish(nc, t, keep, w, mixer):
    order = ["xsT", "gate0", "up0", "u0", "u1", "mixT0", "mixT1", "gate1", "up1", "gate2", "proj", "up2",
             "gate3", "up3", "gate4", "up4", "combT", "bc0", "bc1", "bc2", "bc3", "down", "normT", "router"]
    count = {"xsT": 1, "gate": NC1 + 1, "up": NC1 + 1, "u": 2, "mixT": 2, "proj": 1, "combT": 1, "bc": NC1, "normT": 1, "down": 1, "router": 1}
    back = {"gate", "up", "combT", "bc", "down"}
    nb = 8
    with ExitStack() as ctx:
        l = Mem(nc, ctx)
        xs = l.sb("f_xs", [D, 3, NT, D])
        res = l.sb("f_res", [D, 3, NT, D])
        xsT = l.sb("f_xsT", [D, COL])
        us = l.sb("f_u", [D, 2, COL])
        stage = l.sb("f_mixed", [D, TU, D])
        y = l.sb("f_y", [D, 2, COL])
        h3 = l.sb("f_h3", [D, 3, NT, D])
        xn = l.sb("f_xn", [D, NT, D])
        xnT = l.sb("f_xnT", [D, COL])
        xnp = l.sb("f_xnT_parts", [D, 2, COL], F32R)
        gs = l.sb("f_gate", [D, NC1 + 1, COL])
        gu = l.sb("f_hidden", [D, NC1 + 1, COL])
        st = l.sb("f_stats", [D, NT, 6])
        mv = l.sb("f_meanvar", [D, NT, 2])
        vare = l.sb("f_var_eps", [D, NT])
        rstd = l.sb("f_rstd", [D, NT])
        cons = l.sb("f_consts", [D, 4, NT * E1])
        nmean = l.sb("f_minus_mean", [D, NT])
        shift = l.sb("f_shift", [D, NT])
        lmax = l.sb("f_lmax", [D, NT])
        lsub = l.sb("f_lsub", [D, NT, E1])
        lexp = l.sb("f_lexp", [D, NT, E1])
        lsum = l.sb("f_lsum", [D, 2, NT])
        prob = l.sb("f_prob", [D, NT, E1])
        top = l.sb("f_top", [D, NT, E1])
        topi = l.sb("f_top_i", [D, NT, E1], U32)
        topf = l.sb("f_top_f", [D, NT, E1])
        eq = l.sb("f_eq", [D, 2, NT, E1])
        toppart = l.sb("f_top_part", [D, NT, 3, 2], BF16)
        toprest = l.sb("f_top_rest", [D, 2, NT, 2])
        scaled = l.sb("f_scaled", [D, 2, NT, 3, E1])
        split = l.sb("f_split", [D, NT, D], BF16)
        combT = l.sb("f_combT", [D, COL], BF16)
        bank = [l.ps(f"ps_f{i}", [D, 512]) for i in range(nb)]
        ident = keep["ident"]
        filled = {s: l.sem(f"{s}_filled") for s in count}
        read = {s: l.sem(f"{s}_read") for s in count}
        xin, rin = [l.sem(f"f_xs_in{i}") for i in range(3)], [l.sem(f"f_res_in{i}") for i in range(3)]
        staged, resb, cst, held = (l.sem(n) for n in ("f_staged", "f_res_bias", "f_const", "f_pool_held"))
        mvr, veps, rsr, xnr, expr_, cbr = (l.sem(n) for n in ("f_meanvar_ready", "f_vareps_ready", "f_rstd_ready", "f_xn_ready", "f_lexp_ready", "f_split_ready"))
        dv, dheld, stored = l.sem("f_dve"), l.sem("f_dve_held"), [l.sem(f"f_stored{i}") for i in range(3)]
        xhr, xpr = l.sem("f_xn_high_ready"), l.sem("f_xn_parts_ready")
        zero, sts, lmr = l.sem("f_split_zero"), l.sem("f_stats_ready"), l.sem("f_lmax_ready")

        def parts(s):
            name = s.rstrip("01234")
            return name, int(s[len(name):] or 0)

        def psum(s):
            return bank[order.index(s) % nb]

        def take(pe, n, s):
            i = order.index(s) - nb
            while isinstance(n, int) and n == NU1 and i >= 0 and parts(order[i])[0] not in back:
                i -= nb
            name, k = parts(order[i])
            unit = n - (name in back) - (i < 0)
            if not (isinstance(n, int) and unit < -1):
                pe.wait_ge(read[name], count[name] * (unit + 1) + k + 1)

        def wait(eng, sems, unit, s):
            name, k = parts(s)
            eng.wait_ge(sems[name], count[name] * (unit + (sems is read)) + k + 1)

        def each_step(eng, step):
            step(0, 0, 0, True, False)
            with eng.Fori(0, (NU1 - 3) // 3) as it:
                for r in range(3):
                    step(3 * it + r + 1, (r + 1) % 3, it + (r + 1) // 3, True, True)
            n = 3 * ((NU1 - 3) // 3) + 1
            while n <= NU1:
                step(n, n % 3, n // 3, n < NU1, True)
                n += 1

        with nc.Block() as block:

            @block.sync
            def _(sp):
                def rows(d, n, r):
                    return t[d].rearrange("b (u j r) d -> r b u j d", j=NT, r=2)[r][:, bass.ds(n, 1)].rearrange("b u j d -> b (u j) d")

                def load(n, par):
                    for r in range(2):
                        sp.dma_start(xs[r * B:(r + 1) * B, par, :, :], rows("xs", n, r)).then_inc(xin[par], 16)
                        sp.dma_start(res[r * B:(r + 1) * B, par, :, :], rows("res2", n, r)).then_inc(rin[par], 16)

                def store(n, par):
                    wait(sp, read, n, "down")
                    for r in range(2):
                        k = NT - 1 if isinstance(n, int) and n == NU1 - 1 and r == 1 else NT
                        o = bass.AP(t["out"].tensor, n * (TU * D) + r * D, [[S * D, B], [2 * D, k], [1, D]])
                        sp.dma_start(o, h3[r * B:(r + 1) * B, par, 0:k, :]).then_inc(stored[par], 16)

                for n in range(2):
                    load(n, n)

                def step(n, par, half, front, backs):
                    if front and not (isinstance(n, int) and n + 2 >= NU1):
                        if not (isinstance(n, int) and n == 0):
                            wait(sp, read, n - 1, "proj")
                        load(n + 2, (par + 2) % 3)
                    if backs:
                        store(n - 1, (par + 2) % 3)

                each_step(sp, step)
                for i in range(3):
                    sp.wait_ge(stored[i], 32 * (NU1 // 3) + 32)

            @block.gpsimd
            def _(pool):
                nc.gpsimd.memset(cons[:, 0, :], EPS).then_inc(cst, 1)
                nc.gpsimd.memset(cons[:, 1, :], -0.5).then_inc(cst, 1)
                nc.gpsimd.memset(cons[:, 2, :], 2.718281828459045).then_inc(cst, 1)
                nc.gpsimd.memset(split[:, :, :], 0.0).then_inc(zero, 1)
                for i in range(3):
                    pool.sem_inc(stored[i], 32)
                nc.gpsimd.memset(cons[:, 3, :], 0.0).then_inc(cst, 1)
                pool.wait_ge(cst, 4)

                def copy(n):
                    nc.gpsimd.tensor_copy(stage[:, :, :], mixer[:, :, bass.ds(n * TU, TU)].rearrange("p c t -> p t c")).then_inc(staged, 1)

                copy(0)

                def step(n, par, half, front, backs):
                    if not front:
                        return
                    pool.wait_ge(rin[par], 32 * half + 32)
                    nc.gpsimd.tensor_tensor(res[:, par, :, :], res[:, par, :, :], w["bo"][:, :].unsqueeze(1).broadcast_to([D, NT, D]), ALU.add).then_inc(resb, 1)
                    if not (isinstance(n, int) and n == NU1 - 1):
                        hold(pool, filled["mixT"], 2 * n + 2, held)
                        copy(n + 1)
                    pool.wait_ge(mvr, n + 1)
                    nc.gpsimd.tensor_tensor(vare[:, :], mv[:, :, 1], cons[:, 0, 0:NT], ALU.add).then_inc(veps, 1)
                    nc.gpsimd.tensor_tensor(nmean[:, :], cons[:, 3, 0:NT], mv[:, :, 0], ALU.subtract).then_inc(veps, 1)
                    pool.wait_ge(veps, 2 * n + 2)
                    nc.gpsimd.tensor_tensor(rstd[:, :], vare[:, :], cons[:, 1, 0:NT], ALU.pow).then_inc(rsr, 1)
                    pool.wait_ge(rsr, 2 * n + 1)
                    nc.gpsimd.tensor_tensor(shift[:, :], nmean[:, :], rstd[:, :], ALU.mult).then_inc(rsr, 1)
                    pool.wait_ge(read["router"], n + 2)
                    nc.gpsimd.tensor_tensor(lexp[:, :, :].rearrange("p j e -> p (j e)"), cons[:, 2, :], lsub[:, :, :].rearrange("p j e -> p (j e)"), ALU.pow).then_inc(expr_, 1)

                each_step(pool, step)

            @block.tensor
            def _(pe):
                def step(n, par, half, front, backs):
                    def wide(s, i):
                        if s + str(i) == "gate0":
                            pe.wait_ge(xpr, n)
                        take(pe, n, f"{s}{i}")
                        c = slice(i * D, min((i + 1) * D, (E1 + 1) * F1))
                        for p, (a, b) in enumerate(((1, 1), (1, 0), (0, 1))):
                            x = nc.tensor.matmul(psum(f"{s}{i}")[0:c.stop - c.start, 0:COL], w["wide"][:, a, int(s == "up"), c], xnp[:, b, :], start=p == 0, stop=p == 2)
                        x.then_inc(filled[s], 1)

                    def gate_up(i):
                        wide("gate", i)
                        wide("up", i)

                    if front:
                        take(pe, n, "xsT")
                        pe.wait_ge(xin[par], 32 * half + 32)
                        for j in range(NT):
                            x = nc.tensor.transpose(psum("xsT")[:, j * D:(j + 1) * D], xs[:, par, j, :], ident[:, :])
                        x.then_inc(filled["xsT"], 1)
                    if backs:
                        gate_up(0)
                    if front:
                        wait(pe, read, n, "xsT")
                        for h in range(2):
                            take(pe, n, f"u{h}")
                            nc.tensor.matmul(psum(f"u{h}")[:, 0:COL], w["wu"][:, h * D:(h + 1) * D], xsT[:, :], start=True, stop=True).then_inc(filled["u"], 1)
                        pe.wait_ge(staged, n + 1)
                        for h in range(2):
                            take(pe, n, f"mixT{h}")
                            for k in range(TU // 2):
                                x = nc.tensor.transpose(psum(f"mixT{h}")[:, k * D:(k + 1) * D], stage[:, h * (TU // 2) + k, :], ident[:, :])
                            x.then_inc(filled["mixT"], 1)
                    if backs:
                        gate_up(1)
                        wide("gate", 2)
                    if front:
                        take(pe, n, "proj")
                        wait(pe, read, n, "mixT1")
                        for j in range(NT):
                            for h in range(2):
                                x = nc.tensor.matmul(psum("proj")[:, j * D:(j + 1) * D], y[:, h, j * D:(j + 1) * D], w["wo"][:, h, :], start=h == 0, stop=h == 1)
                        x.then_inc(filled["proj"], 1)
                    if backs:
                        wide("up", 2)
                        gate_up(3)
                        gate_up(4)
                        take(pe, n, "combT")
                        pe.wait_ge(cbr, n)
                        for j in range(NT):
                            x = nc.tensor.transpose(psum("combT")[:, j * D // 2:(j + 1) * D // 2].bitcast(BF16), split[:, j, :], w["identb"][:, :])
                        x.then_inc(filled["combT"], 1)
                        wait(pe, read, n - 1, "combT")
                        for i in range(NC1):
                            take(pe, n, f"bc{i}")
                            nc.tensor.matmul(psum(f"bc{i}")[:, 0:COL], w["pick"][:, i, :], combT[:, :], start=True, stop=True).then_inc(filled["bc"], 1)
                    def down(i):
                        wait(pe, read, n - 1, f"bc{i}")
                        for j in range(NT):
                            x = nc.tensor.matmul(psum("down")[:, j * D:(j + 1) * D], gu[:, i, j * D:(j + 1) * D], w["down"][:, i, :], start=False, stop=i == NC1 - 1, skip_group_check=True)
                        return x

                    if backs:
                        take(pe, n, "down")
                        wait(pe, read, n - 1, "up4")
                        for j in range(NT):
                            nc.tensor.matmul(psum("down")[:, j * D:(j + 1) * D], gu[0:F1, NC1, j * D:(j + 1) * D], w["sdown"][:, :], start=j == 0, stop=False, skip_group_check=True)
                        down(0)
                    if front:
                        take(pe, n, "normT")
                        for j in range(NT):
                            pe.wait_ge(xnr, NT * n + j + 1)
                            x = nc.tensor.transpose(psum("normT")[:, j * D:(j + 1) * D], xn[:, j, :], ident[:, :])
                        x.then_inc(filled["normT"], 1)
                    if backs:
                        down(1)
                    if front:
                        take(pe, n, "router")
                        wait(pe, read, n, "normT")
                        for j in range(NT):
                            x = nc.tensor.matmul(psum("router")[:, j * E1:(j + 1) * E1], xnT[:, j * D:(j + 1) * D], w["router"][:, :], start=True, stop=True)
                        x.then_inc(filled["router"], 1)
                    if backs:
                        down(2)
                        down(3).then_inc(filled["down"], 1)

                each_step(pe, step)

            @block.scalar
            def _(act):
                for s in ("xsT", "gate", "u", "combT", "normT"):
                    act.sem_inc(read[s], count[s])

                def step(n, par, half, front, backs):
                    def gate(i):
                        wait(act, filled, n - 1, f"gate{i}")
                        k = D if i < NC1 else F1
                        nc.scalar.activation(gs[0:k, i, :], psum(f"gate{i}")[0:k, 0:COL], ACT.Silu).then_inc(read["gate"], 1)

                    if front:
                        wait(act, filled, n, "xsT")
                        nc.scalar.copy(xsT[:, :], psum("xsT")[:, 0:COL]).then_inc(read["xsT"], 1)
                    if backs:
                        wait(act, read, n - 2, "up4")
                        gate(0)
                    if front:
                        wait(act, read, n - 1, "mixT1")
                        for h in range(2):
                            wait(act, filled, n, f"u{h}")
                            nc.scalar.activation(us[:, h, :], psum(f"u{h}")[:, 0:COL], ACT.Silu, bias=w["bu"][:, h:h + 1]).then_inc(read["u"], 1)
                    if backs:
                        for i in range(1, NC1 + 1):
                            gate(i)
                        wait(act, filled, n - 1, "combT")
                        nc.scalar.copy(combT[:, :], psum("combT")[:, 0:COL // 2].bitcast(BF16)).then_inc(read["combT"], 1)
                    if front:
                        act.wait_ge(rsr, 2 * n + 2)
                        wait(act, read, n - 1, "normT")
                        for j in range(NT):
                            nc.scalar.activation(xn[:, j, :], h3[:, par, j, :], ACT.Identity, bias=shift[:, j:j + 1], scale=rstd[:, j:j + 1]).then_inc(xnr, 1)
                        wait(act, filled, n, "normT")
                        nc.scalar.copy(xnT[:, :], psum("normT")[:, 0:COL]).then_inc(read["normT"], 1)
                        wait(act, read, n, "normT")
                        if backs:
                            wait(act, filled, n - 1, "up4")
                        nc.scalar.copy(xnp[:, 1, :], xnT[:, :]).then_inc(xhr, 1)

                each_step(act, step)

            @block.vector
            def _(v):
                for s in ("up", "mixT", "proj", "bc", "down", "router"):
                    v.sem_inc(read[s], count[s])
                v.wait_ge(zero, 1)
                NL = 13

                def step(n, par, half, front, backs):
                    u = n - 1
                    i = [0]

                    def link(x):
                        i[0] += 1
                        x.then_inc(dv, 1)

                    def linked():
                        v.wait_ge(dv, NL * u + i[0])

                    def up(i):
                        wait(v, filled, n - 1, f"up{i}")
                        wait(v, read, n - 1, f"gate{i}")
                        k = D if i < NC1 else F1
                        if i == 0 and not (isinstance(n, int) and n < 2):
                            wait(v, filled, n - 2, "down")
                        nc.vector.tensor_tensor(gu[0:k, i, :], psum(f"up{i}")[0:k, 0:COL], gs[0:k, i, :], ALU.mult).then_inc(read["up"], 1)

                    def softmax_sum():
                        v.wait_ge(expr_, u + 1)
                        link(nc.vector.tensor_reduce(lsum[:, 0, :], lexp[:, :, :], AX.X, ALU.add))

                    def softmax():
                        bc = lambda a: a.unsqueeze(2).broadcast_to([D, NT, E1])
                        linked()
                        link(nc.vector.reciprocal(lsum[:, 1, :], lsum[:, 0, :]))
                        linked()
                        link(nc.vector.tensor_tensor(prob[:, :, :], lexp[:, :, :], bc(lsum[:, 1, :]), ALU.mult))

                    def best():
                        hold(v, dv, NL * u + i[0], dheld)
                        for j in range(NT):
                            x = nc.vector.max(top[:, j, :], prob[:, j, :])
                        link(x)
                        linked()
                        link(nc.vector.tensor_copy(toppart[:, :, 0, :], top[:, :, 0:2]))

                    def best_index():
                        linked()
                        link(nc.vector.tensor_tensor(toprest[:, 0, :, :], top[:, :, 0:2], toppart[:, :, 0, :], ALU.subtract))
                        for j in range(NT):
                            x = nc.vector.max_index(topi[:, j, :], top[:, j, :], prob[:, j, :])
                        link(x)
                        linked()
                        link(nc.vector.tensor_copy(toppart[:, :, 1, :], toprest[:, 0, :, :]))
                        link(nc.vector.tensor_copy(topf[:, :, 0:2], topi[:, :, 0:2]))

                    def chosen():
                        linked()
                        link(nc.vector.tensor_tensor(toprest[:, 1, :, :], toprest[:, 0, :, :], toppart[:, :, 1, :], ALU.subtract))
                        ids = w["expid"][:, :].unsqueeze(1).broadcast_to([D, NT, E1])
                        for r in range(2):
                            x = nc.vector.tensor_tensor(eq[:, r, :, :], ids, topf[:, :, r:r + 1].broadcast_to([D, NT, E1]), ALU.is_equal)
                        link(x)
                        linked()
                        link(nc.vector.tensor_copy(toppart[:, :, 2, :], toprest[:, 1, :, :]))

                    def weights():
                        linked()
                        for r in range(2):
                            x = nc.vector.tensor_tensor(scaled[:, r, :, :, :], eq[:, r, :, :].unsqueeze(2).broadcast_to([D, NT, 3, E1]),
                                                        toppart[:, :, :, r:r + 1].broadcast_to([D, NT, 3, E1]), ALU.mult)
                        link(x)
                        linked()
                        nc.vector.tensor_tensor(split[:, :, 0:3 * E1].rearrange("p j (c e) -> p j c e", e=E1), scaled[:, 0, :, :, :], scaled[:, 1, :, :, :], ALU.add).then_inc(cbr, 1)
                        assert i[0] == NL, i[0]

                    def mixed(h):
                        wait(v, filled, n, f"mixT{h}")
                        if h == 0:
                            wait(v, read, n, "u1")
                        k = TU // 2
                        a = psum(f"mixT{h}")[:, 0:k * D].rearrange("p (t h b) -> p h t b", t=k, h=2)
                        c = slice(h * k * B, (h + 1) * k * B)
                        for q in range(2):
                            x = nc.vector.tensor_tensor(y[:, q, c].rearrange("p (t b) -> p t b", b=B), a[:, q], us[:, q, c].rearrange("p (t b) -> p t b", b=B), ALU.mult)
                        x.then_inc(read["mixT"], 1)

                    if backs:
                        up(0)
                    if front:
                        mixed(0)
                    if backs:
                        softmax_sum()
                    if front:
                        mixed(1)
                    if backs:
                        softmax()
                        best()
                        up(1)
                        best_index()
                    if front:
                        v.wait_ge(resb, n + 1)
                        v.wait_ge(stored[par], 32 * half + 32)
                        wait(v, filled, n, "proj")
                        nc.vector.tensor_tensor(h3[:, par, :, :].rearrange("p j d -> p (j d)"), psum("proj")[:, 0:COL], res[:, par, :, :].rearrange("p j d -> p (j d)"), ALU.add).then_inc(read["proj"], 1)
                    if backs:
                        chosen()
                    if front:
                        wait(v, read, n, "proj")
                        for j in range(NT):
                            x = nc.vector.bn_stats(st[:, j, :], h3[:, par, j, :])
                        x.then_inc(sts, 1)
                    if backs:
                        weights()
                    if front:
                        hold(v, sts, n + 1, dheld)
                        for j in range(NT):
                            x = nc.vector.bn_aggr(mv[:, j, :], st[:, j, :])
                        x.then_inc(mvr, 1)
                    if backs:
                        up(2)
                    if backs:
                        up(3)
                        up(4)
                        wait(v, read, n - 1, "up4")
                        for i_ in range(NC1):
                            wait(v, filled, n - 1, f"bc{i_}")
                            nc.vector.tensor_tensor(gu[:, i_, :], gu[:, i_, :], psum(f"bc{i_}")[:, 0:COL], ALU.mult).then_inc(read["bc"], 1)
                    if front:
                        wait(v, read, n, "normT")
                        v.wait_ge(xhr, n + 1)
                        nc.vector.tensor_tensor(xnp[:, 0, :], xnT[:, :], xnp[:, 1, :].bitcast(F32), ALU.subtract).then_inc(xpr, 1)
                    if front:
                        wait(v, filled, n, "router")
                        lg = psum("router")[:, 0:NT * E1].rearrange("p (j e) -> p j e", e=E1)
                        nc.vector.tensor_reduce(lmax[:, :], lg, AX.X, ALU.max).then_inc(lmr, 1)
                        v.wait_ge(lmr, n + 1)
                        nc.vector.tensor_tensor(lsub[:, :, :], lg, lmax[:, :].unsqueeze(2).broadcast_to([D, NT, E1]), ALU.subtract).then_inc(read["router"], 1)
                    if backs:
                        wait(v, filled, n - 1, "down")
                        p = (par + 2) % 3
                        a = h3[:, p, :, :].rearrange("p j d -> p (j d)")
                        nc.vector.tensor_tensor(a, psum("down")[:, 0:COL], a, ALU.add).then_inc(read["down"], 1)

                each_step(v, step)


def tower(nc, t):
    with ExitStack() as whole:
        m = Mem(nc, whole)
        keep = persistent(m)
        with ExitStack() as part:
            pixels = pixel_buffers(Mem(nc, part))
            setup(nc, m, t, keep, pixels)
            embed_and_attend(nc, m, t, keep, pixels)
        w = layer1_weights(m)
        with ExitStack() as part:
            we = expert_inputs(Mem(nc, part))
            choose_tokens(nc, m, t, keep, we, w)
            experts(nc, m, t, keep, we)
        layer1(nc, m, t, keep, w)


_INS = ["x", "L0_tok_W", "L0_tok_b", "L0_tok_token", "L0_tok_pos", "L0_ffn_Wg", "L0_ffn_W1", "L0_ffn_b1", "L0_ffn_W2",
        "L0_ffn_b2", "L1_attn_Wu", "L1_attn_bu", "L1_attn_Wv", "L1_attn_bv", "L1_attn_Wo", "L1_attn_bo", "L1_attn_Wp",
        "L1_attn_bp", "L1_attn_W1", "L1_attn_b1", "L1_attn_W2", "L1_attn_b2", "L1_attn_W3", "L1_attn_b3", "L1_attn_Wz",
        "L1_attn_bz", "L1_ffn_router", "L1_ffn_shared_gate", "L1_ffn_shared_up", "L1_ffn_shared_down", "L1_ffn_W_gate",
        "L1_ffn_W_up", "L1_ffn_W_down"]


def _constants():
    import numpy as np

    pick = np.zeros((D, NC1, D), np.float32)
    for i in range(NC1):
        for r in range(3 * E1):
            if (r % E1) // 2 == i:
                pick[r, i, (r % 2) * F1:(r % 2 + 1) * F1] = 1.0
    return {
        "decay": (np.float32(0.999) ** np.arange(SP, dtype=np.float32)).astype(np.float32).reshape(1, SP),
        "pick": pick,
        "expid": np.arange(E1, dtype=np.float32).reshape(1, E1),
    }


def kernel(**inputs):
    import numpy as _np
    import concourse.bacc as _bacc
    from concourse import mybir as _mybir
    from concourse.bass_utils import run_bass_kernel_spmd as _run

    nc = _bacc.Bacc("TRN2", target_bir_lowering=False, num_devices=1)
    arrays, t = {}, {}
    for name, a in {**{n: inputs[n] for n in _INS}, **_constants()}.items():
        a = _np.ascontiguousarray(a)
        arrays[f"in_{name}"] = a
        t[name] = nc.dram_tensor(f"in_{name}", a.shape, _mybir.dt.from_np(a.dtype), kind="ExternalInput").ap()
    for name, shape in (("apad", (2 * D, TP - 1 + SP)), ("h1", (B, SP, D)), ("xn1", (B, SP, D)), ("res2", (B, SP, D)), ("xs", (B, SP, D))):
        t[name] = nc.dram_tensor(f"scratch_{name}", shape, F32, kind="Internal").ap()
    t["out"] = nc.dram_tensor("out_0_dram", (B, S, D), F32, kind="ExternalOutput").ap()
    tower(nc, t)
    r = _run(nc, [arrays], core_ids=[0])
    return r.results[0]["out_0_dram"]
```
